# Optimizing a Trainium2 kernel written in Bass

```python
import numpy as np
import jax
import jax.numpy as jnp

def _softmax(x, axis=-1):
    return jax.nn.softmax(x, axis=axis)

def _gelu(x):
    return jax.nn.gelu(x, approximate=True)

def _silu(x):
    return jax.nn.silu(x)

def _sigmoid(x):
    return jax.nn.sigmoid(x)

def _layernorm(x, axis=-1, eps=1e-05):
    m = jnp.mean(x, axis=axis, keepdims=True)
    v = jnp.var(x, axis=axis, keepdims=True)
    return (x - m) / jnp.sqrt(v + eps)

def _scatter_add(tgt, idx, src, axis=0):
    return tgt.at[idx].add(src)

def _segment_sum(src, seg, n):
    return jax.ops.segment_sum(src, seg, n)
kernel_name = 'mk_seq_preln_d1_jaxref_r4_709ecd'

def setup_inputs(seed: int=0):
    np.random.seed(seed)
    _w = jnp.asarray

    def _L0_attn_setup():
        import jax, jax.numpy as jnp
        from jax import lax
        import numpy as np
        D_MODEL, D_STATE, D_CONV, EXPAND = (256, 16, 4, 2)
        D_INNER = EXPAND * D_MODEL
        BATCH, SEQ = (2, 256)

        def _selective_scan(u, delta, A, B, C, D):
            u_T = jnp.swapaxes(u, 0, 1)
            delta_T = jnp.swapaxes(delta, 0, 1)
            B_T = jnp.swapaxes(B, 0, 1)
            C_T = jnp.swapaxes(C, 0, 1)

            def step(prev_x, inp):
                delta_t, B_t, u_t = inp
                dA = jnp.exp(jnp.einsum('bi,is->bis', delta_t, A))
                dB_u = jnp.einsum('bi,bs,bi->bis', delta_t, B_t, u_t)
                x_t = dA * prev_x + dB_u
                return (x_t, x_t)
            init = jnp.zeros((u.shape[0], D_INNER, D_STATE), u.dtype)
            _, states = lax.scan(step, init, (delta_T, B_T, u_T))
            y = jnp.einsum('lbis,lbs->lbi', states, C_T) + u_T * D
            return jnp.swapaxes(y, 0, 1)
        key = jax.random.key(seed)
        ks = jax.random.split(key, 9)
        s = 0.02
        return {'inputs': jax.random.normal(ks[0], (BATCH, SEQ, D_MODEL), jnp.float32), 'W_in': jax.random.normal(ks[1], (D_MODEL, 2 * D_INNER), jnp.float32) * s, 'conv_w': jax.random.normal(ks[2], (D_CONV, 1, D_INNER), jnp.float32) * s, 'conv_b': jnp.zeros((D_INNER,), jnp.float32), 'W_x': jax.random.normal(ks[3], (D_INNER, D_MODEL + 2 * D_STATE), jnp.float32) * s, 'W_dt': jax.random.normal(ks[4], (D_MODEL, D_INNER), jnp.float32) * s, 'b_dt': jnp.zeros((D_INNER,), jnp.float32), 'A_log': jax.random.uniform(ks[5], (D_INNER, D_STATE), jnp.float32, -0.05, 0.05), 'W_out': jax.random.normal(ks[6], (D_INNER, D_MODEL), jnp.float32) * s}
    _L0_attn_in = _L0_attn_setup()

    def _L0_ffn_setup():
        import jax, jax.numpy as jnp
        import numpy as np
        import math
        B, L, D = (4, 1024, 256)
        F = 1024
        E = 16
        CAP_FACTOR = 1.0
        EPS = 1e-05
        key = jax.random.key(seed)
        ks = jax.random.split(key, 8)
        std = 0.02
        return {'x': jax.random.normal(ks[0], (B, L, D), dtype=jnp.float32), 'norm_weight': jnp.ones((D,), dtype=jnp.float32), 'router_weight': jax.random.normal(ks[1], (E, D), dtype=jnp.float32) * std, 'router_bias': jnp.zeros((E,), dtype=jnp.float32), 'fc1_weight': jax.random.normal(ks[2], (E, F, D), dtype=jnp.float32) * std, 'fc1_bias': jnp.zeros((E, F), dtype=jnp.float32), 'fc2_weight': jax.random.normal(ks[3], (E, D, F), dtype=jnp.float32) * std, 'fc2_bias': jnp.zeros((E, D), dtype=jnp.float32)}
    _L0_ffn_in = _L0_ffn_setup()
    _d = {'L0_attn_inputs': _L0_attn_in['inputs'], 'L0_attn_W_in': _L0_attn_in['W_in'], 'L0_attn_conv_w': _L0_attn_in['conv_w'], 'L0_attn_conv_b': _L0_attn_in['conv_b'], 'L0_attn_W_x': _L0_attn_in['W_x'], 'L0_attn_W_dt': _L0_attn_in['W_dt'], 'L0_attn_b_dt': _L0_attn_in['b_dt'], 'L0_attn_A_log': _L0_attn_in['A_log'], 'L0_attn_W_out': _L0_attn_in['W_out'], 'L0_ffn_norm_weight': _L0_ffn_in['norm_weight'], 'L0_ffn_router_weight': _L0_ffn_in['router_weight'], 'L0_ffn_router_bias': _L0_ffn_in['router_bias'], 'L0_ffn_fc1_weight': _L0_ffn_in['fc1_weight'], 'L0_ffn_fc1_bias': _L0_ffn_in['fc1_bias'], 'L0_ffn_fc2_weight': _L0_ffn_in['fc2_weight'], 'L0_ffn_fc2_bias': _L0_ffn_in['fc2_bias']}
    _x0 = _d['L0_attn_inputs']
    _d['L0_attn_inputs'] = jax.random.normal(jax.random.fold_in(jax.random.key(seed), 1), (2, 2048, 256), dtype=_x0.dtype)
    del _x0
    return _d

def reference(L0_attn_inputs, L0_attn_W_in, L0_attn_conv_w, L0_attn_conv_b, L0_attn_W_x, L0_attn_W_dt, L0_attn_b_dt, L0_attn_A_log, L0_attn_W_out, L0_ffn_norm_weight, L0_ffn_router_weight, L0_ffn_router_bias, L0_ffn_fc1_weight, L0_ffn_fc1_bias, L0_ffn_fc2_weight, L0_ffn_fc2_bias):

    def _L0_attn_ref(inputs, W_in, conv_w, conv_b, W_x, W_dt, b_dt, A_log, W_out):
        import jax, jax.numpy as jnp
        from jax import lax
        import numpy as np
        D_MODEL, D_STATE, D_CONV, EXPAND = (256, 16, 4, 2)
        D_INNER = EXPAND * D_MODEL
        BATCH, SEQ = (2, 256)

        def _selective_scan(u, delta, A, B, C, D):
            u_T = jnp.swapaxes(u, 0, 1)
            delta_T = jnp.swapaxes(delta, 0, 1)
            B_T = jnp.swapaxes(B, 0, 1)
            C_T = jnp.swapaxes(C, 0, 1)

            def step(prev_x, inp):
                delta_t, B_t, u_t = inp
                dA = jnp.exp(jnp.einsum('bi,is->bis', delta_t, A))
                dB_u = jnp.einsum('bi,bs,bi->bis', delta_t, B_t, u_t)
                x_t = dA * prev_x + dB_u
                return (x_t, x_t)
            init = jnp.zeros((u.shape[0], D_INNER, D_STATE), u.dtype)
            _, states = lax.scan(step, init, (delta_T, B_T, u_T))
            y = jnp.einsum('lbis,lbs->lbi', states, C_T) + u_T * D
            return jnp.swapaxes(y, 0, 1)
        xz = inputs @ W_in
        x, z = jnp.split(xz, 2, axis=-1)
        x = lax.conv_general_dilated(x, conv_w, window_strides=(1,), padding=[(D_CONV - 1, 0)], dimension_numbers=('NWC', 'WIO', 'NWC'), feature_group_count=D_INNER) + conv_b
        x = jax.nn.silu(x)
        x_dbl = x @ W_x
        dt_in, Bm, Cm = jnp.split(x_dbl, [D_MODEL, D_MODEL + D_STATE], axis=-1)
        dt = jax.nn.softplus(dt_in @ W_dt + b_dt)
        A = -jnp.exp(A_log)
        D = jnp.ones((D_INNER,), inputs.dtype)
        y = _selective_scan(x, dt, A, Bm, Cm, D)
        y = y * jax.nn.silu(z)
        return y @ W_out

    def _L0_ffn_ref(x, norm_weight, router_weight, router_bias, fc1_weight, fc1_bias, fc2_weight, fc2_bias):
        import jax, jax.numpy as jnp
        import numpy as np
        import math
        B, L, D = (4, 1024, 256)
        F = 1024
        E = 16
        CAP_FACTOR = 1.0
        EPS = 1e-05
        b, l, d = x.shape
        n_tokens = b * l
        n_experts = router_weight.shape[0]
        capacity = max(1, math.ceil(CAP_FACTOR * n_tokens / n_experts))
        top_k = min(capacity, n_tokens)
        xf = x.reshape(n_tokens, d)
        rms = jnp.sqrt(jnp.mean(xf * xf, axis=-1, keepdims=True) + EPS)
        xn = xf / rms * norm_weight
        logits = xn @ router_weight.T + router_bias
        probs = jax.nn.softmax(logits, axis=-1)
        _, idx = jax.lax.top_k(logits.T, top_k)
        xe = xn[idx]
        h = jnp.einsum('ecd,efd->ecf', xe, fc1_weight) + fc1_bias[:, None, :]
        h = jax.nn.gelu(h, approximate=False)
        y = jnp.einsum('ecf,edf->ecd', h, fc2_weight) + fc2_bias[:, None, :]
        gates = jnp.take_along_axis(probs.T, idx, axis=1)
        flat_idx = idx.reshape(-1)
        contrib = (y * gates[:, :, None]).reshape(-1, d)
        output = jnp.zeros((n_tokens, d), dtype=x.dtype).at[flat_idx].add(contrib)
        gate_sums = jnp.zeros((n_tokens, 1), dtype=x.dtype).at[flat_idx].add(gates.reshape(-1, 1))
        assigned = gate_sums > 0
        output = jnp.where(assigned, output / jnp.where(assigned, gate_sums, 1.0), output)
        return output.reshape(b, l, d)
    x = L0_attn_inputs
    x = x + _L0_attn_ref(_layernorm(x, axis=-1), L0_attn_W_in, L0_attn_conv_w, L0_attn_conv_b, L0_attn_W_x, L0_attn_W_dt, L0_attn_b_dt, L0_attn_A_log, L0_attn_W_out)
    x = x + _L0_ffn_ref(_layernorm(x, axis=-1), L0_ffn_norm_weight, L0_ffn_router_weight, L0_ffn_router_bias, L0_ffn_fc1_weight, L0_ffn_fc1_bias, L0_ffn_fc2_weight, L0_ffn_fc2_bias)
    return x

_drawn_inputs = setup_inputs


def setup_inputs(seed=0):
    import zlib

    import numpy as np

    out = dict(_drawn_inputs(seed))
    spreads = {'L0_attn_conv_b': (0.0, 0.776),
     'L0_attn_b_dt': (0.0, 0.8),
     'L0_ffn_norm_weight': (1.0, 0.6),
     'L0_ffn_router_bias': (0.0, 2.0),
     'L0_ffn_fc1_bias': (0.0, 2.0),
     'L0_ffn_fc2_bias': (0.0, 0.8)}
    factors = {'L0_attn_W_in': 6.348,
     'L0_attn_conv_w': 8.0,
     'L0_attn_W_x': 8.0,
     'L0_attn_W_dt': 8.0,
     'L0_attn_A_log': 8.0,
     'L0_attn_W_out': 5.842,
     'L0_ffn_router_weight': 8.0,
     'L0_ffn_fc1_weight': 8.0,
     'L0_ffn_fc2_weight': 8.0}
    for name, (base, spread) in spreads.items():
        noise = np.random.default_rng([zlib.crc32(name.encode()), seed]).standard_normal(out[name].shape)
        drawn = base * np.exp(spread * noise) if base else spread * noise
        out[name] = jnp.asarray(drawn.astype(out[name].dtype))
    for name, factor in factors.items():
        out[name] = (out[name] * factor).astype(out[name].dtype)
    return out
```

```python
from contextlib import ExitStack

import concourse.bass as bass
from concourse import mybir

ALU = mybir.AluOpType
ACT = mybir.ActivationFunctionType
AX = mybir.AxisListType
F32 = mybir.dt.float32
BF16 = mybir.dt.bfloat16
I32 = mybir.dt.int32

P = 128
EPS = 1e-5
LOG_SET = "natural_log_exp_and_others"
SILU_SET = "silu_and_others"
SOFTPLUS_LINEAR = 40.0


def mixer_moe(nc, x, w_in, conv_w, conv_b, w_x, w_dt, b_dt, a_log, w_out,
              norm_w, w_router, b_router, w_fc1, b_fc1, w_fc2, b_fc2, out):
    BATCH, SEQ, D = x.shape
    DI = w_dt.shape[1]
    NS = a_log.shape[1]
    TAPS = conv_w.shape[0]
    E, F, _ = w_fc1.shape
    N = BATCH * SEQ
    TC = 512
    TT = TC // P
    KD = D // P
    IB = DI // P
    KF = F // P
    CAP = N // E
    CH = CAP // P
    CHUNKS = N // TC
    TILES = N // P
    assert BATCH == 2 and TC == 512 and NS == 16 and E == 16 and CHUNKS == 8 and CAP == 256

    x_rows = x.rearrange("b (c t p) d -> (b c) p t d", t=TT, p=P)
    out_rows = out.rearrange("b (c t p) d -> (b c) p t d", t=TT, p=P)
    out_flat = out.rearrange("b s d -> (b s) d")

    b_scratch = nc.dram_tensor("b_scratch", [2, NS, TC], F32, kind="Internal").ap()
    xhat_dram = nc.dram_tensor("xhat_dram", [N, D], F32, kind="Internal").ap()
    xhat_rows = xhat_dram.rearrange("(c t p) d -> c p t d", t=TT, p=P)
    logit_dram = nc.dram_tensor("logit_dram", [E, N], F32, kind="Internal").ap()
    logit_chunks = logit_dram.rearrange("e (c t) -> c e t", t=TC)
    list_dram = nc.dram_tensor("list_dram", [2, E * CH, P], F32, kind="Internal").ap()

    with ExitStack() as ctx:
        def sb(name, shape, dt=F32):
            return ctx.enter_context(nc.sbuf_tensor(name, shape, dt))

        def psum(name, shape, dt=F32):
            return ctx.enter_context(nc.psum_tensor(name, shape, dt))

        def sem(name):
            return ctx.enter_context(nc.semaphore(name))

        ident = sb("ident", [P, P])
        ones = sb("ones", [P, P])
        NVEC = TAPS * IB + IB + IB + KD
        CONVB, BDT, NW = TAPS * IB, TAPS * IB + IB, TAPS * IB + 2 * IB
        vec_rows = sb("vec_rows", [32, P])
        vecs = sb("vecs", [P, 32])
        b1_rows = sb("b1_rows", [P, P])
        b1_cols = sb("b1_cols", [P, E * KF])
        b_router_sb = sb("b_router_sb", [E, 1])
        w_router_rows = sb("w_router_rows", [E, D])
        w_router_T = sb("w_router_T", [P, KD, E])

        consts_loaded = sem("consts_loaded")
        weights_loaded = sem("weights_loaded")
        ident_ready = sem("ident_ready")
        vec_turned = sem("vec_turned")
        vec_ready = sem("vec_ready")
        a_ready = sem("a_ready")
        carry_zeroed = sem("carry_zeroed")
        wait_held = sem("wait_held")

        x_loaded = sem("x_loaded")
        xres_loaded = sem("xres_loaded")
        stats_in = sem("stats_in")
        aggr_in = sem("aggr_in")
        rs_in = sem("rs_in")
        nw_in = sem("nw_in")
        xn_ready = sem("xn_ready")
        taps_added = sem("taps_added")
        tail_kept = sem("tail_kept")
        u_ready = sem("u_ready")
        zg_ready = sem("zg_ready")
        b_stored = sem("b_stored")
        dtmin_ready = sem("dtmin_ready")
        sp_ready = sem("sp_ready")
        dt_ready = sem("dt_ready")
        du_ready = sem("du_ready")
        mm_full = sem("mm_full")
        mm_free = [sem("mm_free0"), sem("mm_free1")]

        NBB = 4
        bb_loaded = [sem(f"bb_loaded{k}") for k in range(NBB)]
        da_ready = sem("da_ready")
        db_ready = sem("db_ready")
        scan_done = sem("scan_done")
        carry_kept = sem("carry_kept")
        ht_ready = sem("ht_ready")
        y_started = sem("y_started")
        y_added = sem("y_added")
        y_gated = sem("y_gated")
        x1_ready = sem("x1_ready")
        stats_mid = sem("stats_mid")
        aggr_mid = sem("aggr_mid")
        rs_mid = sem("rs_mid")
        nw_mid = sem("nw_mid")
        xhat_ready = sem("xhat_ready")
        x1_stored = sem("x1_stored")
        xhat_stored = sem("xhat_stored")
        logit_stored = sem("logit_stored")

        SLOTS = [["yT0", "yT1", "yT2", "yT3"], ["xnT0", "xnT1", "out0"], ["xi0", "xi1"], ["xi2", "xi3"],
                 ["out1", "out2"], ["out3"], ["bc"], ["dti0"], ["dti1"], ["ct", "dt0", "dt1"],
                 ["dt2", "dt3"], ["z0", "z1"], ["z2", "xhT0", "xhT1"], ["z3", "rt0"], ["rt1"], []]
        OF_POST = ("yT", "out", "xhT", "rt")
        BOTH = [name for slot in SLOTS for name in slot]
        POST = [name for name in BOTH if name.startswith(OF_POST)]
        PRE = [name for name in BOTH if not name.startswith(OF_POST)]
        NPOST, NPRE = len(POST), len(PRE)
        assert NPOST % 2 == 0 and NPRE % 2 == 0

        def uses(s, post, pre):
            return [name for name in SLOTS[s] if (post if name.startswith(OF_POST) else pre)]

        def mm_number(q, post, pre, name):
            order = BOTH if post and pre else POST if post else PRE
            if isinstance(q, int) and q < 1:
                base = NPRE * (q + 1)
            elif isinstance(q, int):
                base = NPRE * min(q + 1, CHUNKS) + NPOST * (q - 1)
            else:
                base = q * (NPRE + NPOST) + (NPRE - NPOST)
            return base, order.index(name)

        def wait(eng, semaphore, value):
            if not isinstance(value, int) or value > 0:
                eng.wait_ge(semaphore, value)

        def banks_before(q, post, pre, name):
            base, k = mm_number(q, post, pre, name)
            bank = k % 2
            if isinstance(base, int):
                return bank, base // 2 + k // 2
            return bank, q * ((NPRE + NPOST) // 2) + ((NPRE - NPOST) // 2 + k // 2)

        def mm_take(q, post, pre, name):
            bank, before = banks_before(q, post, pre, name)
            wait(nc.tensor, mm_free[bank], before)
            return mm[bank]

        def mm_wait(eng, q, post, pre, name):
            base, k = mm_number(q, post, pre, name)
            bank = k % 2
            eng.wait_ge(mm_full, base + (k + 1))
            return mm[bank], mm_free[bank]

        def evacuated(eng, q, post, pre, name):
            bank, before = banks_before(q, post, pre, name)
            eng.wait_ge(mm_free[bank], before + 1)

        def evacuated_before(eng, q, post, pre):
            order = BOTH if post and pre else POST if post else PRE
            for name in order[0:2]:
                bank, before = banks_before(q, post, pre, name)
                wait(eng, mm_free[bank], before)

        def body(chunk):
            def run(eng):
                chunk(-1, 1, 0, units=False, post=False, pre=True)
                chunk(0, 0, 0, units=True, post=False, pre=True)
                with eng.Fori(0, (CHUNKS - 2) // 2) as pair:
                    chunk(pair * 2 + 1, 1, pair, units=True, post=True, pre=True)
                    chunk(pair * 2 + 2, 0, pair, units=True, post=True, pre=True)
                chunk(CHUNKS - 1, 1, CHUNKS // 2 - 1, units=True, post=True, pre=False)
                chunk(CHUNKS, 0, CHUNKS // 2, units=False, post=True, pre=False)
            return run

        with ExitStack() as part1:
            def sb1(name, shape, dt=F32):
                return part1.enter_context(nc.sbuf_tensor(name, shape, dt))

            w_in_sb = sb1("w_in_sb", [P, KD, 2 * DI])
            w_x_sb = sb1("w_x_sb", [P, IB, D + 2 * NS])
            w_dt_sb = sb1("w_dt_sb", [P, KD, DI])
            w_out_sb = sb1("w_out_sb", [P, IB, D])
            a_raw = sb1("a_raw", [P, IB, NS])
            a_exp = sb1("a_exp", [P, IB, NS])
            a_sb = sb1("a_sb", [P, IB, NS])
            newton = sb1("newton", [P, 3, TT])
            eps_mid = sb1("eps_mid", [P, 2, TT])

            x_in = sb1("x_in", [P, TT, D])
            st_in = sb1("st_in", [P, TT, 6])
            mv_in = sb1("mv_in", [P, TT, 2])
            nt_in = sb1("nt_in", [P, 8, TT])
            xn = sb1("xn", [P, TT, D])
            xnT = sb1("xnT", [P, KD, TC])
            xpad = [sb1(f"xpad{k}", [P, IB, TAPS - 1 + TC]) for k in range(2)]
            conv = sb1("conv", [P, IB, TC])
            u = [sb1(f"u{k}", [P, IB, TC]) for k in range(2)]
            zg = [sb1(f"zg{k}", [P, TT, DI]) for k in range(2)]
            bc = sb1("bc", [2 * NS, TC])
            c_tok = [sb1(f"c_tok{k}", [P, TT, 2 * NS]) for k in range(2)]
            dt_in = sb1("dt_in", [P, KD, TC])
            dt_min = conv
            dt = [sb1(f"dt{k}", [P, IB, TC]) for k in range(2)]
            dt_raw = dt
            du = [sb1(f"du{k}", [P, IB, TC]) for k in range(2)]
            bb = [sb1(f"bb{k}", [P, TC]) for k in range(NBB)]
            db = [sb1(f"db{k}", [P, IB, TC]) for k in range(2)]
            h = [sb1(f"h{k}", [P, IB, TC]) for k in range(2)]
            carry = sb1("carry", [P, 2, NS, IB])
            y = sb1("y", [P, TT, DI])
            yg = sb1("yg", [P, TT, DI])
            x_res = sb1("x_res", [P, TT, D])
            x1 = x_res
            st_mid = sb1("st_mid", [P, TT, 6])
            mv_mid = sb1("mv_mid", [P, TT, 2])
            nt_mid = sb1("nt_mid", [P, 8, TT])
            xhat = sb1("xhat", [P, TT, D])
            xhatT = sb1("xhatT", [P, KD, TC])
            logitT = sb1("logitT", [E, TC])

            da = [part1.enter_context(nc.psum_tensor(f"da{k}", [P, TC], F32)) for k in range(4)]
            hT = [part1.enter_context(nc.psum_tensor(f"hT{k}", [P, DI], F32)) for k in range(2)]
            mm = [part1.enter_context(nc.psum_tensor(f"mm{k}", [P, TC], F32)) for k in range(2)]

            with nc.Block() as block:

                @block.sync
                def _(sp):
                    conv_rows = conv_w.rearrange("k a (i p) -> (k a i) p", p=P)
                    sp.dma_start(x_in[:], x_rows[0]).then_inc(x_loaded, 16)
                    for dst, src in (
                        (vec_rows[0:CONVB, :], conv_rows),
                        (vec_rows[CONVB:BDT, :], conv_b.rearrange("(i p) -> i p", p=P)),
                        (vec_rows[BDT:NW, :], b_dt.rearrange("(i p) -> i p", p=P)),
                        (vec_rows[NW:NVEC, :], norm_w.rearrange("(i p) -> i p", p=P)),
                        (b1_rows[:], b_fc1.rearrange("e (f p) -> (e f) p", p=P)),
                        (w_router_rows[:], w_router),
                        (b_router_sb[:], b_router.rearrange("(e a) -> e a", a=1)),
                        (a_raw[:], a_log.rearrange("(i p) s -> p i s", p=P)),
                    ):
                        sp.dma_start(dst, src).then_inc(consts_loaded, 16)
                    for dst, src in (
                        (w_in_sb[:], w_in.rearrange("(k p) n -> p k n", p=P)),
                        (w_x_sb[:], w_x.rearrange("(k p) n -> p k n", p=P)),
                        (w_dt_sb[:], w_dt.rearrange("(k p) n -> p k n", p=P)),
                        (w_out_sb[:], w_out.rearrange("(k p) n -> p k n", p=P)),
                    ):
                        sp.dma_start(dst, src).then_inc(weights_loaded, 16)

                    def chunk(q, par, pair, units, post, pre):
                        if isinstance(q, int):
                            prev = (1 - par) * (CHUNKS // 2) + (q - 1) // 2
                            following = (1 - par) * (CHUNKS // 2) + (q + 1) // 2
                        elif par == 1:
                            prev, following = pair, pair + 1
                        else:
                            prev, following = pair + CHUNKS // 2, pair + (CHUNKS // 2 + 1)
                        a = q + 1
                        nxt = 1 - par
                        if pre and units:
                            wait(sp, xn_ready, a * TT)
                            sp.sem_inc(wait_held, 1)
                            sp.dma_start(x_in[:], x_rows[following]).then_inc(x_loaded, 16)
                        if post:
                            wait(sp, x1_stored, (q - 1) * 16)
                            sp.sem_inc(wait_held, 1)
                            wait(sp, xhat_ready, (q - 1) * TT)
                            sp.sem_inc(wait_held, 1)
                            sp.dma_start(x_res[:], x_rows[prev]).then_inc(xres_loaded, 16)
                        if units:
                            sp.wait_ge(b_stored, (q + 1) * 16)
                            sp.sem_inc(wait_held, 1)
                            for s in range(NS):
                                wait(sp, db_ready, q * NS + (s - NBB + 1))
                                sp.dma_start(bb[s % NBB][:], b_scratch[par, s:s + 1, :].partition_broadcast(P)
                                             ).then_inc(bb_loaded[s % NBB], 16)
                                if s == 11 and pre:
                                    store_b(q, nxt, post)
                                if s == 13 and post:
                                    store_rows(q, prev, pre)
                        else:
                            if pre:
                                store_b(q, nxt, post)
                            if post:
                                store_rows(q, prev, pre)
                        if post:
                            store_logits(q, prev, pre)

                    def store_b(q, nxt, post):
                        evacuated(sp, q, post, True, "bc")
                        for k in range(NBB):
                            sp.sem_inc(wait_held, 1)
                            wait(sp, bb_loaded[k], q * ((NS // NBB) * 16))
                        sp.dma_start(b_scratch[nxt], bc[0:NS, :]).then_inc(b_stored, 16)

                    def store_rows(q, prev, pre):
                        sp.wait_ge(x1_ready, q)
                        sp.sem_inc(wait_held, 1)
                        sp.dma_start(out_rows[prev], x1[:]).then_inc(x1_stored, 16)
                        sp.wait_ge(xhat_ready, q * TT)
                        sp.sem_inc(wait_held, 1)
                        sp.dma_start(xhat_rows[prev], xhat[:]).then_inc(xhat_stored, 16)

                    def store_logits(q, prev, pre):
                        for k in range(2):
                            evacuated(sp, q, True, pre, f"rt{k}")
                            sp.sem_inc(wait_held, 1)
                        sp.dma_start(logit_chunks[prev], logitT[:]).then_inc(logit_stored, 16)

                    body(chunk)(sp)
                    sp.wait_ge(x1_stored, CHUNKS * 16)
                    sp.wait_ge(xhat_stored, CHUNKS * 16)
                    sp.wait_ge(logit_stored, CHUNKS * 16)
                    sp.wait_ge(weights_loaded, 4 * 16)

                @block.gpsimd
                def _(pool):
                    pool.memset(ident[:], 0.0).then_inc(ident_ready, 1)
                    pool.memset(ones[:], 1.0)
                    for k, v in enumerate((EPS, -0.5, 1.5)):
                        pool.memset(newton[:, k, :], v)
                    pool.memset(eps_mid[:, 0, :], 1.0 + EPS)
                    pool.memset(eps_mid[:, 1, :], EPS * EPS)
                    for k in range(2):
                        pool.memset(xpad[k][:, :, 0:TAPS - 1], 0.0)
                    pool.memset(carry[:], 0.0).then_inc(carry_zeroed, 1)
                    pool.wait_ge(ident_ready, 1)
                    pool.affine_select(out=ident[:], in_=ident[:], compare_op=ALU.not_equal, fill=1.0,
                                       base=0, pattern=[[-1, P]], channel_multiplier=1).then_inc(ident_ready, 1)
                    pool.wait_ge(carry_zeroed, 1)
                    pool.wait_ge(a_ready, 1)
                    pool.tensor_scalar(a_sb[:], a_exp[:], -1.0, None, ALU.mult).then_inc(a_ready, 1)

                    def newton_step(nt, done, at, rows):
                        ops = [(3, 0, 2), (4, 3, 2), (5, 4, newton[:, 1, :]), (6, 5, newton[:, 2, :]), (7, 6, 2)]
                        for k, (o, i, j) in enumerate(ops):
                            in1 = j if not isinstance(j, int) else nt[:, j, :]
                            op = ALU.add if k == 3 else ALU.mult
                            pool.wait_ge(done, at + k)
                            pool.tensor_tensor(nt[:, o, :], nt[:, i, :], in1, op).then_inc(done, 1)

                    NIN, NMID = 7, 8

                    def norm_in(a):
                        wait(pool, xn_ready, a * TT)
                        pool.wait_ge(aggr_in, a * TT + TT)
                        pool.tensor_tensor(nt_in[:, 0, :], mv_in[:, :, 1], newton[:, 0, :], ALU.add).then_inc(nw_in, 1)
                        pool.wait_ge(rs_in, a * 2 + 2)
                        newton_step(nt_in, nw_in, a * 6 + 1, NIN)

                    def norm_mid(p):
                        wait(pool, xhat_ready, p * TT)
                        pool.wait_ge(aggr_mid, p * TT + TT)
                        pool.tensor_tensor(nt_mid[:, 1, :], mv_mid[:, :, 1], eps_mid[:, 0, :], ALU.mult).then_inc(nw_mid, 1)
                        pool.wait_ge(nw_mid, p * 7 + 1)
                        pool.tensor_tensor(nt_mid[:, 0, :], nt_mid[:, 1, :], eps_mid[:, 1, :], ALU.add).then_inc(nw_mid, 1)
                        pool.wait_ge(rs_mid, p * 2 + 2)
                        newton_step(nt_mid, nw_mid, p * 7 + 2, NMID)

                    def chunk(q, par, pair, units, post, pre):
                        a = q + 1
                        nxt = 1 - par
                        for s in range(NS):
                            if units:
                                pool.wait_ge(bb_loaded[s % NBB], (q * (NS // NBB) + (s // NBB + 1)) * 16)
                                if s == 0:
                                    pool.wait_ge(du_ready, q + 1)
                                wait(pool, scan_done, q * (NS * IB) + (s - 2) * IB + IB)
                                pool.tensor_tensor(db[s % 2][:], du[par][:],
                                                   bb[s % NBB][:].unsqueeze(1).broadcast_to([P, IB, TC]),
                                                   ALU.mult).then_inc(db_ready, 1)
                            if post and s == 10:
                                norm_mid(q - 1)
                            if pre and s == 1:
                                norm_in(a)
                            if pre and s == 15:
                                pool.wait_ge(dt_ready, a + 1)
                                pool.wait_ge(u_ready, a + 1)
                                pool.tensor_tensor(du[nxt][:], dt[nxt][:], u[nxt][:], ALU.mult).then_inc(du_ready, 1)

                    body(chunk)(pool)

                @block.scalar
                def _(act):
                    act.preload_act_table_set(LOG_SET)
                    act.wait_ge(consts_loaded, 8 * 16)
                    act.activation(a_exp[:], a_raw[:], ACT.Exp).then_inc(a_ready, 1)
                    act.wait_ge(vec_turned, 1)
                    act.activation(vecs[:, 0:NVEC], mm[0][:, 0:NVEC], ACT.Copy).then_inc(vec_ready, 1)
                    act.activation(b1_cols[:], mm[0][:, 128:256], ACT.Copy).then_inc(vec_ready, 1)
                    act.wait_ge(vec_ready, 2)
                    for k in range(KD):
                        act.activation(w_router_T[:, k, :], mm[0][:, 256 + k * E:256 + (k + 1) * E], ACT.Copy,
                                       scale=vecs[:, NW + k:NW + k + 1]).then_inc(vec_ready, 1)
                    act.wait_ge(a_ready, 2)
                    act.wait_ge(weights_loaded, 4 * 16)

                    def chunk(q, par, pair, units, post, pre):
                        a = q + 1
                        p = q - 1
                        nxt = 1 - par

                        for step in range(NS + 2):
                            s = step
                            if units and step < NS:
                                if s == 0:
                                    act.wait_ge(dt_ready, q + 1)
                                for i in range(IB):
                                    wait(act, scan_done, q * (NS * IB) + ((s - 1) * IB + i + 1))
                                    act.activation(da[i][:], dt[par][:, i, :], ACT.Exp,
                                                   scale=a_sb[:, i, s:s + 1]).then_inc(da_ready, 1)
                                if s == 0:
                                    wait(act, y_gated, q)
                                    for t in range(TT):
                                        act.wait_ge(ht_ready, q * ((NS + 1) * TT) + (t + 1))
                                        act.activation(y[:, t, :], hT[t % 2][:], ACT.Copy).then_inc(y_started, 1)
                            if pre and step == 1:
                                act.wait_ge(nw_in, a * 6 + 1)
                                act.activation(nt_in[:, 1, :], nt_in[:, 0, :], ACT.Ln).then_inc(rs_in, 1)
                                act.wait_ge(rs_in, a * 2 + 1)
                                act.activation(nt_in[:, 2, :], nt_in[:, 1, :], ACT.Exp, scale=-0.5).then_inc(rs_in, 1)
                            if step == 6 and (pre or units):
                                act.preload_act_table_set(SILU_SET)
                                if pre:
                                    act.wait_ge(taps_added, a * ((TAPS - 1) * IB) + (TAPS - 1) * IB)
                                    act.activation(u[nxt][:], conv[:], ACT.Silu).then_inc(u_ready, 1)
                                if units:
                                    evacuated_before(act, q, post, pre)
                                    act.activation(zg[par][:], zg[par][:], ACT.Silu).then_inc(zg_ready, 1)
                                act.preload_act_table_set(LOG_SET)
                            if post and step == 10:
                                act.wait_ge(nw_mid, p * 7 + 2)
                                act.activation(nt_mid[:, 1, :], nt_mid[:, 0, :], ACT.Ln).then_inc(rs_mid, 1)
                                act.wait_ge(rs_mid, p * 2 + 1)
                                act.activation(nt_mid[:, 2, :], nt_mid[:, 1, :], ACT.Exp, scale=-0.5).then_inc(rs_mid, 1)
                            if pre and step == 13:
                                act.wait_ge(dtmin_ready, a + 1)
                                act.activation(dt_min[:], dt_min[:], ACT.Exp).then_inc(sp_ready, 1)
                                act.wait_ge(sp_ready, a * 2 + 1)
                                act.activation(dt_min[:], dt_min[:], ACT.Ln, bias=1.0).then_inc(sp_ready, 1)
                            s = step - 2
                            if s < 0:
                                continue
                            for name in uses(s, post, pre):
                                evacuate(q, a, p, nxt, post, pre, name)

                    def evacuate(q, a, p, nxt, post, pre, name):
                        kind, k = name.rstrip("0123456789"), int(name[-1]) if name[-1].isdigit() else 0
                        if name == "out0":
                            wait(act, xhat_stored, p * 16)
                        if name == "xi0":
                            wait(act, tail_kept, a - 1)
                            wait(act, dt_ready, a)
                        if name == "rt0":
                            wait(act, logit_stored, p * 16)
                        if name == "bc":
                            wait(act, b_stored, a * 16)
                        bank, free = mm_wait(act, q, post, pre, name)
                        if kind == "xi":
                            act.activation(conv[:, k, :], bank[:], ACT.Identity,
                                           scale=vecs[:, (TAPS - 1) * IB + k:(TAPS - 1) * IB + k + 1],
                                           bias=vecs[:, CONVB + k:CONVB + k + 1])
                        dst, src, func, kw = {
                            "yT": (du[nxt][:, k, :], bank[:], ACT.Copy, {}),
                            "xnT": (xnT[:, k % KD, :], bank[:], ACT.Copy, {}),
                            "xhT": (xhatT[:, k % KD, :], bank[:], ACT.Copy, {}),
                            "out": (xhat[:, k % TT, :], bank[:, 0:D], ACT.Copy, {}),
                            "xi": (xpad[nxt][:, k, TAPS - 1:], bank[:], ACT.Copy, {}),
                            "z": (zg[nxt][:, k, :], bank[:], ACT.Copy, {}),
                            "bc": (bc[:], bank[0:2 * NS, :], ACT.Copy, {}),
                            "dti": (dt_in[:, k % KD, :], bank[:], ACT.Copy, {}),
                            "ct": (c_tok[nxt][:].rearrange("p t s -> p (t s)"), bank[:, 0:TT * 2 * NS], ACT.Copy, {}),
                            "dt": (dt_raw[nxt][:, k, :], bank[:], ACT.Identity, {"bias": vecs[:, BDT + k:BDT + k + 1]}),
                            "rt": (logitT[:, (k % 2) * 256:(k % 2 + 1) * 256], bank[0:E, 0:256], ACT.Identity,
                                   {"bias": b_router_sb[:, 0:1]}),
                        }[kind]
                        act.activation(dst, src, func, **kw).then_inc(free, 1)

                    body(chunk)(act)

                @block.tensor
                def _(pe):
                    pe.wait_ge(ident_ready, 2)
                    pe.wait_ge(consts_loaded, 8 * 16)
                    pe.transpose(mm[0][:, 0:NVEC], vec_rows[0:NVEC, :], ident[0:NVEC, 0:NVEC])
                    pe.transpose(mm[0][:, 128:256], b1_rows[:], ident[:])
                    for k in range(KD):
                        last = pe.transpose(mm[0][:, 256 + k * E:256 + (k + 1) * E], w_router_rows[:, k * P:(k + 1) * P],
                                            ident[0:E, 0:E])
                    last.then_inc(vec_turned, 1)
                    pe.wait_ge(vec_ready, 2 + KD)
                    pe.wait_ge(weights_loaded, 4 * 16)

                    def chunk(q, par, pair, units, post, pre):
                        a = q + 1
                        p = q - 1
                        nxt = 1 - par

                        if units:
                            for t in range(TT):
                                if t < 2:
                                    wait(pe, y_added, q * (NS * TT) - (1 - t))
                                else:
                                    pe.wait_ge(y_started, q * TT + (t - 1))
                                for i in range(IB):
                                    last = pe.transpose(hT[t % 2][:, i * P:(i + 1) * P],
                                                        u[par][:, i, t * P:(t + 1) * P], ident[:])
                                last.then_inc(ht_ready, 1)
                        for s in range(NS):
                            if units:
                                pe.wait_ge(scan_done, q * (NS * IB) + (s + 1) * IB)
                                for t in range(TT):
                                    n = q * (NS * TT) + (s * TT + t - 1)
                                    if s == 0 and t < 2:
                                        pe.wait_ge(y_started, q * TT + (t + 3))
                                    else:
                                        pe.wait_ge(y_added, n)
                                    for i in range(IB):
                                        last = pe.transpose(hT[t % 2][:, i * P:(i + 1) * P],
                                                            h[s % 2][:, i, t * P:(t + 1) * P], ident[:])
                                    last.then_inc(ht_ready, 1)
                            for name in uses(s, post, pre):
                                product(q, a, p, nxt, post, pre, name)

                    def product(q, a, p, nxt, post, pre, name):
                        kind, k = name.rstrip("0123456789"), int(name[-1]) if name[-1].isdigit() else 0

                        def ready(*names):
                            for n in names:
                                evacuated(pe, q, post, pre, n)

                        if name == "yT0":
                            pe.wait_ge(y_gated, q)
                        if name == "xnT0":
                            pe.wait_ge(xn_ready, a * TT + TT)
                        if name == "xhT0":
                            pe.wait_ge(xhat_ready, p * TT + TT)
                        if name == "out0":
                            ready("yT2", "yT3")
                        if name == "xi0":
                            ready("xnT0", "xnT1")
                        if name == "rt0":
                            ready("xhT0", "xhT1")
                        if name == "bc":
                            pe.wait_ge(u_ready, a + 1)
                        if name == "ct":
                            ready("bc")
                        if name == "dt0":
                            ready("dti0", "dti1")
                        bank = mm_take(q, post, pre, name)
                        if kind == "ct":
                            pe.sem_inc(wait_held, 1)
                            for t in range(TT):
                                last = pe.transpose(bank[:, t * 2 * NS:(t + 1) * 2 * NS], bc[:, t * P:(t + 1) * P],
                                                    ident[0:2 * NS, 0:2 * NS])
                        elif kind in ("yT", "xnT", "xhT"):
                            src = {"yT": yg, "xnT": xn, "xhT": xhat}[kind]
                            for t in range(TT):
                                last = pe.transpose(bank[:, t * P:(t + 1) * P], src[:, t, k * P:(k + 1) * P], ident[:])
                        else:
                            tile = slice(k * P, (k + 1) * P)
                            dst, lhsT, rhs, n = {
                                "xi": (bank[:], lambda j: w_in_sb[:, j, tile], lambda j: xnT[:, j, :], KD),
                                "z": (bank[:], lambda j: xnT[:, j, tile], lambda j: w_in_sb[:, j, DI:2 * DI], KD),
                                "bc": (bank[0:2 * NS, :], lambda j: w_x_sb[:, j, D:D + 2 * NS],
                                       lambda j: u[nxt][:, j, :], IB),
                                "dti": (bank[:], lambda j: w_x_sb[:, j, tile], lambda j: u[nxt][:, j, :], IB),
                                "dt": (bank[:], lambda j: w_dt_sb[:, j, tile], lambda j: dt_in[:, j, :], KD),
                                "out": (bank[:, 0:D], lambda j: du[nxt][:, j, tile], lambda j: w_out_sb[:, j, :], IB),
                                "rt": (bank[0:E, 0:256], lambda j: w_router_T[:, j, :],
                                       lambda j: xhatT[:, j, k * 256:(k + 1) * 256], KD),
                            }[kind]
                            for j in range(n):
                                last = pe.matmul(dst, lhsT(j), rhs(j), start=(j == 0), stop=(j == n - 1))
                        last.then_inc(mm_full, 1)

                    body(chunk)(pe)

                @block.vector
                def _(dve):
                    dve.wait_ge(vec_ready, 2)
                    dve.wait_ge(carry_zeroed, 1)

                    def chunk(q, par, pair, units, post, pre):
                        a = q + 1
                        p = q - 1
                        nxt = 1 - par

                        def add_states(q, par, s):
                            if s == 0:
                                dve.wait_ge(y_started, q * TT + TT)
                            for t in range(TT):
                                dve.wait_ge(ht_ready, q * ((NS + 1) * TT) + ((s + 1) * TT + t + 1))
                                if s > 0:
                                    dve.wait_ge(y_added, q * (NS * TT) + ((s - 1) * TT + t + 1))
                                dve.scalar_tensor_tensor(out=y[:, t, :], in0=hT[t % 2][:],
                                                         scalar=c_tok[par][:, t, NS + s:NS + s + 1], in1=y[:, t, :],
                                                         op0=ALU.mult, op1=ALU.add).then_inc(y_added, 1)

                        for s in range(NS):
                            if units:
                                dve.wait_ge(db_ready, q * NS + (s + 1))
                                if s >= 2:
                                    dve.wait_ge(ht_ready, q * ((NS + 1) * TT) + s * TT)
                                else:
                                    wait(dve, ht_ready, q * ((NS + 1) * TT) - (2 - s - 1) * TT)
                                wait(dve, carry_kept, q * NS + (s - 1))
                                for i in range(IB):
                                    dve.wait_ge(da_ready, q * (NS * IB) + (s * IB + i + 1))
                                    dve.tensor_tensor_scan(h[s % 2][:, i, :], da[i][:], db[s % 2][:, i, :],
                                                           carry[:, par, s, i:i + 1], ALU.mult, ALU.add
                                                           ).then_inc(scan_done, 1)
                                if s > 0:
                                    add_states(q, par, s - 1)
                                dve.wait_ge(scan_done, q * (NS * IB) + (s + 1) * IB)
                                dve.tensor_copy(carry[:, par, s, :], h[s % 2][:, :, TC - 1]).then_inc(carry_kept, 1)
                            if pre and s == 0:
                                dve.wait_ge(x_loaded, (a + 1) * 16)
                                wait(dve, nw_in, a * 6)
                                for t in range(TT):
                                    dve.bn_stats(st_in[:, t, :], x_in[:, t, :]).then_inc(stats_in, 1)
                                wait(dve, xn_ready, a * TT)
                                dve.wait_ge(stats_in, a * TT + TT)
                                dve.sem_inc(wait_held, 1)
                                for t in range(TT):
                                    dve.bn_aggr(mv_in[:, t, :], st_in[:, t, :]).then_inc(aggr_in, 1)
                            if pre and s == 1:
                                dve.wait_ge(nw_in, (a + 1) * 6)
                                dve.wait_ge(aggr_in, a * TT + TT)
                                evacuated_before(dve, q, post, pre)
                                for t in range(TT):
                                    dve.tensor_scalar(xn[:, t, :], x_in[:, t, :], mv_in[:, t, 0:1], nt_in[:, 7, t:t + 1],
                                                      ALU.subtract, ALU.mult).then_inc(xn_ready, 1)
                            if pre and s in (4, 5):
                                tiles = (0, 1) if s == 4 else (2, 3)
                                for i in tiles:
                                    evacuated(dve, q, post, pre, f"xi{i}")
                                for k in range(TAPS - 1):
                                    for i in tiles:
                                        if k:
                                            dve.wait_ge(taps_added, a * ((TAPS - 1) * IB)
                                                        + ((s - 4) * 2 * (TAPS - 1) + 2 * k - 1 + i % 2))
                                        dve.scalar_tensor_tensor(out=conv[:, i, :], in0=xpad[nxt][:, i, k:k + TC],
                                                                 scalar=vecs[:, k * IB + i:k * IB + i + 1],
                                                                 in1=conv[:, i, :], op0=ALU.mult, op1=ALU.add
                                                                 ).then_inc(taps_added, 1)
                            if pre and s == 6:
                                dve.wait_ge(taps_added, (a + 1) * ((TAPS - 1) * IB))
                                dve.tensor_copy(xpad[nxt][:, :, 0:TAPS - 1], xpad[nxt][:, :, TC:TC + TAPS - 1]
                                                ).then_inc(tail_kept, 1)
                            if post and s == 8:
                                dve.wait_ge(xres_loaded, q * 16)
                                for t in range(TT):
                                    evacuated(dve, q, post, pre, f"out{t}")
                                dve.tensor_tensor(x1[:], xhat[:], x1[:], ALU.add).then_inc(x1_ready, 1)
                                dve.wait_ge(x1_ready, p + 1)
                                wait(dve, nw_mid, p * 7)
                                for t in range(TT):
                                    dve.bn_stats(st_mid[:, t, :], x1[:, t, :]).then_inc(stats_mid, 1)
                                wait(dve, xhat_ready, p * TT)
                                dve.wait_ge(stats_mid, p * TT + TT)
                                dve.sem_inc(wait_held, 1)
                                for t in range(TT):
                                    dve.bn_aggr(mv_mid[:, t, :], st_mid[:, t, :]).then_inc(aggr_mid, 1)
                            if post and s == 11:
                                dve.wait_ge(nw_mid, (p + 1) * 7)
                                dve.wait_ge(aggr_mid, p * TT + TT)
                                for t in range(TT):
                                    dve.tensor_scalar(xhat[:, t, :], x1[:, t, :], mv_mid[:, t, 0:1], nt_mid[:, 7, t:t + 1],
                                                      ALU.subtract, ALU.mult).then_inc(xhat_ready, 1)
                            if pre and s == 12:
                                for i in range(IB):
                                    evacuated(dve, q, post, pre, f"dt{i}")
                                dve.wait_ge(u_ready, a + 1)
                                dve.tensor_scalar(dt_min[:], dt_raw[nxt][:], SOFTPLUS_LINEAR, None, ALU.min
                                                  ).then_inc(dtmin_ready, 1)
                            if pre and s == 14:
                                dve.wait_ge(sp_ready, a * 2 + 2)
                                dve.tensor_tensor(dt[nxt][:], dt_min[:], dt_raw[nxt][:], ALU.max).then_inc(dt_ready, 1)
                        if units:
                            add_states(q, par, NS - 1)
                            dve.wait_ge(y_added, (q + 1) * (NS * TT))
                            dve.wait_ge(zg_ready, q + 1)
                            dve.tensor_tensor(yg[:], y[:], zg[par][:], ALU.mult).then_inc(y_gated, 1)

                    body(chunk)(dve)

        idx_all = sb("idx_all", [P, E * CH], I32)
        wt_all = sb("wt_all", [P, E * CH])
        with ExitStack() as part2:
            def sb2(name, shape, dt=F32):
                return part2.enter_context(nc.sbuf_tensor(name, shape, dt))

            NC = CHUNKS
            BIG = 8192.0
            BITS = 25
            HB = 16
            EH = P // HB
            GROUPS = E // EH

            same = sb2("same", [P, P])
            before = sb2("before", [P, P])
            own = sb2("own", [P, EH])
            iota_hb = sb2("iota_hb", [P, HB], I32)
            token = sb2("token", [P, TT, NC])
            lt = sb2("lt", [P, TC])
            work = sb2("work", [P, TC])
            zero = sb2("zero", [P, TC])
            r_own = sb2("r_own", [P, 1])
            r_all = sb2("r_all", [P, 1])
            lo = sb2("lo", [P, 1])
            mid = sb2("mid", [P, 1])
            taken = sb2("taken", [P, 1])
            step = [sb2(f"step{k}", [P, 1]) for k in range(2)]
            count = sb2("count", [P, 1])
            hi = sb2("hi", [P, 1])
            above = sb2("above", [P, TC])
            band = sb2("band", [P, TC])
            c_above = sb2("c_above", [P, TC])
            c_band = sb2("c_band", [P, TC])
            totals = sb2("totals", [P, 2])
            offs = sb2("offs", [P, 5])
            slot = sb2("slot", [P, TC])
            lg = sb2("lg", [P, TC])
            mask = sb2("mask", [P, TC])
            slot_i = sb2("slot_i", [P, TC], I32)
            slot_hi = sb2("slot_hi", [P, TC], I32)
            slot_lo = sb2("slot_lo", [P, TC], I32)
            ex = sb2("ex", [P, TC])
            wts = sb2("wts", [P, TC])
            best = sb2("best", [P, 4, TT * NC])
            hot_hi = [sb2(f"hot_hi{k}", [P, NC, E, HB]) for k in range(2)]
            hot_lo = [sb2(f"hot_lo{k}", [P, NC, E, HB]) for k in range(2)]
            values = [sb2(f"values{k}", [P, 2, NC, E, HB]) for k in range(2)]
            diag = [sb2(f"diag{k}", [P, 2, HB, EH]) for k in range(GROUPS)]
            listed = sb2("listed", [P, GROUPS, 2, HB])
            list_rows = sb2("list_rows", [2 * E * CH, P])

            route_ready = sem("route_ready")
            lt_loaded = sem("lt_loaded")
            r_ready = sem("r_ready")
            bis = sem("bis")
            counted = sem("counted")
            lg_turned = sem("lg_turned")
            ranked = sem("ranked")
            totalled = sem("totalled")
            slot_turned = sem("slot_turned")
            wt_step = sem("wt_step")
            wt_exp = sem("wt_exp")
            hot_ready = sem("hot_ready")
            tok_ready = sem("tok_ready")
            wv_ready = sem("wv_ready")
            scanned = sem("scanned")
            lists_kept = sem("lists_kept")
            lists_done = sem("lists_done")
            lists_read = sem("lists_read")
            lists_stored = sem("lists_stored")
            lists_loaded = sem("lists_loaded")
            lists_turned = sem("lists_turned")
            idx_ready = sem("idx_ready")

            with ExitStack() as banks:
                ps_count = banks.enter_context(nc.psum_tensor("ps_count", [P, TC], F32))
                ps_lg = banks.enter_context(nc.psum_tensor("ps_lg", [P, TC], F32))
                ps_slot = banks.enter_context(nc.psum_tensor("ps_slot", [P, TC], F32))
                ps_list = [banks.enter_context(nc.psum_tensor(f"ps_list{k}", [P, TC], F32)) for k in range(GROUPS)]
                ps_turn = banks.enter_context(nc.psum_tensor("ps_turn", [P, TC], F32))
                by_jec = ps_lg[:].rearrange("p (j e c) -> p j c e", e=E, c=NC)

                with nc.Block() as block:

                    @block.sync
                    def _(sp):
                        sp.dma_start(lt[:], logit_dram.rearrange("e (c t) -> (e c) t", t=TC)).then_inc(lt_loaded, 16)
                        sp.wait_ge(lists_read, GROUPS)
                        for v in range(2):
                            sp.dma_start(list_dram[v].rearrange("r (a b) -> (r a) b", b=HB).rearrange(
                                "(g p) b -> p g b", p=P), listed[:, :, v, :]).then_inc(lists_stored, 16)
                        sp.wait_ge(lists_stored, 32)
                        sp.dma_start(list_rows[:], list_dram.rearrange("v r s -> (v r) s")).then_inc(lists_loaded, 16)

                    @block.gpsimd
                    def _(pool):
                        pool.memset(same[:], 1.0).then_inc(route_ready, 1)
                        pool.memset(own[:], 1.0).then_inc(route_ready, 1)
                        pool.memset(zero[:], 0.0)
                        pool.memset(taken[:], 0.0)
                        pool.iota(iota_hb[:], pattern=[[1, HB]], base=0, channel_multiplier=0,
                                  )
                        pool.iota(token[:], pattern=[[P, TT], [TC, NC]], base=0, channel_multiplier=1,
                                  allow_small_or_imprecise_dtypes=True)
                        pool.wait_ge(route_ready, 2)
                        groups = same[:].rearrange("p (e c) -> p e c", c=NC)
                        pool.affine_select(out=groups, in_=groups, compare_op=ALU.is_ge, fill=0.0, base=0,
                                           pattern=[[-NC, E], [0, NC]], channel_multiplier=1).then_inc(route_ready, 1)
                        pool.affine_select(out=own[:], in_=own[:], compare_op=ALU.is_ge, fill=0.0, base=0,
                                           pattern=[[-HB, EH]], channel_multiplier=1).then_inc(route_ready, 1)
                        pool.wait_ge(route_ready, 4)
                        pool.affine_select(out=groups, in_=groups, compare_op=ALU.is_ge, fill=0.0, base=NC - 1,
                                           pattern=[[NC, E], [0, NC]], channel_multiplier=-1).then_inc(route_ready, 1)
                        pool.affine_select(out=own[:], in_=own[:], compare_op=ALU.is_ge, fill=0.0, base=HB - 1,
                                           pattern=[[HB, EH]], channel_multiplier=-1).then_inc(route_ready, 1)
                        pool.wait_ge(route_ready, 6)
                        pool.affine_select(out=before[:], in_=same[:], compare_op=ALU.is_ge, fill=0.0, base=-1,
                                           pattern=[[1, P]], channel_multiplier=-1).then_inc(route_ready, 1)
                        pool.wait_ge(r_ready, 1)
                        pool.partition_all_reduce(r_all[:], r_own[:], P, bass.bass_isa.ReduceOp.max).then_inc(r_ready, 1)
                        for j in range(TT):
                            if j >= 2:
                                pool.wait_ge(lists_done, j - 1)
                            pool.wait_ge(hot_ready, 2 * j + 2)
                            pool.tensor_tensor(values[j % 2][:, 0, :, :, :].rearrange("p c e b -> p c (e b)"),
                                               hot_lo[j % 2][:].rearrange("p c e b -> p c (e b)"),
                                               token[:, j, :].unsqueeze(2).broadcast_to([P, NC, E * HB]),
                                               ALU.mult).then_inc(tok_ready, 1)

                    @block.scalar
                    def _(act):
                        act.wait_ge(wt_step, 7)
                        act.activation(ex[:], ex[:], ACT.Exp).then_inc(wt_exp, 1)
                        act.activation(best[:, 2, :], best[:, 2, :], ACT.Exp).then_inc(wt_exp, 1)

                    @block.tensor
                    def _(pe):
                        pe.wait_ge(lt_loaded, 16)
                        for j in range(TT):
                            last = pe.transpose(ps_lg[:, j * P:(j + 1) * P], lt[:, j * P:(j + 1) * P], ident[:])
                        last.then_inc(lg_turned, 1)
                        pe.wait_ge(route_ready, 7)

                        def count_experts(it, k):
                            pe.wait_ge(bis, it * 10 + (5 * k + 1))
                            pe.matmul(ps_count[:, 0:1], same[:], count[:], start=True, stop=True
                                      ).then_inc(counted, 1)

                        with pe.Fori(0, BITS // 2) as it:
                            count_experts(it, 0)
                            count_experts(it, 1)
                        count_experts(BITS // 2, 0)
                        pe.wait_ge(ranked, 6)
                        pe.matmul(ps_count[:, 2:4], before[:], totals[:], start=True, stop=True)
                        pe.matmul(ps_count[:, 4:5], same[:], totals[:, 0:1], start=True, stop=True).then_inc(totalled, 1)
                        pe.wait_ge(ranked, 12)
                        for j in range(TT):
                            last = pe.transpose(ps_slot[:, j * P:(j + 1) * P], slot[:, j * P:(j + 1) * P], ident[:])
                        last.then_inc(slot_turned, 1)
                        for j in range(TT):
                            pe.wait_ge(hot_ready, 2 * j + 2)
                            pe.wait_ge(tok_ready, j + 1)
                            pe.wait_ge(wv_ready, j + 1)
                            for c in range(NC):
                                for g in range(GROUPS):
                                    e = slice(g * EH, (g + 1) * EH)
                                    last = pe.matmul(
                                        ps_list[g][:, 0:2 * EH * HB],
                                        hot_hi[j % 2][:, c, e, :].rearrange("p e a -> p (e a)"),
                                        values[j % 2][:, :, c, e, :].rearrange("p v e b -> p v (e b)"),
                                        start=(j == 0 and c == 0), stop=(j == TT - 1 and c == NC - 1))
                            last.then_inc(lists_done, 1)
                        pe.wait_ge(lists_loaded, 16)
                        pe.transpose(ps_turn[:, 0:2 * E * CH], list_rows[:], ident[0:2 * E * CH, 0:2 * E * CH]
                                     ).then_inc(lists_turned, 1)

                    @block.vector
                    def _(dve):
                        dve.wait_ge(lt_loaded, 16)
                        dve.tensor_reduce(r_own[:], lt[:], AX.X, ALU.max, apply_absolute_value=True).then_inc(r_ready, 1)
                        dve.wait_ge(r_ready, 2)
                        dve.tensor_scalar(r_own[:].bitcast(I32), r_all[:].bitcast(I32), 0x7F800000, None,
                                          ALU.bitwise_and).then_inc(r_ready, 1)
                        dve.wait_ge(r_ready, 3)
                        dve.tensor_scalar(step[0][:], r_own[:], 2.0, None, ALU.mult).then_inc(r_ready, 1)
                        dve.tensor_scalar(lo[:], r_own[:], -2.0, None, ALU.mult).then_inc(r_ready, 1)
                        dve.wait_ge(route_ready, 7)
                        dve.memset(mid[:], 0.0).then_inc(r_ready, 1)
                        dve.wait_ge(r_ready, 6)

                        def halve(it, k):
                            dve.tensor_scalar(work[:], lt[:], mid[:, 0:1], 0.0, ALU.is_ge, ALU.add,
                                              accum_out=count[:]).then_inc(bis, 1)
                            dve.tensor_tensor(lo[:], lo[:], taken[:], ALU.add).then_inc(bis, 1)
                            dve.tensor_scalar(step[1 - k][:], step[k][:], 0.5, None, ALU.mult).then_inc(bis, 1)
                            dve.wait_ge(bis, it * 10 + (5 * k + 3))
                            dve.wait_ge(counted, it * 2 + (k + 1))
                            dve.tensor_scalar(taken[:], ps_count[:, 0:1], float(CAP), step[k][:, 0:1],
                                              ALU.is_ge, ALU.mult).then_inc(bis, 1)
                            dve.wait_ge(bis, it * 10 + (5 * k + 4))
                            dve.scalar_tensor_tensor(out=mid[:], in0=taken[:], scalar=step[1 - k][:, 0:1],
                                                     in1=lo[:], op0=ALU.add, op1=ALU.add).then_inc(bis, 1)
                            dve.wait_ge(bis, it * 10 + (5 * k + 5))

                        with dve.Fori(0, BITS // 2) as it:
                            halve(it, 0)
                            halve(it, 1)
                        halve(BITS // 2, 0)
                        dve.tensor_tensor(lo[:], lo[:], taken[:], ALU.add).then_inc(ranked, 1)
                        dve.wait_ge(ranked, 1)
                        dve.tensor_tensor(hi[:], lo[:], step[0][:], ALU.add).then_inc(ranked, 1)
                        dve.wait_ge(ranked, 2)
                        dve.tensor_scalar(above[:], lt[:], hi[:, 0:1], None, ALU.is_ge).then_inc(ranked, 1)
                        dve.wait_ge(ranked, 3)
                        dve.scalar_tensor_tensor(out=band[:], in0=lt[:], scalar=lo[:, 0:1], in1=above[:],
                                                 op0=ALU.is_ge, op1=ALU.subtract).then_inc(ranked, 1)
                        dve.tensor_tensor_scan(c_above[:], above[:], zero[:], 0.0, ALU.add, ALU.add).then_inc(scanned, 1)
                        dve.wait_ge(ranked, 4)
                        dve.tensor_tensor_scan(c_band[:], band[:], zero[:], 0.0, ALU.add, ALU.add).then_inc(scanned, 1)
                        dve.wait_ge(scanned, 2)
                        dve.tensor_copy(totals[:, 0:1], c_above[:, TC - 1:TC]).then_inc(ranked, 1)
                        dve.tensor_copy(totals[:, 1:2], c_band[:, TC - 1:TC]).then_inc(ranked, 1)
                        dve.wait_ge(totalled, 1)
                        dve.tensor_copy(offs[:, 0:3], ps_count[:, 2:5]).then_inc(ranked, 1)
                        dve.wait_ge(ranked, 7)
                        dve.tensor_scalar(offs[:, 3:4], offs[:, 1:2], offs[:, 2:3], -1.0 - BIG, ALU.add, ALU.add
                                          ).then_inc(ranked, 1)
                        dve.tensor_scalar(offs[:, 4:5], offs[:, 0:1], -1.0 - BIG, None, ALU.add).then_inc(ranked, 1)
                        dve.wait_ge(ranked, 9)
                        dve.scalar_tensor_tensor(out=c_above[:], in0=c_above[:], scalar=offs[:, 4:5], in1=above[:],
                                                 op0=ALU.add, op1=ALU.mult).then_inc(ranked, 1)
                        dve.scalar_tensor_tensor(out=c_band[:], in0=c_band[:], scalar=offs[:, 3:4], in1=band[:],
                                                 op0=ALU.add, op1=ALU.mult).then_inc(ranked, 1)
                        dve.wait_ge(ranked, 11)
                        dve.scalar_tensor_tensor(out=slot[:], in0=c_above[:], scalar=BIG, in1=c_band[:],
                                                 op0=ALU.add, op1=ALU.add).then_inc(ranked, 1)
                        dve.wait_ge(slot_turned, 1)
                        dve.tensor_copy(slot_i[:], ps_slot[:]).then_inc(ranked, 1)
                        dve.tensor_scalar(mask[:], ps_slot[:], float(CAP), None, ALU.is_lt).then_inc(ranked, 1)
                        dve.wait_ge(ranked, 13)
                        dve.tensor_scalar(slot_hi[:], slot_i[:], 4, None, ALU.arith_shift_right).then_inc(ranked, 1)
                        dve.tensor_scalar(slot_lo[:], slot_i[:], HB - 1, None, ALU.bitwise_and).then_inc(ranked, 1)

                        def jec(tile):
                            return tile[:].rearrange("p (j e c) -> p j e c", e=E, c=NC)

                        def over_e(k):
                            return best[:, k, :].rearrange("p (j c) -> p j c", c=NC).unsqueeze(2).broadcast_to(
                                [P, TT, E, NC])

                        def row(k):
                            return best[:, k, :].rearrange("p (j c) -> p j c", c=NC)

                        dve.wait_ge(lg_turned, 1)
                        dve.tensor_reduce(row(0), by_jec, AX.X, ALU.max).then_inc(wt_step, 1)
                        dve.wait_ge(ranked, 14)
                        dve.tensor_scalar(work[:], mask[:], -1.0, 1e30, ALU.add, ALU.mult).then_inc(wt_step, 1)
                        dve.tensor_tensor(lg[:], ps_lg[:], mask[:], ALU.mult).then_inc(wt_step, 1)
                        dve.wait_ge(wt_step, 3)
                        dve.tensor_tensor(lg[:], lg[:], work[:], ALU.add).then_inc(wt_step, 1)
                        dve.wait_ge(wt_step, 4)
                        dve.tensor_reduce(row(1), lg[:].rearrange("p (j e c) -> p j c e", e=E, c=NC), AX.X, ALU.max
                                          ).then_inc(wt_step, 1)
                        dve.wait_ge(wt_step, 5)
                        dve.tensor_tensor(best[:, 2, :], best[:, 1, :], best[:, 0, :], ALU.subtract).then_inc(wt_step, 1)
                        dve.tensor_tensor(jec(ex), jec(lg), over_e(1), ALU.subtract).then_inc(wt_step, 1)

                        def hot(j):
                            if j >= 2:
                                dve.wait_ge(lists_done, j - 1)
                            for dst, part in ((hot_hi, slot_hi), (hot_lo, slot_lo)):
                                dve.tensor_tensor(
                                    dst[j % 2][:],
                                    part[:, j * P:(j + 1) * P].rearrange("p (e c) -> p c e", c=NC).unsqueeze(3
                                                                         ).broadcast_to([P, NC, E, HB]),
                                    iota_hb[:].unsqueeze(1).unsqueeze(1).broadcast_to([P, NC, E, HB]),
                                    ALU.is_equal).then_inc(hot_ready, 1)

                        def weights_by_low(j):
                            dve.wait_ge(hot_ready, 2 * j + 2)
                            dve.tensor_tensor(
                                values[j % 2][:, 1], hot_lo[j % 2][:],
                                wts[:, j * P:(j + 1) * P].rearrange("p (e c) -> p c e", c=NC).unsqueeze(3
                                                                    ).broadcast_to([P, NC, E, HB]),
                                ALU.mult).then_inc(wv_ready, 1)

                        dve.wait_ge(ranked, 16)
                        hot(0)
                        dve.wait_ge(wt_exp, 2)
                        dve.tensor_tensor(ex[:], ex[:], mask[:], ALU.mult).then_inc(wt_step, 1)
                        dve.wait_ge(wt_step, 8)
                        dve.tensor_reduce(row(3), ex[:].rearrange("p (j e c) -> p j c e", e=E, c=NC), AX.X, ALU.add
                                          ).then_inc(wt_step, 1)
                        dve.wait_ge(wt_step, 9)
                        dve.scalar_tensor_tensor(out=best[:, 3, :], in0=best[:, 3, :], scalar=0.0, in1=best[:, 3, :],
                                                 op0=ALU.is_le, op1=ALU.add).then_inc(wt_step, 1)
                        dve.wait_ge(wt_step, 10)
                        dve.reciprocal(best[:, 3, :], best[:, 3, :]).then_inc(wt_step, 1)
                        dve.wait_ge(wt_step, 11)
                        dve.scalar_tensor_tensor(out=best[:, 3, :], in0=best[:, 2, :], scalar=0.0, in1=best[:, 3, :],
                                                 op0=ALU.is_gt, op1=ALU.mult).then_inc(wt_step, 1)
                        dve.wait_ge(wt_step, 12)
                        dve.tensor_tensor(jec(wts), jec(ex), over_e(3), ALU.mult).then_inc(wt_step, 1)
                        dve.wait_ge(wt_step, 13)
                        weights_by_low(0)
                        for j in range(1, TT):
                            hot(j)
                            weights_by_low(j)
                        dve.wait_ge(lists_done, TT)
                        for g in range(GROUPS):
                            dve.tensor_tensor(diag[g][:],
                                              ps_list[g][:, 0:2 * EH * HB].rearrange("p (v e b) -> p v b e", e=EH, b=HB),
                                              own[:].unsqueeze(1).unsqueeze(1).broadcast_to([P, 2, HB, EH]),
                                              ALU.mult).then_inc(lists_kept, 1)
                        for g in range(GROUPS):
                            dve.wait_ge(lists_kept, g + 1)
                            dve.tensor_reduce(listed[:, g], diag[g][:], AX.X, ALU.add).then_inc(lists_read, 1)
                        dve.wait_ge(lists_turned, 1)
                        dve.tensor_copy(idx_all[:], ps_turn[:, 0:E * CH]).then_inc(idx_ready, 1)
                        dve.tensor_copy(wt_all[:], ps_turn[:, E * CH:2 * E * CH]).then_inc(idx_ready, 1)

        with ExitStack() as part3:
            def sb3(name, shape, dt=F32):
                return part3.enter_context(nc.sbuf_tensor(name, shape, dt))

            def psum3(name):
                return part3.enter_context(nc.psum_tensor(name, [P, 512], F32))

            w1 = [sb3(f"w1_{k}", [P, KF, D]) for k in range(2)]
            w2 = [sb3(f"w2_{k}", [P, KD, F]) for k in range(2)]
            w1T = sb3("w1T", [P, KD, F])
            w2T = [sb3(f"w2T_{k}", [P, KF, D]) for k in range(2)]
            b2_all = sb3("b2_all", [P, E, D])
            xe = [[sb3(f"xe{k}_{half}", [P, D]) for half in range(CH)] for k in range(2)]
            xeT = sb3("xeT", [P, KD, CAP])
            hid = sb3("hid", [P, KF, CAP])
            ye = [sb3(f"ye{half}", [P, D]) for half in range(CH)]
            gather_idx = [sb3(f"gather_idx{k}", [P, CH], I32) for k in range(2)]
            scatter_idx = sb3("scatter_idx", [P, CH], I32)
            wt_e = sb3("wt_e", [P, CH])
            b1_e = [sb3(f"b1_e{k}", [P, KF]) for k in range(2)]

            hb = [psum3(f"hb{k}") for k in range(KF // 2)]
            yb = psum3("yb")
            TURNS = 3
            turn = [psum3(f"turn{k}") for k in range(TURNS)]
            USES = [("x", 0)] + [("w1", k) for k in range(4)] + [("w2", k) for k in range(4)]
            NU = len(USES)
            assert NU % TURNS == 0

            b2_loaded = sem("b2_loaded")
            w_loaded = [sem(f"w_loaded{k}") for k in range(2)]
            xe_loaded = [sem(f"xe_loaded{k}") for k in range(2)]
            gidx_ready = sem("gidx_ready")
            b1_ready = sem("b1_ready")
            turn_full = sem("turn_full")
            turn_free = [sem(f"turn_free{k}") for k in range(TURNS)]
            h_full = sem("h_full")
            gelu_done = sem("gelu_done")
            y_full = sem("y_full")
            y_cols = sem("y_cols")
            y_biased = sem("y_biased")
            y_ready = sem("y_ready")
            scattered = sem("scattered")

            w_fc1_rows = w_fc1.rearrange("e (f p) d -> e p f d", p=P)
            w_fc2_rows = w_fc2.rearrange("e (k p) f -> e p k f", p=P)

            def span(e, n):
                return slice(e * n, (e + 1) * n) if isinstance(e, int) else bass.ds(e * n, n)

            def experts(first, expert):
                with_next = dict(turn_next=True, fetch_next=True)

                def run(eng):
                    first()
                    with eng.Fori(0, (E - 2) // 2) as pair:
                        expert(pair * 2, 0, pair, **with_next)
                        expert(pair * 2 + 1, 1, pair, **with_next)
                    expert(E - 2, 0, E // 2 - 1, turn_next=True, fetch_next=False)
                    expert(E - 1, 1, E // 2 - 1, turn_next=False, fetch_next=False)
                return run

            with nc.Block() as block:

                @block.sync
                def _(sp):
                    def load(e, par):
                        sp.dma_start(w1[par][:], w_fc1_rows[e]).then_inc(w_loaded[par], 16)
                        sp.dma_start(w2[par][:], w_fc2_rows[e]).then_inc(w_loaded[par], 16)

                    def first():
                        load(0, 0)
                        load(1, 1)
                        sp.dma_start(b2_all[:], b_fc2.rearrange("(a e) d -> a e d", a=1).partition_broadcast(P)
                                     ).then_inc(b2_loaded, 16)

                    def expert(e, par, pair, turn_next, fetch_next):
                        if fetch_next:
                            sp.wait_ge(turn_full, (e + 1) * NU)
                            sp.sem_inc(wait_held, 1)
                            load(e + 2, par)

                    experts(first, expert)(sp)
                    sp.wait_ge(b2_loaded, 16)
                    sp.wait_ge(scattered, E * CH * 16)

                @block.gpsimd
                def _(pool):
                    def gather(e, par):
                        pool.wait_ge(gidx_ready, e + 1)
                        if not isinstance(e, int):
                            pool.sem_inc(wait_held, 1)
                        for half in range(CH):
                            pool.indirect_dma_start(
                                out=xe[par][half][:], out_offset=None, in_=xhat_dram,
                                in_offset=bass.IndirectOffsetOnAxis(ap=gather_idx[par][:, half:half + 1], axis=0)
                            ).then_inc(xe_loaded[par], 16)

                    def first():
                        gather(0, 0)
                        gather(1, 1)

                    def expert(e, par, pair, turn_next, fetch_next):
                        if fetch_next:
                            pool.wait_ge(turn_full, e * NU + 1)
                            gather(e + 2, par)
                        pool.wait_ge(y_ready, e * CH + CH)
                        pool.wait_ge(scattered, e * (CH * 16))
                        pool.sem_inc(wait_held, 1)
                        for half in range(CH):
                            pool.indirect_dma_start(
                                out=out_flat, out_offset=bass.IndirectOffsetOnAxis(
                                    ap=scatter_idx[:, half:half + 1], axis=0),
                                in_=ye[half][:], in_offset=None, compute_op=ALU.add
                            ).then_inc(scattered, 16)

                    experts(first, expert)(pool)

                def turned(eng, on_act, e, par):
                    for n, (kind, k) in enumerate(USES):
                        if (n % 2 == 1) != on_act:
                            continue
                        eng.wait_ge(turn_full, e * NU + (n + 1))
                        bank = turn[n % TURNS]
                        if kind == "x":
                            done = eng.tensor_copy(xeT[:].rearrange("p k s -> p (k s)"), bank[:])
                        elif kind == "w1":
                            dst, scale = w1T[:, k // 2, k % 2 * 512:(k % 2 + 1) * 512], vecs[:, NW + k // 2:NW + k // 2 + 1]
                            if on_act:
                                done = eng.activation(dst, bank[:], ACT.Copy, scale=scale)
                            else:
                                done = eng.tensor_scalar(dst, bank[:], scale, None, ALU.mult)
                        else:
                            dst = w2T[par][:, 2 * k:2 * k + 2, :].rearrange("p f d -> p (f d)")
                            done = eng.copy(dst, bank[:]) if on_act else eng.tensor_copy(dst, bank[:])
                        done.then_inc(turn_free[n % TURNS], 1)

                @block.scalar
                def _(act):
                    act.preload_act_table_set("gelu_and_others")

                    def first():
                        turned(act, True, 0, 0)

                    def expert(e, par, pair, turn_next, fetch_next):
                        act.wait_ge(b1_ready, e + 1)
                        for f in range(KF):
                            act.wait_ge(h_full, e * (KF // 2) + (f // 2 + 1))
                            act.activation(hid[:, f, :], hb[f // 2][:, f % 2 * CAP:(f % 2 + 1) * CAP], ACT.Gelu,
                                           bias=b1_e[par][:, f:f + 1]).then_inc(gelu_done, 1)
                        if turn_next:
                            turned(act, True, e + 1, 1 - par)

                    experts(first, expert)(act)

                @block.tensor
                def _(pe):
                    def turns(e, par, loads):
                        for n, (kind, k) in enumerate(USES):
                            if kind == "x":
                                pe.wait_ge(xe_loaded[par], loads * (CH * 16))
                            if kind == "w1" and k == 0:
                                pe.wait_ge(w_loaded[par], loads * 32)
                            bank = turn[n % TURNS]
                            before = e * (NU // TURNS) + n // TURNS
                            if not isinstance(before, int) or before > 0:
                                pe.wait_ge(turn_free[n % TURNS], before)
                            pe.sem_inc(wait_held, 1)
                            for i in range(4):
                                if kind == "x":
                                    src = xe[par][i % 2][:, i // 2 * P:(i // 2 + 1) * P]
                                elif kind == "w1":
                                    src = w1[par][:, k % 2 * 4 + i, k // 2 * P:(k // 2 + 1) * P]
                                else:
                                    f = 2 * k + i // 2
                                    src = w2[par][:, i % 2, f * P:(f + 1) * P]
                                last = pe.transpose(bank[:, i * P:(i + 1) * P], src, ident[:])
                            last.then_inc(turn_full, 1)

                    def first():
                        turns(0, 0, 1)

                    def expert(e, par, pair, turn_next, fetch_next):
                        for k in range(TURNS):
                            pe.wait_ge(turn_free[k], (e + 1) * (NU // TURNS))
                        for f in range(KF):
                            for k in range(KD):
                                last = pe.matmul(hb[f // 2][:, f % 2 * CAP:(f % 2 + 1) * CAP],
                                                 w1T[:, k, f * P:(f + 1) * P], xeT[:, k, :],
                                                 start=(k == 0), stop=(k == KD - 1))
                            if f % 2:
                                last.then_inc(h_full, 1)
                        if turn_next:
                            turns(e + 1, 1 - par, pair + 1 + par)
                        pe.wait_ge(gelu_done, (e + 1) * KF)
                        pe.wait_ge(y_biased, e * CH)
                        for half in range(CH):
                            for f in range(KF):
                                last = pe.matmul(yb[:, half * D:(half + 1) * D], hid[:, f, half * P:(half + 1) * P],
                                                 w2T[par][:, f, :], start=(f == 0), stop=(f == KF - 1))
                        last.then_inc(y_full, 1)

                    experts(first, expert)(pe)

                @block.vector
                def _(dve):
                    def columns(e, par):
                        dve.tensor_copy(gather_idx[par][:], idx_all[:, span(e, CH)]).then_inc(gidx_ready, 1)

                    def biases(e, par):
                        dve.tensor_copy(b1_e[par][:], b1_cols[:, span(e, KF)]).then_inc(b1_ready, 1)

                    def first():
                        columns(0, 0)
                        columns(1, 1)
                        biases(0, 0)
                        turned(dve, False, 0, 0)
                        dve.wait_ge(b2_loaded, 16)

                    def expert(e, par, pair, turn_next, fetch_next):
                        if fetch_next:
                            dve.wait_ge(turn_full, e * NU + 1)
                            dve.sem_inc(wait_held, 1)
                            columns(e + 2, par)
                        if turn_next:
                            dve.wait_ge(gelu_done, e * KF)
                            dve.sem_inc(wait_held, 1)
                            biases(e + 1, 1 - par)
                            turned(dve, False, e + 1, 1 - par)
                        dve.wait_ge(scattered, e * (CH * 16))
                        dve.sem_inc(wait_held, 1)
                        dve.tensor_copy(scatter_idx[:], idx_all[:, span(e, CH)]).then_inc(y_cols, 1)
                        dve.wait_ge(y_ready, e * CH)
                        dve.sem_inc(wait_held, 1)
                        dve.tensor_copy(wt_e[:], wt_all[:, span(e, CH)]).then_inc(y_cols, 1)
                        dve.wait_ge(y_full, e + 1)
                        for half in range(CH):
                            dve.tensor_tensor(ye[half][:], yb[:, half * D:(half + 1) * D], b2_all[:, e, :], ALU.add
                                              ).then_inc(y_biased, 1)
                        dve.wait_ge(y_cols, e * 2 + 2)
                        for half in range(CH):
                            dve.wait_ge(y_biased, e * CH + (half + 1))
                            last = dve.tensor_scalar(ye[half][:], ye[half][:], wt_e[:, half:half + 1], None, ALU.mult)
                            last.then_inc(y_ready, 1)

                    experts(first, expert)(dve)


_INS = ['L0_attn_inputs', 'L0_attn_W_in', 'L0_attn_conv_w', 'L0_attn_conv_b', 'L0_attn_W_x', 'L0_attn_W_dt',
        'L0_attn_b_dt', 'L0_attn_A_log', 'L0_attn_W_out', 'L0_ffn_norm_weight', 'L0_ffn_router_weight',
        'L0_ffn_router_bias', 'L0_ffn_fc1_weight', 'L0_ffn_fc1_bias', 'L0_ffn_fc2_weight', 'L0_ffn_fc2_bias']
_OUTS = [((2, 2048, 256), 'float32')]


def kernel(**inputs):
    import numpy as _np
    import concourse.bacc as _bacc
    from concourse import mybir as _mybir
    from concourse.bass_utils import run_bass_kernel_spmd as _run

    nc = _bacc.Bacc("TRN2", target_bir_lowering=False, num_devices=1)
    arrays, args = {}, []
    for name in _INS:
        a = _np.ascontiguousarray(inputs[name])
        arrays[f"in_{name}_dram"] = a
        args.append(nc.dram_tensor(f"in_{name}_dram", a.shape, _mybir.dt.from_np(a.dtype), kind="ExternalInput").ap())
    for i, (shape, dtype) in enumerate(_OUTS):
        dt = _mybir.dt.from_np(_np.dtype(dtype))
        args.append(nc.dram_tensor(f"out_{i}_dram", shape, dt, kind="ExternalOutput").ap())
    mixer_moe(nc, *args)
    r = _run(nc, [arrays], core_ids=[0])
    return r.results[0]["out_0_dram"]
```

```python
from contextlib import ExitStack

import concourse.bass as bass
from concourse import mybir

ALU = mybir.AluOpType
ACT = mybir.ActivationFunctionType
AX = mybir.AxisListType
F32 = mybir.dt.float32
BF16 = mybir.dt.bfloat16
I32 = mybir.dt.int32

P = 128
EPS = 1e-5
LOG_SET = "natural_log_exp_and_others"
SILU_SET = "silu_and_others"
SOFTPLUS_LINEAR = 40.0


def mixer_moe(nc, x, w_in, conv_w, conv_b, w_x, w_dt, b_dt, a_log, w_out,
              norm_w, w_router, b_router, w_fc1, b_fc1, w_fc2, b_fc2, out):
    BATCH, SEQ, D = x.shape
    DI = w_dt.shape[1]
    NS = a_log.shape[1]
    TAPS = conv_w.shape[0]
    E, F, _ = w_fc1.shape
    N = BATCH * SEQ
    TC = 512
    TT = TC // P
    KD = D // P
    IB = DI // P
    KF = F // P
    CAP = N // E
    CH = CAP // P
    CHUNKS = N // TC
    TILES = N // P
    assert BATCH == 2 and TC == 512 and NS == 16 and E == 16 and CHUNKS == 8 and CAP == 256

    x_rows = x.rearrange("b (c t p) d -> (b c) p t d", t=TT, p=P)
    out_rows = out.rearrange("b (c t p) d -> (b c) p t d", t=TT, p=P)
    out_flat = out.rearrange("b s d -> (b s) d")

    b_scratch = nc.dram_tensor("b_scratch", [2, NS, TC], F32, kind="Internal").ap()
    xhat_dram = nc.dram_tensor("xhat_dram", [N, D], F32, kind="Internal").ap()
    xhat_rows = xhat_dram.rearrange("(c t p) d -> c p t d", t=TT, p=P)
    logit_dram = nc.dram_tensor("logit_dram", [E, N], F32, kind="Internal").ap()
    logit_chunks = logit_dram.rearrange("e (c t) -> c e t", t=TC)
    list_dram = nc.dram_tensor("list_dram", [2, E * CH, P], F32, kind="Internal").ap()

    with ExitStack() as ctx:
        def sb(name, shape, dt=F32):
            return ctx.enter_context(nc.sbuf_tensor(name, shape, dt))

        def psum(name, shape, dt=F32):
            return ctx.enter_context(nc.psum_tensor(name, shape, dt))

        def sem(name):
            return ctx.enter_context(nc.semaphore(name))

        ident = sb("ident", [P, P])
        ones = sb("ones", [P, P])
        NVEC = TAPS * IB + IB + IB + KD
        CONVB, BDT, NW = TAPS * IB, TAPS * IB + IB, TAPS * IB + 2 * IB
        vec_rows = sb("vec_rows", [32, P])
        vecs = sb("vecs", [P, 32])
        b1_rows = sb("b1_rows", [P, P])
        b1_cols = sb("b1_cols", [P, E * KF])
        b_router_sb = sb("b_router_sb", [E, 1])
        w_router_rows = sb("w_router_rows", [E, D])
        w_router_T = sb("w_router_T", [P, KD, E])

        consts_loaded = sem("consts_loaded")
        w_in_loaded = sem("w_in_loaded")
        weights_loaded = sem("weights_loaded")
        ident_ready = sem("ident_ready")
        vec_turned = sem("vec_turned")
        vec_ready = sem("vec_ready")
        a_ready = sem("a_ready")
        carry_zeroed = sem("carry_zeroed")
        wait_held = sem("wait_held")

        x_loaded = sem("x_loaded")
        xres_loaded = sem("xres_loaded")
        stats_in = sem("stats_in")
        aggr_in = sem("aggr_in")
        rs_in = sem("rs_in")
        nw_in = sem("nw_in")
        xn_ready = sem("xn_ready")
        taps_added = sem("taps_added")
        tail_kept = sem("tail_kept")
        u_ready = sem("u_ready")
        zg_ready = sem("zg_ready")
        b_stored = sem("b_stored")
        sp_ready = sem("sp_ready")
        dt_ready = sem("dt_ready")
        du_ready = sem("du_ready")
        mm_full = sem("mm_full")
        mm_free = [sem("mm_free0"), sem("mm_free1")]

        NBB = 4
        bb_loaded = [sem(f"bb_loaded{k}") for k in range(NBB)]
        da_ready = sem("da_ready")
        db_ready = sem("db_ready")
        scan_done = sem("scan_done")
        carry_kept = sem("carry_kept")
        ht_ready = sem("ht_ready")
        y_started = sem("y_started")
        y_added = sem("y_added")
        y_gated = sem("y_gated")
        x1_ready = sem("x1_ready")
        stats_mid = sem("stats_mid")
        aggr_mid = sem("aggr_mid")
        rs_mid = sem("rs_mid")
        nw_mid = sem("nw_mid")
        shift_ready = sem("shift_ready")
        xhat_ready = sem("xhat_ready")
        x1_stored = sem("x1_stored")
        xhat_stored = sem("xhat_stored")
        logit_stored = sem("logit_stored")

        SLOTS = [["yT0", "yT1", "yT2", "yT3"], ["xnT0", "xnT1"], ["xi0", "xi1"], ["xi2", "xi3"],
                 ["out0", "out1"], ["out2", "out3"], ["dti0"], ["dti1"], ["dt0", "dt1"], ["dt2", "dt3"],
                 ["bc"], ["ct", "z0", "z1"], ["xhT0", "xhT1", "z2"], ["z3", "rt0"], ["rt1"], []]
        OF_POST = ("yT", "out", "xhT", "rt")
        BOTH = [name for slot in SLOTS for name in slot]
        POST = [name for name in BOTH if name.startswith(OF_POST)]
        PRE = [name for name in BOTH if not name.startswith(OF_POST)]
        NPOST, NPRE = len(POST), len(PRE)
        assert NPOST % 2 == 0 and NPRE % 2 == 0

        def uses(s, post, pre):
            return [name for name in SLOTS[s] if (post if name.startswith(OF_POST) else pre)]

        def mm_number(q, post, pre, name):
            order = BOTH if post and pre else POST if post else PRE
            if isinstance(q, int) and q < 1:
                base = NPRE * (q + 1)
            elif isinstance(q, int):
                base = NPRE * min(q + 1, CHUNKS) + NPOST * (q - 1)
            else:
                base = q * (NPRE + NPOST) + (NPRE - NPOST)
            return base, order.index(name)

        def wait(eng, semaphore, value):
            if not isinstance(value, int) or value > 0:
                eng.wait_ge(semaphore, value)

        def banks_before(q, post, pre, name):
            base, k = mm_number(q, post, pre, name)
            bank = k % 2
            if isinstance(base, int):
                return bank, base // 2 + k // 2
            return bank, q * ((NPRE + NPOST) // 2) + ((NPRE - NPOST) // 2 + k // 2)

        def mm_take(q, post, pre, name):
            bank, before = banks_before(q, post, pre, name)
            wait(nc.tensor, mm_free[bank], before)
            return mm[bank]

        def mm_wait(eng, q, post, pre, name):
            base, k = mm_number(q, post, pre, name)
            bank = k % 2
            eng.wait_ge(mm_full, base + (k + 1))
            return mm[bank], mm_free[bank]

        def evacuated(eng, q, post, pre, name):
            bank, before = banks_before(q, post, pre, name)
            eng.wait_ge(mm_free[bank], before + 1)

        def evacuated_before(eng, q, post, pre):
            order = BOTH if post and pre else POST if post else PRE
            for name in order[0:2]:
                bank, before = banks_before(q, post, pre, name)
                wait(eng, mm_free[bank], before)

        def body(chunk):
            def run(eng):
                chunk(-1, 1, 0, units=False, post=False, pre=True)
                chunk(0, 0, 0, units=True, post=False, pre=True)
                with eng.Fori(0, (CHUNKS - 2) // 2) as pair:
                    chunk(pair * 2 + 1, 1, pair, units=True, post=True, pre=True)
                    chunk(pair * 2 + 2, 0, pair, units=True, post=True, pre=True)
                chunk(CHUNKS - 1, 1, CHUNKS // 2 - 1, units=True, post=True, pre=False)
                chunk(CHUNKS, 0, CHUNKS // 2, units=False, post=True, pre=False)
            return run

        def neighbours(q, par, pair):
            if isinstance(q, int):
                return (1 - par) * (CHUNKS // 2) + (q - 1) // 2, (1 - par) * (CHUNKS // 2) + (q + 1) // 2
            if par == 1:
                return pair, pair + 1
            return pair + CHUNKS // 2, pair + (CHUNKS // 2 + 1)

        with ExitStack() as part1:
            def sb1(name, shape, dt=F32):
                return part1.enter_context(nc.sbuf_tensor(name, shape, dt))

            w_in_sb = sb1("w_in_sb", [P, KD, 2 * DI])
            w_x_sb = sb1("w_x_sb", [P, IB, D + 2 * NS])
            w_dt_sb = sb1("w_dt_sb", [P, KD, DI])
            w_out_sb = sb1("w_out_sb", [P, IB, D])
            a_raw = sb1("a_raw", [P, IB, NS])
            a_exp = sb1("a_exp", [P, IB, NS])
            a_sb = sb1("a_sb", [P, IB, NS])

            x_in = sb1("x_in", [P, TT, D])
            st_in = sb1("st_in", [P, TT, 6])
            mv_in = sb1("mv_in", [P, TT, 2])
            nt_in = sb1("nt_in", [P, 7, TT])
            xn = sb1("xn", [P, TT, D])
            xnT = sb1("xnT", [P, KD, TC])
            xpad = [sb1(f"xpad{k}", [P, IB, TAPS - 1 + TC]) for k in range(2)]
            conv = sb1("conv", [P, IB, TC])
            u = [sb1(f"u{k}", [P, IB, TC]) for k in range(2)]
            zg = [sb1(f"zg{k}", [P, TT, DI]) for k in range(2)]
            bc = sb1("bc", [2 * NS, TC])
            c_tok = [sb1(f"c_tok{k}", [P, TT, 2 * NS]) for k in range(2)]
            dt_in = sb1("dt_in", [P, KD, TC])
            dt_log = conv
            dt = [sb1(f"dt{k}", [P, IB, TC]) for k in range(2)]
            du = [sb1(f"du{k}", [P, IB, TC]) for k in range(2)]
            bb = [sb1(f"bb{k}", [P, TC]) for k in range(NBB)]
            db = [sb1(f"db{k}", [P, IB, TC]) for k in range(2)]
            h = [sb1(f"h{k}", [P, IB, TC]) for k in range(2)]
            carry = sb1("carry", [P, 2, NS, IB])
            y = sb1("y", [P, TT, DI])
            yg = sb1("yg", [P, TT, DI])
            x_res = sb1("x_res", [P, TT, D])
            x1 = x_res
            st_mid = sb1("st_mid", [P, TT, 6])
            mv_mid = sb1("mv_mid", [P, TT, 2])
            nt_mid = sb1("nt_mid", [P, 8, TT])
            xhat = sb1("xhat", [P, TT, D])
            xhatT = sb1("xhatT", [P, KD, TC])
            logitT = sb1("logitT", [E, TC])

            da = [part1.enter_context(nc.psum_tensor(f"da{k}", [P, TC], F32)) for k in range(2)]
            hT = [part1.enter_context(nc.psum_tensor(f"hT{k}", [P, DI], F32)) for k in range(TT)]
            mm = [part1.enter_context(nc.psum_tensor(f"mm{k}", [P, TC], F32)) for k in range(2)]

            with nc.Block() as block:

                @block.sync
                def _(sp):
                    conv_rows = conv_w.rearrange("k a (i p) -> (k a i) p", p=P)
                    sp.dma_start(x_in[:], x_rows[0]).then_inc(x_loaded, 16)
                    for dst, src in (
                        (vec_rows[0:CONVB, :], conv_rows),
                        (vec_rows[CONVB:BDT, :], conv_b.rearrange("(i p) -> i p", p=P)),
                        (vec_rows[BDT:NW, :], b_dt.rearrange("(i p) -> i p", p=P)),
                        (vec_rows[NW:NVEC, :], norm_w.rearrange("(i p) -> i p", p=P)),
                        (b1_rows[:], b_fc1.rearrange("e (f p) -> (e f) p", p=P)),
                        (w_router_rows[:], w_router),
                        (b_router_sb[:], b_router.rearrange("(e a) -> e a", a=1)),
                        (a_raw[:], a_log.rearrange("(i p) s -> p i s", p=P)),
                    ):
                        sp.dma_start(dst, src).then_inc(consts_loaded, 16)
                    sp.dma_start(w_in_sb[:], w_in.rearrange("(k p) n -> p k n", p=P)).then_inc(w_in_loaded, 16)
                    for dst, src in (
                        (w_x_sb[:], w_x.rearrange("(k p) n -> p k n", p=P)),
                        (w_dt_sb[:], w_dt.rearrange("(k p) n -> p k n", p=P)),
                        (w_out_sb[:], w_out.rearrange("(k p) n -> p k n", p=P)),
                    ):
                        sp.dma_start(dst, src).then_inc(weights_loaded, 16)

                    def chunk(q, par, pair, units, post, pre):
                        prev, following = neighbours(q, par, pair)
                        a = q + 1
                        nxt = 1 - par
                        if pre and units:
                            wait(sp, xn_ready, a * TT)
                            sp.sem_inc(wait_held, 1)
                            sp.dma_start(x_in[:], x_rows[following]).then_inc(x_loaded, 16)
                        if post:
                            sp.wait_ge(x1_stored, q * 16)
                            sp.sem_inc(wait_held, 1)
                            sp.dma_start(x_res[:], x_rows[prev]).then_inc(xres_loaded, 16)
                        if units:
                            sp.wait_ge(b_stored, (q + 1) * 16)
                            sp.sem_inc(wait_held, 1)
                            for s in range(NS):
                                wait(sp, db_ready, q * NS + (s - NBB + 1))
                                sp.dma_start(bb[s % NBB][:], b_scratch[par, s:s + 1, :].partition_broadcast(P)
                                             ).then_inc(bb_loaded[s % NBB], 16)
                        if post:
                            store_rows(q, prev, pre)
                        if pre:
                            store_b(q, nxt, post)

                    def store_b(q, nxt, post):
                        evacuated(sp, q, post, True, "bc")
                        for k in range(NBB):
                            sp.sem_inc(wait_held, 1)
                            wait(sp, bb_loaded[k], q * ((NS // NBB) * 16))
                        sp.dma_start(b_scratch[nxt], bc[0:NS, :]).then_inc(b_stored, 16)

                    def store_rows(q, prev, pre):
                        sp.wait_ge(x1_ready, q)
                        sp.sem_inc(wait_held, 1)
                        sp.dma_start(out_rows[prev], x1[:]).then_inc(x1_stored, 16)
                        sp.wait_ge(xhat_ready, q * TT)
                        sp.sem_inc(wait_held, 1)
                        sp.dma_start(xhat_rows[prev], xhat[:]).then_inc(xhat_stored, 16)

                    for stored in (x1_stored, xhat_stored, logit_stored):
                        sp.sem_inc(stored, 16)
                    body(chunk)(sp)
                    for stored in (x1_stored, xhat_stored, logit_stored):
                        sp.wait_ge(stored, (CHUNKS + 1) * 16)
                    sp.wait_ge(weights_loaded, 3 * 16)

                @block.gpsimd
                def _(pool):
                    pool.memset(ident[:], 0.0).then_inc(ident_ready, 1)
                    pool.memset(ones[:], 1.0)
                    for k in range(2):
                        pool.memset(xpad[k][:, :, 0:TAPS - 1], 0.0)
                    pool.memset(carry[:], 0.0).then_inc(carry_zeroed, 1)
                    pool.wait_ge(ident_ready, 1)
                    pool.affine_select(out=ident[:], in_=ident[:], compare_op=ALU.not_equal, fill=1.0,
                                       base=0, pattern=[[-1, P]], channel_multiplier=1).then_inc(ident_ready, 1)
                    pool.wait_ge(carry_zeroed, 1)
                    pool.wait_ge(a_ready, 1)
                    pool.tensor_scalar(a_sb[:], a_exp[:], -1.0, None, ALU.mult).then_inc(a_ready, 1)

                    def chunk(q, par, pair, units, post, pre):
                        a = q + 1
                        nxt = 1 - par
                        for s in range(NS):
                            if units:
                                pool.wait_ge(bb_loaded[s % NBB], (q * (NS // NBB) + (s // NBB + 1)) * 16)
                                if s == 0:
                                    pool.wait_ge(du_ready, q * 2 + 2)
                                wait(pool, scan_done, q * (NS * IB) + (s - 2) * IB + IB)
                                pool.tensor_tensor(db[s % 2][:], du[par][:],
                                                   bb[s % NBB][:].unsqueeze(1).broadcast_to([P, IB, TC]),
                                                   ALU.mult).then_inc(db_ready, 1)
                            if post and s == 9:
                                pool.wait_ge(xres_loaded, q * 16)
                                for t in range(TT):
                                    evacuated(pool, q, post, pre, f"out{t}")
                                pool.tensor_tensor(x1[:], xhat[:], x1[:], ALU.add).then_inc(x1_ready, 1)
                            if pre and s in (14, 15):
                                pool.wait_ge(dt_ready, a + 1)
                                half = slice((s - 14) * 2, (s - 14) * 2 + 2)
                                pool.tensor_tensor(du[nxt][:, half], dt[nxt][:, half], u[nxt][:, half],
                                                   ALU.mult).then_inc(du_ready, 1)

                    body(chunk)(pool)

                @block.scalar
                def _(act):
                    act.preload_act_table_set(LOG_SET)
                    act.wait_ge(consts_loaded, 8 * 16)
                    act.activation(a_exp[:], a_raw[:], ACT.Exp).then_inc(a_ready, 1)
                    act.wait_ge(vec_turned, 1)
                    act.activation(vecs[:, 0:NVEC], mm[0][:, 0:NVEC], ACT.Copy).then_inc(vec_ready, 1)
                    act.activation(b1_cols[:], mm[0][:, 128:256], ACT.Copy).then_inc(vec_ready, 1)
                    act.wait_ge(vec_ready, 2)
                    for k in range(KD):
                        act.activation(w_router_T[:, k, :], mm[0][:, 256 + k * E:256 + (k + 1) * E], ACT.Copy,
                                       scale=vecs[:, NW + k:NW + k + 1]).then_inc(vec_ready, 1)
                    act.wait_ge(a_ready, 2)

                    def chunk(q, par, pair, units, post, pre):
                        a = q + 1
                        p = q - 1
                        nxt = 1 - par
                        prev = neighbours(q, par, pair)[0]

                        for s in range(NS + 2):
                            if units and s < NS:
                                if s == 0:
                                    act.wait_ge(dt_ready, q + 1)
                                decay(q, par, s, 0)
                                decay(q, par, s, 1)
                            if s >= 2:
                                for name in uses(s - 2, post, pre):
                                    evacuate(q, a, p, nxt, post, pre, name)
                            if s == 6 and (pre or units):
                                act.preload_act_table_set(SILU_SET)
                                if pre:
                                    act.wait_ge(taps_added, (a + 1) * ((TAPS - 1) * IB))
                                    act.activation(u[nxt][:], conv[:], ACT.Silu).then_inc(u_ready, 1)
                                if units:
                                    evacuated_before(act, q, post, pre)
                                    act.activation(zg[par][:], zg[par][:], ACT.Silu).then_inc(zg_ready, 1)
                                act.preload_act_table_set(LOG_SET)
                            if pre and s == 12:
                                act.wait_ge(sp_ready, a * 2 + 1)
                                act.activation(dt_log[:], dt_log[:], ACT.Ln, bias=1.0).then_inc(sp_ready, 1)
                            if units and s < NS:
                                decay(q, par, s, 2)
                                decay(q, par, s, 3)
                                if s == 0:
                                    wait(act, y_gated, q)
                                    for t in range(TT):
                                        act.wait_ge(ht_ready, q * ((NS + 1) * TT) + (t + 1))
                                        act.activation(y[:, t, :], hT[t][:], ACT.Copy).then_inc(y_started, 1)
                            if pre and s == 1:
                                act.wait_ge(nw_in, a * 5 + 1)
                                act.activation(nt_in[:, 1, :], nt_in[:, 0, :], ACT.Ln).then_inc(rs_in, 1)
                                act.wait_ge(rs_in, a * 2 + 1)
                                act.activation(nt_in[:, 2, :], nt_in[:, 1, :], ACT.Exp, scale=-0.5).then_inc(rs_in, 1)
                            if post and s == 10:
                                act.wait_ge(nw_mid, p * 5 + 1)
                                act.activation(nt_mid[:, 1, :], nt_mid[:, 0, :], ACT.Ln).then_inc(rs_mid, 1)
                                act.wait_ge(rs_mid, p * 2 + 1)
                                act.activation(nt_mid[:, 2, :], nt_mid[:, 1, :], ACT.Exp, scale=-0.5).then_inc(rs_mid, 1)
                            if post and s == 12:
                                act.wait_ge(shift_ready, p + 1)
                                for t in range(TT):
                                    act.activation(xhat[:, t, :], x1[:, t, :], ACT.Identity,
                                                   scale=nt_mid[:, 6, t:t + 1], bias=nt_mid[:, 7, t:t + 1]
                                                   ).then_inc(xhat_ready, 1)
                            if pre and s == 11:
                                for i in range(IB):
                                    evacuated(act, q, post, pre, f"dt{i}")
                                act.activation(dt_log[:], dt_log[:], ACT.Exp, scale=-1.0).then_inc(sp_ready, 1)
                        if post:
                            for name in ("rt0", "rt1"):
                                evacuated(act, q, post, pre, name)
                                act.sem_inc(wait_held, 1)
                            act.dma_start(logit_chunks[prev], logitT[:]).then_inc(logit_stored, 16)

                    def decay(q, par, s, i):
                        wait(act, scan_done, q * (NS * IB) + (s * IB + i - 1))
                        act.activation(da[i % 2][:], dt[par][:, i, :], ACT.Exp,
                                       scale=a_sb[:, i, s:s + 1]).then_inc(da_ready, 1)

                    def evacuate(q, a, p, nxt, post, pre, name):
                        kind, k = name.rstrip("0123456789"), int(name[-1]) if name[-1].isdigit() else 0
                        if name == "out0":
                            act.wait_ge(xhat_stored, q * 16)
                        if name == "xi0":
                            wait(act, tail_kept, a - 1)
                            wait(act, dt_ready, a)
                        if name == "rt0":
                            act.wait_ge(logit_stored, q * 16)
                        if name == "bc":
                            wait(act, b_stored, a * 16)
                        if name == "dt0":
                            act.wait_ge(u_ready, a + 1)
                        bank, free = mm_wait(act, q, post, pre, name)
                        if kind == "xi":
                            act.activation(conv[:, k, :], bank[:], ACT.Identity,
                                           scale=vecs[:, (TAPS - 1) * IB + k:(TAPS - 1) * IB + k + 1],
                                           bias=vecs[:, CONVB + k:CONVB + k + 1])
                        if kind == "dt":
                            act.activation(dt[nxt][:, k, :], bank[:], ACT.Relu, bias=vecs[:, BDT + k:BDT + k + 1])
                        dst, src, func, kw = {
                            "yT": (du[nxt][:, k, :], bank[:], ACT.Copy, {}),
                            "xnT": (xnT[:, k % KD, :], bank[:], ACT.Copy, {}),
                            "xhT": (xhatT[:, k % KD, :], bank[:], ACT.Copy, {}),
                            "out": (xhat[:, k % TT, :], bank[:, 0:D], ACT.Copy, {}),
                            "xi": (xpad[nxt][:, k, TAPS - 1:], bank[:], ACT.Copy, {}),
                            "z": (zg[nxt][:, k, :], bank[:], ACT.Copy, {}),
                            "bc": (bc[:], bank[0:2 * NS, :], ACT.Copy, {}),
                            "dti": (dt_in[:, k % KD, :], bank[:], ACT.Copy, {}),
                            "ct": (c_tok[nxt][:].rearrange("p t s -> p (t s)"), bank[:, 0:TT * 2 * NS], ACT.Copy, {}),
                            "dt": (dt_log[:, k, :], bank[:], ACT.Abs, {"bias": vecs[:, BDT + k:BDT + k + 1]}),
                            "rt": (logitT[:, (k % 2) * 256:(k % 2 + 1) * 256], bank[0:E, 0:256], ACT.Identity,
                                   {"bias": b_router_sb[:, 0:1]}),
                        }[kind]
                        act.activation(dst, src, func, **kw).then_inc(free, 1)

                    body(chunk)(act)

                @block.tensor
                def _(pe):
                    pe.wait_ge(ident_ready, 2)
                    pe.wait_ge(consts_loaded, 8 * 16)
                    pe.transpose(mm[0][:, 0:NVEC], vec_rows[0:NVEC, :], ident[0:NVEC, 0:NVEC])
                    pe.transpose(mm[0][:, 128:256], b1_rows[:], ident[:])
                    for k in range(KD):
                        last = pe.transpose(mm[0][:, 256 + k * E:256 + (k + 1) * E], w_router_rows[:, k * P:(k + 1) * P],
                                            ident[0:E, 0:E])
                    last.then_inc(vec_turned, 1)
                    pe.wait_ge(vec_ready, 2 + KD)

                    def chunk(q, par, pair, units, post, pre):
                        a = q + 1
                        p = q - 1
                        nxt = 1 - par

                        if units:
                            for t in range(TT):
                                wait(pe, y_added, q * (NS * TT) - (TT - 1 - t))
                                for i in range(IB):
                                    last = pe.transpose(hT[t][:, i * P:(i + 1) * P],
                                                        u[par][:, i, t * P:(t + 1) * P], ident[:])
                                last.then_inc(ht_ready, 1)
                        for s in range(NS):
                            names = uses(s, post, pre)
                            first, rest = (names[:len(names) // 2], names[len(names) // 2:]) if units else ([], names)
                            if units:
                                pe.wait_ge(scan_done, q * (NS * IB) + (s + 1) * IB)
                                for t in range(TT):
                                    if s == 0:
                                        pe.wait_ge(y_started, q * TT + (t + 1))
                                    else:
                                        pe.wait_ge(y_added, q * (NS * TT) + ((s - 1) * TT + t + 1))
                                    for i in range(IB):
                                        last = pe.transpose(hT[t][:, i * P:(i + 1) * P],
                                                            h[s % 2][:, i, t * P:(t + 1) * P], ident[:])
                                    last.then_inc(ht_ready, 1)
                                    if t == 1:
                                        for name in first:
                                            product(q, a, p, nxt, post, pre, name)
                            for name in rest:
                                product(q, a, p, nxt, post, pre, name)

                    def product(q, a, p, nxt, post, pre, name):
                        kind, k = name.rstrip("0123456789"), int(name[-1]) if name[-1].isdigit() else 0

                        def ready(*names):
                            for n in names:
                                evacuated(pe, q, post, pre, n)

                        if name == "yT0":
                            pe.wait_ge(y_gated, q)
                        if name == "xnT0":
                            pe.wait_ge(xn_ready, a * TT + TT)
                        if name == "xhT0":
                            pe.wait_ge(xhat_ready, p * TT + TT)
                        if name == "out0":
                            ready("yT2", "yT3")
                        if name == "xi0":
                            ready("xnT0", "xnT1")
                            if isinstance(q, int) and q < 0:
                                pe.wait_ge(w_in_loaded, 16)
                        if name == "rt0":
                            ready("xhT0", "xhT1")
                        if name == "dti0":
                            pe.wait_ge(u_ready, a + 1)
                            if isinstance(q, int) and q < 0:
                                pe.wait_ge(weights_loaded, 3 * 16)
                        if name == "ct":
                            ready("bc")
                        if name == "dt0":
                            ready("dti0", "dti1")
                        bank = mm_take(q, post, pre, name)
                        if kind == "ct":
                            pe.sem_inc(wait_held, 1)
                            for t in range(TT):
                                last = pe.transpose(bank[:, t * 2 * NS:(t + 1) * 2 * NS], bc[:, t * P:(t + 1) * P],
                                                    ident[0:2 * NS, 0:2 * NS])
                        elif kind in ("yT", "xnT", "xhT"):
                            src = {"yT": yg, "xnT": xn, "xhT": xhat}[kind]
                            for t in range(TT):
                                last = pe.transpose(bank[:, t * P:(t + 1) * P], src[:, t, k * P:(k + 1) * P], ident[:])
                        else:
                            tile = slice(k * P, (k + 1) * P)
                            dst, lhsT, rhs, n = {
                                "xi": (bank[:], lambda j: w_in_sb[:, j, tile], lambda j: xnT[:, j, :], KD),
                                "z": (bank[:], lambda j: xnT[:, j, tile], lambda j: w_in_sb[:, j, DI:2 * DI], KD),
                                "bc": (bank[0:2 * NS, :], lambda j: w_x_sb[:, j, D:D + 2 * NS],
                                       lambda j: u[nxt][:, j, :], IB),
                                "dti": (bank[:], lambda j: w_x_sb[:, j, tile], lambda j: u[nxt][:, j, :], IB),
                                "dt": (bank[:], lambda j: w_dt_sb[:, j, tile], lambda j: dt_in[:, j, :], KD),
                                "out": (bank[:, 0:D], lambda j: du[nxt][:, j, tile], lambda j: w_out_sb[:, j, :], IB),
                                "rt": (bank[0:E, 0:256], lambda j: w_router_T[:, j, :],
                                       lambda j: xhatT[:, j, k * 256:(k + 1) * 256], KD),
                            }[kind]
                            for j in range(n):
                                last = pe.matmul(dst, lhsT(j), rhs(j), start=(j == 0), stop=(j == n - 1))
                        last.then_inc(mm_full, 1)

                    body(chunk)(pe)

                @block.vector
                def _(dve):
                    dve.wait_ge(vec_ready, 2)
                    dve.wait_ge(carry_zeroed, 1)

                    def chunk(q, par, pair, units, post, pre):
                        a = q + 1
                        p = q - 1
                        nxt = 1 - par

                        def add_state(s, t):
                            if s == 0:
                                dve.wait_ge(y_started, q * TT + (t + 1))
                            else:
                                dve.wait_ge(y_added, q * (NS * TT) + ((s - 1) * TT + t + 1))
                            dve.wait_ge(ht_ready, q * ((NS + 1) * TT) + ((s + 1) * TT + t + 1))
                            dve.scalar_tensor_tensor(out=y[:, t, :], in0=hT[t][:],
                                                     scalar=c_tok[par][:, t, NS + s:NS + s + 1], in1=y[:, t, :],
                                                     op0=ALU.mult, op1=ALU.add).then_inc(y_added, 1)

                        def newton(nt, guessed, done, at, guesses):
                            dve.wait_ge(guessed, guesses)
                            dve.tensor_tensor(nt[:, 3, :], nt[:, 0, :], nt[:, 2, :], ALU.mult).then_inc(done, 1)
                            dve.wait_ge(done, at + 2)
                            dve.tensor_tensor(nt[:, 4, :], nt[:, 3, :], nt[:, 2, :], ALU.mult).then_inc(done, 1)
                            dve.wait_ge(done, at + 3)
                            dve.tensor_scalar(nt[:, 5, :], nt[:, 4, :], -0.5, 1.5, ALU.mult, ALU.add).then_inc(done, 1)
                            dve.wait_ge(done, at + 4)
                            dve.tensor_tensor(nt[:, 6, :], nt[:, 5, :], nt[:, 2, :], ALU.mult).then_inc(done, 1)
                            dve.wait_ge(done, at + 5)

                        def softplus():
                            dve.wait_ge(sp_ready, a * 2 + 2)
                            dve.tensor_tensor(dt[nxt][:], dt_log[:], dt[nxt][:], ALU.add).then_inc(dt_ready, 1)

                        def adds_after(s, i):
                            if s == 0:
                                return ()
                            if s == 6:
                                return ((), (0, 1, 2, 3), (), ())[i]
                            return ((), (0,), (1,), (2, 3))[i]

                        def other_taps(s):
                            tiles = (0, 1) if s == 4 else (2, 3)
                            for i in tiles:
                                evacuated(dve, q, post, pre, f"xi{i}")
                            for k in range(TAPS - 1):
                                for i in tiles:
                                    if k:
                                        dve.wait_ge(taps_added, a * ((TAPS - 1) * IB)
                                                    + ((s - 4) * 2 * (TAPS - 1) + 2 * k - 1 + i % 2))
                                    dve.scalar_tensor_tensor(out=conv[:, i, :], in0=xpad[nxt][:, i, k:k + TC],
                                                             scalar=vecs[:, k * IB + i:k * IB + i + 1],
                                                             in1=conv[:, i, :], op0=ALU.mult, op1=ALU.add
                                                             ).then_inc(taps_added, 1)

                        for s in range(NS):
                            if units:
                                dve.wait_ge(db_ready, q * NS + (s + 1))
                                if s >= 2:
                                    dve.wait_ge(ht_ready, q * ((NS + 1) * TT) + s * TT)
                                else:
                                    wait(dve, ht_ready, q * ((NS + 1) * TT) - (2 - s - 1) * TT)
                                wait(dve, carry_kept, q * NS + (s - 1))
                                for i in range(IB):
                                    dve.wait_ge(da_ready, q * (NS * IB) + (s * IB + i + 1))
                                    dve.tensor_tensor_scan(h[s % 2][:, i, :], da[i % 2][:], db[s % 2][:, i, :],
                                                           carry[:, par, s, i:i + 1], ALU.mult, ALU.add
                                                           ).then_inc(scan_done, 1)
                                    for t in adds_after(s, i):
                                        add_state(s - 1, t)
                                    if pre and s in (4, 5) and i == 1:
                                        other_taps(s)
                                    if pre and s == 12 and i == IB - 1:
                                        softplus()
                                dve.wait_ge(scan_done, q * (NS * IB) + (s + 1) * IB)
                                dve.tensor_copy(carry[:, par, s, :], h[s % 2][:, :, TC - 1]).then_inc(carry_kept, 1)
                            if pre and s == 0:
                                dve.wait_ge(x_loaded, (a + 1) * 16)
                                for t in range(TT):
                                    dve.bn_stats(st_in[:, t, :], x_in[:, t, :]).then_inc(stats_in, 1)
                                wait(dve, xn_ready, a * TT)
                                dve.wait_ge(stats_in, a * TT + TT)
                                dve.sem_inc(wait_held, 1)
                                for t in range(TT):
                                    dve.bn_aggr(mv_in[:, t, :], st_in[:, t, :]).then_inc(aggr_in, 1)
                                dve.wait_ge(aggr_in, a * TT + TT)
                                dve.tensor_scalar(nt_in[:, 0, :], mv_in[:, :, 1], EPS, None, ALU.add).then_inc(nw_in, 1)
                            if pre and s == 1:
                                newton(nt_in, rs_in, nw_in, a * 5, a * 2 + 2)
                                evacuated_before(dve, q, post, pre)
                                for t in range(TT):
                                    dve.tensor_scalar(xn[:, t, :], x_in[:, t, :], mv_in[:, t, 0:1], nt_in[:, 6, t:t + 1],
                                                      ALU.subtract, ALU.mult).then_inc(xn_ready, 1)
                            if pre and s in (4, 5) and not units:
                                other_taps(s)
                            if pre and s == 12 and not units:
                                softplus()
                            if pre and s == 5:
                                dve.wait_ge(taps_added, (a + 1) * ((TAPS - 1) * IB))
                                dve.tensor_copy(xpad[nxt][:, :, 0:TAPS - 1], xpad[nxt][:, :, TC:TC + TAPS - 1]
                                                ).then_inc(tail_kept, 1)
                            if post and s == 9:
                                dve.wait_ge(x1_ready, p + 1)
                                for t in range(TT):
                                    dve.bn_stats(st_mid[:, t, :], x1[:, t, :]).then_inc(stats_mid, 1)
                                dve.wait_ge(stats_mid, p * TT + TT)
                                dve.sem_inc(wait_held, 1)
                                for t in range(TT):
                                    dve.bn_aggr(mv_mid[:, t, :], st_mid[:, t, :]).then_inc(aggr_mid, 1)
                                dve.wait_ge(aggr_mid, p * TT + TT)
                                dve.tensor_scalar(nt_mid[:, 0, :], mv_mid[:, :, 1], 1.0 + EPS, EPS * EPS, ALU.mult,
                                                  ALU.add).then_inc(nw_mid, 1)
                            if post and s == 10:
                                newton(nt_mid, rs_mid, nw_mid, p * 5, p * 2 + 2)
                                dve.scalar_tensor_tensor(out=nt_mid[:, 7, :], in0=mv_mid[:, :, 0], scalar=-1.0,
                                                         in1=nt_mid[:, 6, :], op0=ALU.mult, op1=ALU.mult
                                                         ).then_inc(shift_ready, 1)
                        if units:
                            for t in range(TT):
                                add_state(NS - 1, t)
                            dve.wait_ge(y_added, (q + 1) * (NS * TT))
                            dve.wait_ge(zg_ready, q + 1)
                            dve.tensor_tensor(yg[:], y[:], zg[par][:], ALU.mult).then_inc(y_gated, 1)

                    body(chunk)(dve)

        idx_all = sb("idx_all", [P, E * CH], I32)
        wt_all = sb("wt_all", [P, E * CH])
        w1 = [sb(f"w1_{k}", [P, KF, D]) for k in range(2)]
        w2 = [sb(f"w2_{k}", [P, KD, F]) for k in range(2)]
        b2_all = sb("b2_all", [P, E, D])
        b2_loaded = sem("b2_loaded")
        w_loaded = [sem(f"w_loaded{k}") for k in range(2)]
        w_fc1_rows = w_fc1.rearrange("e (f p) d -> e p f d", p=P)
        w_fc2_rows = w_fc2.rearrange("e (k p) f -> e p k f", p=P)

        def load_weights(sp, e, par):
            sp.dma_start(w1[par][:], w_fc1_rows[e]).then_inc(w_loaded[par], 16)
            sp.dma_start(w2[par][:], w_fc2_rows[e]).then_inc(w_loaded[par], 16)

        with ExitStack() as part2:
            def sb2(name, shape, dt=F32):
                return part2.enter_context(nc.sbuf_tensor(name, shape, dt))

            NC = CHUNKS
            BIG = 8192.0
            BITS = 25
            HB = 16
            EH = P // HB
            GROUPS = E // EH

            same = sb2("same", [P, P])
            before = sb2("before", [P, P])
            own = sb2("own", [P, EH])
            iota_hb = sb2("iota_hb", [P, HB], I32)
            token = sb2("token", [P, TT, NC])
            lt = sb2("lt", [P, TC])
            work = sb2("work", [P, TC])
            zero = sb2("zero", [P, TC])
            r_own = sb2("r_own", [P, 1])
            r_all = sb2("r_all", [P, 1])
            lo = sb2("lo", [P, 1])
            mid = sb2("mid", [P, 1])
            taken = sb2("taken", [P, 1])
            step = [sb2(f"step{k}", [P, 1]) for k in range(2)]
            count = sb2("count", [P, 1])
            hi = sb2("hi", [P, 1])
            above = sb2("above", [P, TC])
            band = sb2("band", [P, TC])
            c_above = sb2("c_above", [P, TC])
            c_band = sb2("c_band", [P, TC])
            totals = sb2("totals", [P, 2])
            offs = sb2("offs", [P, 5])
            slot = sb2("slot", [P, TC])
            lg = sb2("lg", [P, TC])
            mask = sb2("mask", [P, TC])
            slot_i = sb2("slot_i", [P, TC], I32)
            slot_hi = sb2("slot_hi", [P, TC], I32)
            slot_lo = sb2("slot_lo", [P, TC], I32)
            ex = sb2("ex", [P, TC])
            wts = sb2("wts", [P, TC])
            best = sb2("best", [P, 4, TT * NC])
            hot_hi = [sb2(f"hot_hi{k}", [P, NC, E, HB]) for k in range(2)]
            hot_lo = [sb2(f"hot_lo{k}", [P, NC, E, HB]) for k in range(2)]
            values = [sb2(f"values{k}", [P, 2, NC, E, HB]) for k in range(2)]
            diag = [sb2(f"diag{k}", [P, 2, HB, EH]) for k in range(GROUPS)]
            listed = sb2("listed", [P, GROUPS, 2, HB])
            list_rows = sb2("list_rows", [2 * E * CH, P])

            route_ready = sem("route_ready")
            lt_loaded = sem("lt_loaded")
            r_ready = sem("r_ready")
            bis = sem("bis")
            counted = sem("counted")
            lg_turned = sem("lg_turned")
            ranked = sem("ranked")
            totalled = sem("totalled")
            slot_turned = sem("slot_turned")
            wt_step = sem("wt_step")
            wt_exp = sem("wt_exp")
            hot_ready = sem("hot_ready")
            tok_ready = sem("tok_ready")
            wv_ready = sem("wv_ready")
            scanned = sem("scanned")
            lists_kept = sem("lists_kept")
            lists_done = sem("lists_done")
            lists_read = sem("lists_read")
            lists_stored = sem("lists_stored")
            lists_loaded = sem("lists_loaded")
            lists_turned = sem("lists_turned")
            idx_ready = sem("idx_ready")

            with ExitStack() as banks:
                ps_count = banks.enter_context(nc.psum_tensor("ps_count", [P, TC], F32))
                ps_lg = banks.enter_context(nc.psum_tensor("ps_lg", [P, TC], F32))
                ps_slot = banks.enter_context(nc.psum_tensor("ps_slot", [P, TC], F32))
                ps_list = [banks.enter_context(nc.psum_tensor(f"ps_list{k}", [P, TC], F32)) for k in range(GROUPS)]
                ps_turn = banks.enter_context(nc.psum_tensor("ps_turn", [P, TC], F32))
                by_jec = ps_lg[:].rearrange("p (j e c) -> p j c e", e=E, c=NC)

                with nc.Block() as block:

                    @block.sync
                    def _(sp):
                        sp.dma_start(lt[:], logit_dram.rearrange("e (c t) -> (e c) t", t=TC)).then_inc(lt_loaded, 16)
                        load_weights(sp, 0, 0)
                        load_weights(sp, 1, 1)
                        sp.dma_start(b2_all[:], b_fc2.rearrange("(a e) d -> a e d", a=1).partition_broadcast(P)
                                     ).then_inc(b2_loaded, 16)
                        sp.wait_ge(lists_read, GROUPS)
                        for v in range(2):
                            sp.dma_start(list_dram[v].rearrange("r (a b) -> (r a) b", b=HB).rearrange(
                                "(g p) b -> p g b", p=P), listed[:, :, v, :]).then_inc(lists_stored, 16)
                        sp.wait_ge(lists_stored, 32)
                        sp.dma_start(list_rows[:], list_dram.rearrange("v r s -> (v r) s")).then_inc(lists_loaded, 16)

                    @block.gpsimd
                    def _(pool):
                        pool.memset(same[:], 1.0).then_inc(route_ready, 1)
                        pool.memset(own[:], 1.0).then_inc(route_ready, 1)
                        pool.memset(zero[:], 0.0)
                        pool.memset(taken[:], 0.0)
                        pool.iota(iota_hb[:], pattern=[[1, HB]], base=0, channel_multiplier=0,
                                  )
                        pool.iota(token[:], pattern=[[P, TT], [TC, NC]], base=0, channel_multiplier=1,
                                  allow_small_or_imprecise_dtypes=True)
                        pool.wait_ge(route_ready, 2)
                        groups = same[:].rearrange("p (e c) -> p e c", c=NC)
                        pool.affine_select(out=groups, in_=groups, compare_op=ALU.is_ge, fill=0.0, base=0,
                                           pattern=[[-NC, E], [0, NC]], channel_multiplier=1).then_inc(route_ready, 1)
                        pool.affine_select(out=own[:], in_=own[:], compare_op=ALU.is_ge, fill=0.0, base=0,
                                           pattern=[[-HB, EH]], channel_multiplier=1).then_inc(route_ready, 1)
                        pool.wait_ge(route_ready, 4)
                        pool.affine_select(out=groups, in_=groups, compare_op=ALU.is_ge, fill=0.0, base=NC - 1,
                                           pattern=[[NC, E], [0, NC]], channel_multiplier=-1).then_inc(route_ready, 1)
                        pool.affine_select(out=own[:], in_=own[:], compare_op=ALU.is_ge, fill=0.0, base=HB - 1,
                                           pattern=[[HB, EH]], channel_multiplier=-1).then_inc(route_ready, 1)
                        pool.wait_ge(route_ready, 6)
                        pool.affine_select(out=before[:], in_=same[:], compare_op=ALU.is_ge, fill=0.0, base=-1,
                                           pattern=[[1, P]], channel_multiplier=-1).then_inc(route_ready, 1)
                        pool.wait_ge(r_ready, 1)
                        pool.partition_all_reduce(r_all[:], r_own[:], P, bass.bass_isa.ReduceOp.max).then_inc(r_ready, 1)
                        for j in range(TT):
                            if j >= 2:
                                pool.wait_ge(lists_done, j - 1)
                            pool.wait_ge(hot_ready, 2 * j + 2)
                            pool.tensor_tensor(values[j % 2][:, 0, :, :, :].rearrange("p c e b -> p c (e b)"),
                                               hot_lo[j % 2][:].rearrange("p c e b -> p c (e b)"),
                                               token[:, j, :].unsqueeze(2).broadcast_to([P, NC, E * HB]),
                                               ALU.mult).then_inc(tok_ready, 1)

                    @block.scalar
                    def _(act):
                        act.wait_ge(wt_step, 7)
                        act.activation(ex[:], ex[:], ACT.Exp).then_inc(wt_exp, 1)
                        act.activation(best[:, 2, :], best[:, 2, :], ACT.Exp).then_inc(wt_exp, 1)

                    @block.tensor
                    def _(pe):
                        pe.wait_ge(lt_loaded, 16)
                        for j in range(TT):
                            last = pe.transpose(ps_lg[:, j * P:(j + 1) * P], lt[:, j * P:(j + 1) * P], ident[:])
                        last.then_inc(lg_turned, 1)
                        pe.wait_ge(route_ready, 7)

                        def count_experts(it, k):
                            pe.wait_ge(bis, it * 10 + (5 * k + 1))
                            pe.matmul(ps_count[:, 0:1], same[:], count[:], start=True, stop=True
                                      ).then_inc(counted, 1)

                        with pe.Fori(0, BITS // 2) as it:
                            count_experts(it, 0)
                            count_experts(it, 1)
                        count_experts(BITS // 2, 0)
                        pe.wait_ge(ranked, 6)
                        pe.matmul(ps_count[:, 2:4], before[:], totals[:], start=True, stop=True)
                        pe.matmul(ps_count[:, 4:5], same[:], totals[:, 0:1], start=True, stop=True).then_inc(totalled, 1)
                        pe.wait_ge(ranked, 12)
                        for j in range(TT):
                            last = pe.transpose(ps_slot[:, j * P:(j + 1) * P], slot[:, j * P:(j + 1) * P], ident[:])
                        last.then_inc(slot_turned, 1)
                        for j in range(TT):
                            pe.wait_ge(hot_ready, 2 * j + 2)
                            pe.wait_ge(tok_ready, j + 1)
                            pe.wait_ge(wv_ready, j + 1)
                            for c in range(NC):
                                for g in range(GROUPS):
                                    e = slice(g * EH, (g + 1) * EH)
                                    last = pe.matmul(
                                        ps_list[g][:, 0:2 * EH * HB],
                                        hot_hi[j % 2][:, c, e, :].rearrange("p e a -> p (e a)"),
                                        values[j % 2][:, :, c, e, :].rearrange("p v e b -> p v (e b)"),
                                        start=(j == 0 and c == 0), stop=(j == TT - 1 and c == NC - 1))
                            last.then_inc(lists_done, 1)
                        pe.wait_ge(lists_loaded, 16)
                        pe.transpose(ps_turn[:, 0:2 * E * CH], list_rows[:], ident[0:2 * E * CH, 0:2 * E * CH]
                                     ).then_inc(lists_turned, 1)

                    @block.vector
                    def _(dve):
                        dve.wait_ge(lt_loaded, 16)
                        dve.tensor_reduce(r_own[:], lt[:], AX.X, ALU.max, apply_absolute_value=True).then_inc(r_ready, 1)
                        dve.wait_ge(r_ready, 2)
                        dve.tensor_scalar(r_own[:].bitcast(I32), r_all[:].bitcast(I32), 0x7F800000, None,
                                          ALU.bitwise_and).then_inc(r_ready, 1)
                        dve.wait_ge(r_ready, 3)
                        dve.tensor_scalar(step[0][:], r_own[:], 2.0, None, ALU.mult).then_inc(r_ready, 1)
                        dve.tensor_scalar(lo[:], r_own[:], -2.0, None, ALU.mult).then_inc(r_ready, 1)
                        dve.wait_ge(route_ready, 7)
                        dve.memset(mid[:], 0.0).then_inc(r_ready, 1)
                        dve.wait_ge(r_ready, 6)
                        def jec(tile):
                            return tile[:].rearrange("p (j e c) -> p j e c", e=E, c=NC)

                        def over_e(k):
                            return best[:, k, :].rearrange("p (j c) -> p j c", c=NC).unsqueeze(2).broadcast_to(
                                [P, TT, E, NC])

                        def row(k):
                            return best[:, k, :].rearrange("p (j c) -> p j c", c=NC)

                        dve.wait_ge(lg_turned, 1)
                        dve.tensor_reduce(row(0), by_jec, AX.X, ALU.max).then_inc(wt_step, 1)

                        def halve(it, k):
                            dve.tensor_scalar(work[:], lt[:], mid[:, 0:1], 0.0, ALU.is_ge, ALU.add,
                                              accum_out=count[:]).then_inc(bis, 1)
                            dve.tensor_tensor(lo[:], lo[:], taken[:], ALU.add).then_inc(bis, 1)
                            dve.tensor_scalar(step[1 - k][:], step[k][:], 0.5, None, ALU.mult).then_inc(bis, 1)
                            dve.wait_ge(bis, it * 10 + (5 * k + 3))
                            dve.wait_ge(counted, it * 2 + (k + 1))
                            dve.tensor_scalar(taken[:], ps_count[:, 0:1], float(CAP), step[k][:, 0:1],
                                              ALU.is_ge, ALU.mult).then_inc(bis, 1)
                            dve.wait_ge(bis, it * 10 + (5 * k + 4))
                            dve.scalar_tensor_tensor(out=mid[:], in0=taken[:], scalar=step[1 - k][:, 0:1],
                                                     in1=lo[:], op0=ALU.add, op1=ALU.add).then_inc(bis, 1)
                            dve.wait_ge(bis, it * 10 + (5 * k + 5))

                        with dve.Fori(0, BITS // 2) as it:
                            halve(it, 0)
                            halve(it, 1)
                        halve(BITS // 2, 0)
                        dve.tensor_tensor(lo[:], lo[:], taken[:], ALU.add).then_inc(ranked, 1)
                        dve.wait_ge(ranked, 1)
                        dve.tensor_tensor(hi[:], lo[:], step[0][:], ALU.add).then_inc(ranked, 1)
                        dve.wait_ge(ranked, 2)
                        dve.tensor_scalar(above[:], lt[:], hi[:, 0:1], None, ALU.is_ge).then_inc(ranked, 1)
                        dve.wait_ge(ranked, 3)
                        dve.scalar_tensor_tensor(out=band[:], in0=lt[:], scalar=lo[:, 0:1], in1=above[:],
                                                 op0=ALU.is_ge, op1=ALU.subtract).then_inc(ranked, 1)
                        dve.tensor_tensor_scan(c_above[:], above[:], zero[:], 0.0, ALU.add, ALU.add).then_inc(scanned, 1)
                        dve.wait_ge(ranked, 4)
                        dve.tensor_tensor_scan(c_band[:], band[:], zero[:], 0.0, ALU.add, ALU.add).then_inc(scanned, 1)
                        dve.wait_ge(scanned, 2)
                        dve.tensor_copy(totals[:, 0:1], c_above[:, TC - 1:TC]).then_inc(ranked, 1)
                        dve.tensor_copy(totals[:, 1:2], c_band[:, TC - 1:TC]).then_inc(ranked, 1)
                        dve.wait_ge(totalled, 1)
                        dve.tensor_copy(offs[:, 0:3], ps_count[:, 2:5]).then_inc(ranked, 1)
                        dve.wait_ge(ranked, 7)
                        dve.tensor_scalar(offs[:, 3:4], offs[:, 1:2], offs[:, 2:3], -1.0 - BIG, ALU.add, ALU.add
                                          ).then_inc(ranked, 1)
                        dve.tensor_scalar(offs[:, 4:5], offs[:, 0:1], -1.0 - BIG, None, ALU.add).then_inc(ranked, 1)
                        dve.wait_ge(ranked, 9)
                        dve.scalar_tensor_tensor(out=c_above[:], in0=c_above[:], scalar=offs[:, 4:5], in1=above[:],
                                                 op0=ALU.add, op1=ALU.mult).then_inc(ranked, 1)
                        dve.scalar_tensor_tensor(out=c_band[:], in0=c_band[:], scalar=offs[:, 3:4], in1=band[:],
                                                 op0=ALU.add, op1=ALU.mult).then_inc(ranked, 1)
                        dve.wait_ge(ranked, 11)
                        dve.scalar_tensor_tensor(out=slot[:], in0=c_above[:], scalar=BIG, in1=c_band[:],
                                                 op0=ALU.add, op1=ALU.add).then_inc(ranked, 1)
                        dve.wait_ge(slot_turned, 1)
                        dve.tensor_copy(slot_i[:], ps_slot[:]).then_inc(ranked, 1)
                        dve.tensor_scalar(mask[:], ps_slot[:], float(CAP), None, ALU.is_lt).then_inc(ranked, 1)
                        dve.wait_ge(ranked, 13)
                        dve.tensor_scalar(slot_hi[:], slot_i[:], 4, None, ALU.arith_shift_right).then_inc(ranked, 1)
                        dve.tensor_scalar(slot_lo[:], slot_i[:], HB - 1, None, ALU.bitwise_and).then_inc(ranked, 1)

                        dve.wait_ge(ranked, 14)
                        dve.tensor_scalar(work[:], mask[:], -1.0, 1e30, ALU.add, ALU.mult).then_inc(wt_step, 1)
                        dve.tensor_tensor(lg[:], ps_lg[:], mask[:], ALU.mult).then_inc(wt_step, 1)
                        dve.wait_ge(wt_step, 3)
                        dve.tensor_tensor(lg[:], lg[:], work[:], ALU.add).then_inc(wt_step, 1)
                        dve.wait_ge(wt_step, 4)
                        dve.tensor_reduce(row(1), lg[:].rearrange("p (j e c) -> p j c e", e=E, c=NC), AX.X, ALU.max
                                          ).then_inc(wt_step, 1)
                        dve.wait_ge(wt_step, 5)
                        dve.tensor_tensor(best[:, 2, :], best[:, 1, :], best[:, 0, :], ALU.subtract).then_inc(wt_step, 1)
                        dve.tensor_tensor(jec(ex), jec(lg), over_e(1), ALU.subtract).then_inc(wt_step, 1)

                        def hot(j):
                            if j >= 2:
                                dve.wait_ge(lists_done, j - 1)
                            for dst, part in ((hot_hi, slot_hi), (hot_lo, slot_lo)):
                                dve.tensor_tensor(
                                    dst[j % 2][:],
                                    part[:, j * P:(j + 1) * P].rearrange("p (e c) -> p c e", c=NC).unsqueeze(3
                                                                         ).broadcast_to([P, NC, E, HB]),
                                    iota_hb[:].unsqueeze(1).unsqueeze(1).broadcast_to([P, NC, E, HB]),
                                    ALU.is_equal).then_inc(hot_ready, 1)

                        def weights_by_low(j):
                            dve.wait_ge(hot_ready, 2 * j + 2)
                            dve.tensor_tensor(
                                values[j % 2][:, 1], hot_lo[j % 2][:],
                                wts[:, j * P:(j + 1) * P].rearrange("p (e c) -> p c e", c=NC).unsqueeze(3
                                                                    ).broadcast_to([P, NC, E, HB]),
                                ALU.mult).then_inc(wv_ready, 1)

                        dve.wait_ge(ranked, 16)
                        hot(0)
                        dve.wait_ge(wt_exp, 2)
                        dve.tensor_tensor(ex[:], ex[:], mask[:], ALU.mult).then_inc(wt_step, 1)
                        dve.wait_ge(wt_step, 8)
                        dve.tensor_reduce(row(3), ex[:].rearrange("p (j e c) -> p j c e", e=E, c=NC), AX.X, ALU.add
                                          ).then_inc(wt_step, 1)
                        dve.wait_ge(wt_step, 9)
                        dve.scalar_tensor_tensor(out=best[:, 3, :], in0=best[:, 3, :], scalar=0.0, in1=best[:, 3, :],
                                                 op0=ALU.is_le, op1=ALU.add).then_inc(wt_step, 1)
                        dve.wait_ge(wt_step, 10)
                        dve.reciprocal(best[:, 3, :], best[:, 3, :]).then_inc(wt_step, 1)
                        dve.wait_ge(wt_step, 11)
                        dve.scalar_tensor_tensor(out=best[:, 3, :], in0=best[:, 2, :], scalar=0.0, in1=best[:, 3, :],
                                                 op0=ALU.is_gt, op1=ALU.mult).then_inc(wt_step, 1)
                        dve.wait_ge(wt_step, 12)
                        dve.tensor_tensor(jec(wts), jec(ex), over_e(3), ALU.mult).then_inc(wt_step, 1)
                        dve.wait_ge(wt_step, 13)
                        weights_by_low(0)
                        for j in range(1, TT):
                            hot(j)
                            weights_by_low(j)
                        dve.wait_ge(lists_done, TT)
                        for g in range(GROUPS):
                            dve.tensor_tensor(diag[g][:],
                                              ps_list[g][:, 0:2 * EH * HB].rearrange("p (v e b) -> p v b e", e=EH, b=HB),
                                              own[:].unsqueeze(1).unsqueeze(1).broadcast_to([P, 2, HB, EH]),
                                              ALU.mult).then_inc(lists_kept, 1)
                        for g in range(GROUPS):
                            dve.wait_ge(lists_kept, g + 1)
                            dve.tensor_reduce(listed[:, g], diag[g][:], AX.X, ALU.add).then_inc(lists_read, 1)
                        dve.wait_ge(lists_turned, 1)
                        dve.tensor_copy(idx_all[:], ps_turn[:, 0:E * CH]).then_inc(idx_ready, 1)
                        dve.tensor_copy(wt_all[:], ps_turn[:, E * CH:2 * E * CH]).then_inc(idx_ready, 1)

        with ExitStack() as part3:
            def sb3(name, shape, dt=F32):
                return part3.enter_context(nc.sbuf_tensor(name, shape, dt))

            def psum3(name):
                return part3.enter_context(nc.psum_tensor(name, [P, 512], F32))

            def parts(name, shape):
                return [sb3(f"{name}_{part}", shape, BF16) for part in ("hi", "lo")]

            w1T = [parts(f"w1T{k}", [P, KD, F]) for k in range(2)]
            w2T = [parts(f"w2T{k}", [P, KF, D]) for k in range(2)]
            xe = [[sb3(f"xe{k}_{half}", [P, D]) for half in range(CH)] for k in range(2)]
            xeT = [parts(f"xeT{k}", [P, KD, CAP]) for k in range(2)]
            hid = sb3("hid", [P, KF, CAP])
            hid_parts = parts("hid", [P, KF, CAP])
            ye = [sb3(f"ye{half}", [P, D]) for half in range(CH)]
            gather_idx = [sb3(f"gather_idx{k}", [P, CH], I32) for k in range(2)]
            scatter_idx = sb3("scatter_idx", [P, CH], I32)
            wt_e = sb3("wt_e", [P, CH])
            b1_e = [sb3(f"b1_e{k}", [P, KF]) for k in range(2)]

            hb = [psum3(f"hb{k}") for k in range(KF // 2)]
            yb = psum3("yb")
            TURNS = 3
            turn = [psum3(f"turn{k}") for k in range(TURNS)]
            USES = [("w1", k) for k in range(4)] + [("w2", k) for k in range(4)] + [("x", 0)]
            NU = len(USES)
            BETWEEN = [[0], [1], [2], [3, 4, 5]]
            AFTER = [6, 7, 8]
            assert NU % TURNS == 0

            xe_loaded = [sem(f"xe_loaded{k}") for k in range(2)]
            gidx_ready = sem("gidx_ready")
            b1_ready = sem("b1_ready")
            turn_full = sem("turn_full")
            turn_free = [sem(f"turn_free{k}") for k in range(TURNS)]
            hi_ready = sem("hi_ready")
            hid_hi = sem("hid_hi")
            hid_lo = sem("hid_lo")
            h_full = sem("h_full")
            gelu_done = sem("gelu_done")
            y_full = sem("y_full")
            y_cols = sem("y_cols")
            y_biased = sem("y_biased")
            y_ready = sem("y_ready")
            scattered = sem("scattered")

            def span(e, n):
                return slice(e * n, (e + 1) * n) if isinstance(e, int) else bass.ds(e * n, n)

            def experts(first, expert):
                with_next = dict(turn_next=True, fetch_next=True)

                def run(eng):
                    first()
                    expert(0, 0, **with_next)
                    with eng.Fori(0, (E - 4) // 2) as pair:
                        expert(pair * 2 + 1, 1, loads=pair + 2, **with_next)
                        expert(pair * 2 + 2, 0, loads=pair + 2, **with_next)
                    expert(E - 3, 1, **with_next)
                    expert(E - 2, 0, turn_next=True, fetch_next=False)
                    expert(E - 1, 1, turn_next=False, fetch_next=False)
                return run

            with nc.Block() as block:

                @block.sync
                def _(sp):
                    def expert(e, par, turn_next, fetch_next, loads=None):
                        if fetch_next:
                            sp.wait_ge(turn_full, (e + 1) * NU)
                            sp.sem_inc(wait_held, 1)
                            load_weights(sp, e + 2, par)

                    experts(lambda: None, expert)(sp)
                    sp.wait_ge(b2_loaded, 16)
                    sp.wait_ge(scattered, E * CH * 16)

                @block.gpsimd
                def _(pool):
                    def gather(e, par):
                        pool.wait_ge(gidx_ready, e + 1)
                        if not isinstance(e, int):
                            pool.sem_inc(wait_held, 1)
                        for half in range(CH):
                            pool.indirect_dma_start(
                                out=xe[par][half][:], out_offset=None, in_=xhat_dram,
                                in_offset=bass.IndirectOffsetOnAxis(ap=gather_idx[par][:, half:half + 1], axis=0)
                            ).then_inc(xe_loaded[par], 16)

                    def first():
                        gather(0, 0)
                        gather(1, 1)

                    def expert(e, par, turn_next, fetch_next, loads=None):
                        if fetch_next:
                            pool.wait_ge(turn_full, e * NU + NU)
                            gather(e + 2, par)
                        pool.wait_ge(y_ready, e * CH + CH)
                        wait(pool, scattered, e * (CH * 16))
                        pool.sem_inc(wait_held, 1)
                        for half in range(CH):
                            pool.indirect_dma_start(
                                out=out_flat, out_offset=bass.IndirectOffsetOnAxis(
                                    ap=scatter_idx[:, half:half + 1], axis=0),
                                in_=ye[half][:], in_offset=None, compute_op=ALU.add
                            ).then_inc(scattered, 16)

                    experts(first, expert)(pool)

                def target(n, par):
                    kind, k = USES[n]
                    if kind == "x":
                        return [part[:].rearrange("p k s -> p (k s)") for part in xeT[par]], None
                    if kind == "w1":
                        cols = slice(k % 2 * 512, (k % 2 + 1) * 512)
                        return [part[:, k // 2, cols] for part in w1T[par]], vecs[:, NW + k // 2:NW + k // 2 + 1]
                    return [part[:, 2 * k:2 * k + 2, :].rearrange("p f d -> p (f d)") for part in w2T[par]], None

                def turned_hi(act, e, par, n):
                    (high, _), scale = target(n, par)
                    act.wait_ge(turn_full, e * NU + (n + 1))
                    act.activation(high, turn[n % TURNS][:], ACT.Copy, scale=1.0 if scale is None else scale
                                   ).then_inc(hi_ready, 1)

                def turned_lo(dve, e, par, n):
                    (high, low), scale = target(n, par)
                    dve.wait_ge(hi_ready, e * NU + (n + 1))
                    bank = turn[n % TURNS]
                    if scale is None:
                        done = dve.tensor_tensor(low, bank[:], high, ALU.subtract)
                    else:
                        done = dve.scalar_tensor_tensor(out=low, in0=bank[:], scalar=scale, in1=high,
                                                        op0=ALU.mult, op1=ALU.subtract)
                    done.then_inc(turn_free[n % TURNS], 1)

                @block.scalar
                def _(act):
                    act.preload_act_table_set("gelu_and_others")

                    def first():
                        for n in range(NU):
                            turned_hi(act, 0, 0, n)

                    def expert(e, par, turn_next, fetch_next, loads=None):
                        act.wait_ge(b1_ready, e + 1)
                        for k in range(KF // 2):
                            act.wait_ge(h_full, e * (KF // 2) + (k + 1))
                            for f in (2 * k, 2 * k + 1):
                                act.activation(hid[:, f, :], hb[k][:, f % 2 * CAP:(f % 2 + 1) * CAP], ACT.Gelu,
                                               bias=b1_e[par][:, f:f + 1]).then_inc(gelu_done, 1)
                            act.wait_ge(gelu_done, e * KF + (2 * k + 2))
                            act.activation(hid_parts[0][:, 2 * k:2 * k + 2, :], hid[:, 2 * k:2 * k + 2, :], ACT.Copy
                                           ).then_inc(hid_hi, 1)
                            if turn_next:
                                for n in BETWEEN[k]:
                                    turned_hi(act, e + 1, 1 - par, n)
                        if turn_next:
                            for n in AFTER:
                                turned_hi(act, e + 1, 1 - par, n)

                    experts(first, expert)(act)

                @block.tensor
                def _(pe):
                    def turn_use(e, par, loads, n):
                        kind, k = USES[n]
                        if kind == "x":
                            pe.wait_ge(xe_loaded[par], loads * (CH * 16))
                            pe.sem_inc(wait_held, 1)
                        if kind == "w1" and k == 0:
                            pe.wait_ge(w_loaded[par], loads * 32)
                            pe.sem_inc(wait_held, 1)
                        bank = turn[n % TURNS]
                        before = e * (NU // TURNS) + n // TURNS
                        wait(pe, turn_free[n % TURNS], before)
                        pe.sem_inc(wait_held, 1)
                        for i in range(4):
                            if kind == "x":
                                src = xe[par][i % 2][:, i // 2 * P:(i // 2 + 1) * P]
                            elif kind == "w1":
                                src = w1[par][:, k % 2 * 4 + i, k // 2 * P:(k // 2 + 1) * P]
                            else:
                                f = 2 * k + i // 2
                                src = w2[par][:, i % 2, f * P:(f + 1) * P]
                            last = pe.transpose(bank[:, i * P:(i + 1) * P], src, ident[:])
                        last.then_inc(turn_full, 1)

                    def product3(out, a, b, cols_a, cols_b, start, stop):
                        for i, (x, y) in enumerate(((0, 0), (0, 1), (1, 0))):
                            last = pe.matmul(out, cols_a(a[x]), cols_b(b[y]), start=start and i == 0, stop=stop and i == 2)
                        return last

                    def first():
                        for n in range(NU):
                            turn_use(0, 0, 1, n)

                    def expert(e, par, turn_next, fetch_next, loads=None):
                        if isinstance(e, int):
                            loads = (e + 1) // 2 + 1

                        def turn_next_use(n):
                            if turn_next:
                                turn_use(e + 1, 1 - par, loads, n)

                        for k in range(TURNS):
                            pe.wait_ge(turn_free[k], (e + 1) * (NU // TURNS))
                        for f in range(KF):
                            for k in range(KD):
                                last = product3(hb[f // 2][:, f % 2 * CAP:(f % 2 + 1) * CAP], w1T[par], xeT[par],
                                                lambda part: part[:, k, f * P:(f + 1) * P], lambda part: part[:, k, :],
                                                k == 0, k == KD - 1)
                            if f % 2:
                                last.then_inc(h_full, 1)
                                for n in BETWEEN[f // 2]:
                                    turn_next_use(n)
                        wait(pe, y_biased, e * CH)
                        after = list(AFTER)
                        for half in range(CH):
                            for f in range(KF):
                                if half == 0 and f % 2 == 0:
                                    pe.wait_ge(hid_lo, e * (KF // 2) + (f // 2 + 1))
                                last = product3(yb[:, half * D:(half + 1) * D], hid_parts, w2T[par],
                                                lambda part: part[:, f, half * P:(half + 1) * P],
                                                lambda part: part[:, f, :], f == 0, f == KF - 1)
                                if f % 4 == 3 and after:
                                    if half == CH - 1 and f == KF - 1:
                                        break
                                    turn_next_use(after.pop(0))
                        last.then_inc(y_full, 1)

                    experts(first, expert)(pe)

                @block.vector
                def _(dve):
                    def columns(e, par):
                        dve.tensor_copy(gather_idx[par][:], idx_all[:, span(e, CH)]).then_inc(gidx_ready, 1)

                    def biases(e, par):
                        dve.tensor_copy(b1_e[par][:], b1_cols[:, span(e, KF)]).then_inc(b1_ready, 1)

                    def first():
                        columns(0, 0)
                        columns(1, 1)
                        biases(0, 0)
                        for n in range(NU):
                            turned_lo(dve, 0, 0, n)
                        dve.wait_ge(b2_loaded, 16)

                    def expert(e, par, turn_next, fetch_next, loads=None):
                        if fetch_next:
                            dve.wait_ge(turn_full, e * NU + NU)
                            dve.sem_inc(wait_held, 1)
                            columns(e + 2, par)
                        if turn_next:
                            wait(dve, gelu_done, e * KF)
                            dve.sem_inc(wait_held, 1)
                            biases(e + 1, 1 - par)
                        for k in range(KF // 2):
                            dve.wait_ge(hid_hi, e * (KF // 2) + (k + 1))
                            two = slice(2 * k, 2 * k + 2)
                            dve.tensor_tensor(hid_parts[1][:, two, :], hid[:, two, :], hid_parts[0][:, two, :],
                                              ALU.subtract).then_inc(hid_lo, 1)
                            if turn_next:
                                for n in BETWEEN[k]:
                                    turned_lo(dve, e + 1, 1 - par, n)
                        if turn_next:
                            for n in AFTER:
                                turned_lo(dve, e + 1, 1 - par, n)
                        wait(dve, scattered, e * (CH * 16))
                        dve.sem_inc(wait_held, 1)
                        dve.tensor_copy(scatter_idx[:], idx_all[:, span(e, CH)]).then_inc(y_cols, 1)
                        wait(dve, y_ready, e * CH)
                        dve.sem_inc(wait_held, 1)
                        dve.tensor_copy(wt_e[:], wt_all[:, span(e, CH)]).then_inc(y_cols, 1)
                        dve.wait_ge(y_full, e + 1)
                        for half in range(CH):
                            dve.tensor_tensor(ye[half][:], yb[:, half * D:(half + 1) * D], b2_all[:, e, :], ALU.add
                                              ).then_inc(y_biased, 1)
                        dve.wait_ge(y_cols, e * 2 + 2)
                        for half in range(CH):
                            dve.wait_ge(y_biased, e * CH + (half + 1))
                            last = dve.tensor_scalar(ye[half][:], ye[half][:], wt_e[:, half:half + 1], None, ALU.mult)
                            last.then_inc(y_ready, 1)

                    experts(first, expert)(dve)


_INS = ['L0_attn_inputs', 'L0_attn_W_in', 'L0_attn_conv_w', 'L0_attn_conv_b', 'L0_attn_W_x', 'L0_attn_W_dt',
        'L0_attn_b_dt', 'L0_attn_A_log', 'L0_attn_W_out', 'L0_ffn_norm_weight', 'L0_ffn_router_weight',
        'L0_ffn_router_bias', 'L0_ffn_fc1_weight', 'L0_ffn_fc1_bias', 'L0_ffn_fc2_weight', 'L0_ffn_fc2_bias']
_OUTS = [((2, 2048, 256), 'float32')]


def kernel(**inputs):
    import numpy as _np
    import concourse.bacc as _bacc
    from concourse import mybir as _mybir
    from concourse.bass_utils import run_bass_kernel_spmd as _run

    nc = _bacc.Bacc("TRN2", target_bir_lowering=False, num_devices=1)
    arrays, args = {}, []
    for name in _INS:
        a = _np.ascontiguousarray(inputs[name])
        arrays[f"in_{name}_dram"] = a
        args.append(nc.dram_tensor(f"in_{name}_dram", a.shape, _mybir.dt.from_np(a.dtype), kind="ExternalInput").ap())
    for i, (shape, dtype) in enumerate(_OUTS):
        dt = _mybir.dt.from_np(_np.dtype(dtype))
        args.append(nc.dram_tensor(f"out_{i}_dram", shape, dt, kind="ExternalOutput").ap())
    mixer_moe(nc, *args)
    r = _run(nc, [arrays], core_ids=[0])
    return r.results[0]["out_0_dram"]
```

```python
from contextlib import ExitStack

import concourse.bass as bass
from concourse import mybir

ALU = mybir.AluOpType
ACT = mybir.ActivationFunctionType
AX = mybir.AxisListType
F32 = mybir.dt.float32
BF16 = mybir.dt.bfloat16
I32 = mybir.dt.int32

P = 128
EPS = 1e-5
LOG_SET = "natural_log_exp_and_others"
SILU_SET = "silu_and_others"


def mixer_moe(nc, x, w_in, conv_w, conv_b, w_x, w_dt, b_dt, a_log, w_out,
              norm_w, w_router, b_router, w_fc1, b_fc1, w_fc2, b_fc2, out):
    BATCH, SEQ, D = x.shape
    DI = w_dt.shape[1]
    NS = a_log.shape[1]
    TAPS = conv_w.shape[0]
    E, F, _ = w_fc1.shape
    N = BATCH * SEQ
    TC = 512
    TT = TC // P
    KD = D // P
    IB = DI // P
    KF = F // P
    CAP = N // E
    CH = CAP // P
    CHUNKS = N // TC
    TILES = N // P
    assert BATCH == 2 and TC == 512 and NS == 16 and E == 16 and CHUNKS == 8 and CAP == 256

    x_rows = x.rearrange("b (c t p) d -> (b c) p t d", t=TT, p=P)
    out_rows = out.rearrange("b (c t p) d -> (b c) p t d", t=TT, p=P)
    out_flat = out.rearrange("b s d -> (b s) d")

    b_scratch = nc.dram_tensor("b_scratch", [2, NS, TC], F32, kind="Internal").ap()
    xhat_dram = nc.dram_tensor("xhat_dram", [N, D], F32, kind="Internal").ap()
    xhat_rows = xhat_dram.rearrange("(c t p) d -> c p t d", t=TT, p=P)
    logit_dram = nc.dram_tensor("logit_dram", [E, N], F32, kind="Internal").ap()
    logit_chunks = logit_dram.rearrange("e (c t) -> c e t", t=TC)
    list_dram = nc.dram_tensor("list_dram", [2, E * CH, P], F32, kind="Internal").ap()

    with ExitStack() as ctx:
        def sb(name, shape, dt=F32):
            return ctx.enter_context(nc.sbuf_tensor(name, shape, dt))

        def psum(name, shape, dt=F32):
            return ctx.enter_context(nc.psum_tensor(name, shape, dt))

        def sem(name):
            return ctx.enter_context(nc.semaphore(name))

        ident = sb("ident", [P, P])
        NVEC = TAPS * IB + IB + IB + KD
        CONVB, BDT, NW = TAPS * IB, TAPS * IB + IB, TAPS * IB + 2 * IB
        vec_rows = sb("vec_rows", [32, P])
        vecs = sb("vecs", [P, 32])
        b1_rows = sb("b1_rows", [P, P])
        b1_cols = sb("b1_cols", [P, E * KF])
        b_router_sb = sb("b_router_sb", [E, 1])
        w_router_rows = sb("w_router_rows", [E, D])
        w_router_T = sb("w_router_T", [P, KD, E])

        NC = CHUNKS
        HB = 16
        EH = P // HB
        GROUPS = E // EH
        same = sb("same", [P, P])
        before = sb("before", [P, P])
        own = sb("own", [P, EH])
        iota_hb = sb("iota_hb", [P, HB], I32)
        token = sb("token", [P, TT, NC])

        route_ready = sem("route_ready")
        consts_loaded = sem("consts_loaded")
        w_in_loaded = sem("w_in_loaded")
        weights_loaded = sem("weights_loaded")
        ident_ready = sem("ident_ready")
        vec_turned = sem("vec_turned")
        vec_ready = sem("vec_ready")
        a_ready = sem("a_ready")
        carry_zeroed = sem("carry_zeroed")
        wait_held = sem("wait_held")

        x_loaded = sem("x_loaded")
        xres_loaded = sem("xres_loaded")
        stats_in = sem("stats_in")
        aggr_in = sem("aggr_in")
        rs_in = sem("rs_in")
        nw_in = sem("nw_in")
        shift_in = sem("shift_in")
        xn_ready = sem("xn_ready")
        taps_added = sem("taps_added")
        taps_scaled = sem("taps_scaled")
        taps_shared = sem("taps_shared")
        tail_kept = sem("tail_kept")
        u_ready = sem("u_ready")
        zg_ready = sem("zg_ready")
        b_stored = sem("b_stored")
        sp_ready = sem("sp_ready")
        dt_ready = sem("dt_ready")
        dt_shared = sem("dt_shared")
        du_ready = sem("du_ready")
        mm_full = sem("mm_full")
        mm_free = [sem("mm_free0"), sem("mm_free1")]

        NBB = 4
        bb_loaded = [sem(f"bb_loaded{k}") for k in range(NBB)]
        da_ready = sem("da_ready")
        db_ready = sem("db_ready")
        scan_done = sem("scan_done")
        carry_kept = sem("carry_kept")
        ht_ready = sem("ht_ready")
        last_scaled = sem("last_scaled")
        last_added = sem("last_added")
        y_started = sem("y_started")
        y_added = sem("y_added")
        y_gated = sem("y_gated")
        x1_ready = sem("x1_ready")
        stats_mid = sem("stats_mid")
        aggr_mid = sem("aggr_mid")
        rs_mid = sem("rs_mid")
        nw_mid = sem("nw_mid")
        shift_ready = sem("shift_ready")
        xhat_ready = sem("xhat_ready")
        x1_stored = sem("x1_stored")
        xhat_stored = sem("xhat_stored")
        logit_stored = sem("logit_stored")

        VT = TT - 1
        SHARED = (1, 3, 5, 7, 9, 13)

        def shared_before(s):
            return sum(k < s for k in SHARED)

        SLOTS = [["yT0", "yT1", "yT2", "yT3"], ["xnT0", "xnT1"], ["xi0", "xi1"], ["xi2", "xi3"],
                 ["out0", "out1"], ["out2", "out3"], ["dti0"], ["dti1"], ["dt0", "dt1"], ["dt2", "dt3"],
                 ["bc"], ["ct", "z0", "z1"], ["xhT0", "xhT1", "z2"], ["z3", "rt0"], ["rt1"], []]
        OF_POST = ("yT", "out", "xhT", "rt")
        BOTH = [name for slot in SLOTS for name in slot]
        POST = [name for name in BOTH if name.startswith(OF_POST)]
        PRE = [name for name in BOTH if not name.startswith(OF_POST)]
        NPOST, NPRE = len(POST), len(PRE)
        assert NPOST % 2 == 0 and NPRE % 2 == 0

        def uses(s, post, pre):
            return [name for name in SLOTS[s] if (post if name.startswith(OF_POST) else pre)]

        def mm_number(q, post, pre, name):
            order = BOTH if post and pre else POST if post else PRE
            if isinstance(q, int) and q < 1:
                base = NPRE * (q + 1)
            elif isinstance(q, int):
                base = NPRE * min(q + 1, CHUNKS) + NPOST * (q - 1)
            else:
                base = q * (NPRE + NPOST) + (NPRE - NPOST)
            return base, order.index(name)

        def wait(eng, semaphore, value):
            if not isinstance(value, int) or value > 0:
                eng.wait_ge(semaphore, value)

        def banks_before(q, post, pre, name):
            base, k = mm_number(q, post, pre, name)
            bank = k % 2
            if isinstance(base, int):
                return bank, base // 2 + k // 2
            return bank, q * ((NPRE + NPOST) // 2) + ((NPRE - NPOST) // 2 + k // 2)

        def mm_take(q, post, pre, name):
            bank, before = banks_before(q, post, pre, name)
            wait(nc.tensor, mm_free[bank], before)
            return mm[bank]

        def mm_wait(eng, q, post, pre, name):
            base, k = mm_number(q, post, pre, name)
            bank = k % 2
            eng.wait_ge(mm_full, base + (k + 1))
            return mm[bank], mm_free[bank]

        def evacuated(eng, q, post, pre, name):
            bank, before = banks_before(q, post, pre, name)
            eng.wait_ge(mm_free[bank], before + 1)

        def evacuated_before(eng, q, post, pre):
            order = BOTH if post and pre else POST if post else PRE
            for name in order[0:2]:
                bank, before = banks_before(q, post, pre, name)
                wait(eng, mm_free[bank], before)

        def body(chunk):
            def run(eng):
                chunk(-1, 1, 0, units=False, post=False, pre=True)
                chunk(0, 0, 0, units=True, post=False, pre=True)
                with eng.Fori(0, (CHUNKS - 2) // 2) as pair:
                    chunk(pair * 2 + 1, 1, pair, units=True, post=True, pre=True)
                    chunk(pair * 2 + 2, 0, pair, units=True, post=True, pre=True)
                chunk(CHUNKS - 1, 1, CHUNKS // 2 - 1, units=True, post=True, pre=False)
                chunk(CHUNKS, 0, CHUNKS // 2, units=False, post=True, pre=False)
            return run

        def neighbours(q, par, pair):
            if isinstance(q, int):
                return (1 - par) * (CHUNKS // 2) + (q - 1) // 2, (1 - par) * (CHUNKS // 2) + (q + 1) // 2
            if par == 1:
                return pair, pair + 1
            return pair + CHUNKS // 2, pair + (CHUNKS // 2 + 1)

        with ExitStack() as part1:
            def sb1(name, shape, dt=F32):
                return part1.enter_context(nc.sbuf_tensor(name, shape, dt))

            w_in_sb = sb1("w_in_sb", [P, KD, 2 * DI])
            w_x_sb = sb1("w_x_sb", [P, IB, D + 2 * NS])
            w_dt_sb = sb1("w_dt_sb", [P, KD, DI])
            w_out_sb = sb1("w_out_sb", [P, IB, D])
            a_raw = sb1("a_raw", [P, IB, NS])
            a_exp = sb1("a_exp", [P, IB, NS])
            a_sb = sb1("a_sb", [P, IB, NS])

            x_in = sb1("x_in", [P, TT, D])
            st_in = sb1("st_in", [P, TT, 6])
            mv_in = sb1("mv_in", [P, TT, 2])
            nt_in = sb1("nt_in", [P, 8, TT])
            xn = sb1("xn", [P, TT, D])
            xnT = sb1("xnT", [P, KD, TC])
            xpad = [sb1(f"xpad{k}", [P, IB, TAPS - 1 + TC]) for k in range(2)]
            conv = sb1("conv", [P, IB, TC])
            u = [sb1(f"u{k}", [P, IB, TC]) for k in range(2)]
            zg = [sb1(f"zg{k}", [P, TT, DI]) for k in range(2)]
            bc = sb1("bc", [2 * NS, TC])
            c_tok = [sb1(f"c_tok{k}", [P, TT, 2 * NS]) for k in range(2)]
            dt_in = sb1("dt_in", [P, KD, TC])
            dt_log = conv
            dt = [sb1(f"dt{k}", [P, IB, TC]) for k in range(2)]
            du = [sb1(f"du{k}", [P, IB, TC]) for k in range(2)]
            bb = [sb1(f"bb{k}", [P, TC]) for k in range(NBB)]
            db = [sb1(f"db{k}", [P, IB, TC]) for k in range(2)]
            h = [sb1(f"h{k}", [P, IB, TC]) for k in range(2)]
            carry = sb1("carry", [P, 2, NS, IB])
            y = sb1("y", [P, TT, DI])
            scaled = sb1("scaled", [P, DI])
            yg = sb1("yg", [P, TT, DI])
            x_res = sb1("x_res", [P, TT, D])
            x1 = x_res
            st_mid = sb1("st_mid", [P, TT, 6])
            mv_mid = sb1("mv_mid", [P, TT, 2])
            nt_mid = sb1("nt_mid", [P, 8, TT])
            xhat = sb1("xhat", [P, TT, D])
            xhatT = sb1("xhatT", [P, KD, TC])
            logitT = sb1("logitT", [E, TC])

            da = [part1.enter_context(nc.psum_tensor(f"da{k}", [P, TC], F32)) for k in range(2)]
            hT = [part1.enter_context(nc.psum_tensor(f"hT{k}", [P, DI], F32)) for k in range(TT)]
            mm = [part1.enter_context(nc.psum_tensor(f"mm{k}", [P, TC], F32)) for k in range(2)]

            with nc.Block() as block:

                @block.sync
                def _(sp):
                    conv_rows = conv_w.rearrange("k a (i p) -> (k a i) p", p=P)
                    sp.dma_start(x_in[:], x_rows[0]).then_inc(x_loaded, 16)
                    for dst, src in (
                        (vec_rows[0:CONVB, :], conv_rows),
                        (vec_rows[CONVB:BDT, :], conv_b.rearrange("(i p) -> i p", p=P)),
                        (vec_rows[BDT:NW, :], b_dt.rearrange("(i p) -> i p", p=P)),
                        (vec_rows[NW:NVEC, :], norm_w.rearrange("(i p) -> i p", p=P)),
                        (b1_rows[:], b_fc1.rearrange("e (f p) -> (e f) p", p=P)),
                        (w_router_rows[:], w_router),
                        (b_router_sb[:], b_router.rearrange("(e a) -> e a", a=1)),
                        (a_raw[:], a_log.rearrange("(i p) s -> p i s", p=P)),
                    ):
                        sp.dma_start(dst, src).then_inc(consts_loaded, 16)
                    sp.dma_start(w_in_sb[:], w_in.rearrange("(k p) n -> p k n", p=P)).then_inc(w_in_loaded, 16)
                    for dst, src in (
                        (w_x_sb[:], w_x.rearrange("(k p) n -> p k n", p=P)),
                        (w_dt_sb[:], w_dt.rearrange("(k p) n -> p k n", p=P)),
                        (w_out_sb[:], w_out.rearrange("(k p) n -> p k n", p=P)),
                    ):
                        sp.dma_start(dst, src).then_inc(weights_loaded, 16)

                    def chunk(q, par, pair, units, post, pre):
                        prev, following = neighbours(q, par, pair)
                        a = q + 1
                        nxt = 1 - par
                        if pre and units:
                            wait(sp, xn_ready, a * TT)
                            sp.sem_inc(wait_held, 1)
                            sp.dma_start(x_in[:], x_rows[following]).then_inc(x_loaded, 16)
                        if post:
                            sp.wait_ge(x1_stored, q * 16)
                            sp.sem_inc(wait_held, 1)
                            sp.dma_start(x_res[:], x_rows[prev]).then_inc(xres_loaded, 16)
                        if units:
                            sp.wait_ge(b_stored, (q + 1) * 16)
                            sp.sem_inc(wait_held, 1)
                            for s in range(NS):
                                wait(sp, db_ready, q * NS + (s - NBB + 1))
                                sp.dma_start(bb[s % NBB][:], b_scratch[par, s:s + 1, :].partition_broadcast(P)
                                             ).then_inc(bb_loaded[s % NBB], 16)
                        if post:
                            store_rows(q, prev, pre)
                        if pre:
                            store_b(q, nxt, post)

                    def store_b(q, nxt, post):
                        evacuated(sp, q, post, True, "bc")
                        for k in range(NBB):
                            sp.sem_inc(wait_held, 1)
                            wait(sp, bb_loaded[k], q * ((NS // NBB) * 16))
                        sp.dma_start(b_scratch[nxt], bc[0:NS, :]).then_inc(b_stored, 16)

                    def store_rows(q, prev, pre):
                        sp.wait_ge(x1_ready, q)
                        sp.sem_inc(wait_held, 1)
                        sp.dma_start(out_rows[prev], x1[:]).then_inc(x1_stored, 16)
                        sp.wait_ge(xhat_ready, q * TT)
                        sp.sem_inc(wait_held, 1)
                        sp.dma_start(xhat_rows[prev], xhat[:]).then_inc(xhat_stored, 16)

                    for stored in (x1_stored, xhat_stored, logit_stored):
                        sp.sem_inc(stored, 16)
                    body(chunk)(sp)
                    for stored in (x1_stored, xhat_stored, logit_stored):
                        sp.wait_ge(stored, (CHUNKS + 1) * 16)
                    sp.wait_ge(weights_loaded, 3 * 16)

                @block.gpsimd
                def _(pool):
                    pool.memset(ident[:], 0.0).then_inc(ident_ready, 1)
                    for k in range(2):
                        pool.memset(xpad[k][:, :, 0:TAPS - 1], 0.0)
                    pool.memset(carry[:], 0.0).then_inc(carry_zeroed, 1)
                    pool.wait_ge(ident_ready, 1)
                    pool.affine_select(out=ident[:], in_=ident[:], compare_op=ALU.not_equal, fill=1.0,
                                       base=0, pattern=[[-1, P]], channel_multiplier=1).then_inc(ident_ready, 1)
                    pool.memset(same[:], 1.0).then_inc(route_ready, 1)
                    pool.memset(own[:], 1.0).then_inc(route_ready, 1)
                    pool.iota(iota_hb[:], pattern=[[1, HB]], base=0, channel_multiplier=0)
                    pool.iota(token[:], pattern=[[P, TT], [TC, NC]], base=0, channel_multiplier=1,
                              allow_small_or_imprecise_dtypes=True)
                    pool.wait_ge(route_ready, 2)
                    groups = same[:].rearrange("p (e c) -> p e c", c=NC)
                    pool.affine_select(out=groups, in_=groups, compare_op=ALU.is_ge, fill=0.0, base=0,
                                       pattern=[[-NC, E], [0, NC]], channel_multiplier=1).then_inc(route_ready, 1)
                    pool.affine_select(out=own[:], in_=own[:], compare_op=ALU.is_ge, fill=0.0, base=0,
                                       pattern=[[-HB, EH]], channel_multiplier=1).then_inc(route_ready, 1)
                    pool.wait_ge(route_ready, 4)
                    pool.affine_select(out=groups, in_=groups, compare_op=ALU.is_ge, fill=0.0, base=NC - 1,
                                       pattern=[[NC, E], [0, NC]], channel_multiplier=-1).then_inc(route_ready, 1)
                    pool.affine_select(out=own[:], in_=own[:], compare_op=ALU.is_ge, fill=0.0, base=HB - 1,
                                       pattern=[[HB, EH]], channel_multiplier=-1).then_inc(route_ready, 1)
                    pool.wait_ge(route_ready, 6)
                    pool.affine_select(out=before[:], in_=same[:], compare_op=ALU.is_ge, fill=0.0, base=-1,
                                       pattern=[[1, P]], channel_multiplier=-1).then_inc(route_ready, 1)
                    pool.wait_ge(carry_zeroed, 1)
                    pool.wait_ge(a_ready, 1)
                    pool.tensor_scalar(a_sb[:], a_exp[:], -1.0, None, ALU.mult).then_inc(a_ready, 1)

                    def chunk(q, par, pair, units, post, pre):
                        a = q + 1
                        nxt = 1 - par
                        for s in range(NS):
                            if units:
                                pool.wait_ge(bb_loaded[s % NBB], (q * (NS // NBB) + (s // NBB + 1)) * 16)
                                if s == 0:
                                    pool.wait_ge(du_ready, q * 2 + 2)
                                wait(pool, scan_done, q * (NS * IB) + (s - 2) * IB + IB)
                                pool.tensor_tensor(db[s % 2][:], du[par][:],
                                                   bb[s % NBB][:].unsqueeze(1).broadcast_to([P, IB, TC]),
                                                   ALU.mult).then_inc(db_ready, 1)
                            if pre and s == 5:
                                evacuated(pool, q, post, pre, "xi1")
                                for k in range(TAPS - 1):
                                    wait(pool, taps_shared, a * (TAPS - 1) + k)
                                    pool.wait_ge(taps_scaled, a * (TAPS - 1) + (k + 1))
                                    pool.tensor_tensor(conv[:, 1, :], conv[:, 1, :], yg[:, k, :], ALU.add
                                                       ).then_inc(taps_shared, 1)
                            if units and s - 2 in SHARED:
                                pool.wait_ge(last_scaled, q * len(SHARED) + shared_before(s - 1))
                                pool.wait_ge(last_added, q * NS + (s - 2))
                                pool.tensor_tensor(y[:, TT - 1, :], y[:, TT - 1, :], scaled[:], ALU.add
                                                   ).then_inc(last_added, 1)
                            if post and units and s == 9:
                                pool.wait_ge(xres_loaded, q * 16)
                                for t in range(TT):
                                    evacuated(pool, q, post, pre, f"out{t}")
                                pool.tensor_tensor(x1[:], xhat[:], x1[:], ALU.add).then_inc(x1_ready, 1)
                            if pre and s == 13:
                                pool.wait_ge(sp_ready, a * 2 + 2)
                                pool.tensor_tensor(dt[nxt][:, 2:4], dt_log[:, 2:4], dt[nxt][:, 2:4], ALU.add
                                                   ).then_inc(dt_shared, 1)
                            if pre and s in (14, 15):
                                pool.wait_ge(dt_ready, a + 1)
                                pool.wait_ge(dt_shared, a + 1)
                                half = slice((s - 14) * 2, (s - 14) * 2 + 2)
                                pool.tensor_tensor(du[nxt][:, half], dt[nxt][:, half], u[nxt][:, half],
                                                   ALU.mult).then_inc(du_ready, 1)

                    body(chunk)(pool)

                @block.scalar
                def _(act):
                    act.preload_act_table_set(LOG_SET)
                    act.wait_ge(consts_loaded, 8 * 16)
                    act.activation(a_exp[:], a_raw[:], ACT.Exp).then_inc(a_ready, 1)
                    act.wait_ge(vec_turned, 1)
                    act.activation(vecs[:, 0:NVEC], mm[0][:, 0:NVEC], ACT.Copy).then_inc(vec_ready, 1)
                    act.activation(b1_cols[:], mm[0][:, 128:256], ACT.Copy).then_inc(vec_ready, 1)
                    act.wait_ge(vec_ready, 2)
                    for k in range(KD):
                        act.activation(w_router_T[:, k, :], mm[0][:, 256 + k * E:256 + (k + 1) * E], ACT.Copy,
                                       scale=vecs[:, NW + k:NW + k + 1]).then_inc(vec_ready, 1)
                    act.wait_ge(a_ready, 2)

                    def chunk(q, par, pair, units, post, pre):
                        a = q + 1
                        p = q - 1
                        nxt = 1 - par
                        prev = neighbours(q, par, pair)[0]

                        for s in range(NS + 2):
                            if units and s < NS:
                                if s == 0:
                                    act.wait_ge(dt_ready, q + 1)
                                    act.wait_ge(dt_shared, q + 1)
                                decay(q, par, s, 0)
                                decay(q, par, s, 1)
                            if s >= 2:
                                for name in uses(s - 2, post, pre):
                                    evacuate(q, a, p, nxt, post, pre, name)
                            if pre and s == 2:
                                act.wait_ge(shift_in, a + 1)
                                for t in range(TT):
                                    act.activation(xn[:, t, :], x_in[:, t, :], ACT.Identity,
                                                   scale=nt_in[:, 6, t:t + 1], bias=nt_in[:, 7, t:t + 1]
                                                   ).then_inc(xn_ready, 1)
                            if s == 6 and (pre or units):
                                act.preload_act_table_set(SILU_SET)
                                if pre:
                                    act.wait_ge(taps_added, (a + 1) * (3 * (TAPS - 1)))
                                    act.wait_ge(taps_shared, (a + 1) * (TAPS - 1))
                                    act.activation(u[nxt][:], conv[:], ACT.Silu).then_inc(u_ready, 1)
                                if units:
                                    evacuated_before(act, q, post, pre)
                                    act.activation(zg[par][:], zg[par][:], ACT.Silu).then_inc(zg_ready, 1)
                                act.preload_act_table_set(LOG_SET)
                            if pre and s == 12:
                                act.wait_ge(sp_ready, a * 2 + 1)
                                act.activation(dt_log[:], dt_log[:], ACT.Ln, bias=1.0).then_inc(sp_ready, 1)
                            if pre and s == 4:
                                evacuated(act, q, post, pre, "xi1")
                                for k in range(TAPS - 1):
                                    act.activation(yg[:, k, :], xpad[nxt][:, 1, k:k + TC], ACT.Copy,
                                                   scale=vecs[:, k * IB + 1:k * IB + 2]).then_inc(taps_scaled, 1)
                            if units and s < NS:
                                decay(q, par, s, 2)
                                decay(q, par, s, 3)
                                if s == 0:
                                    wait(act, y_gated, q)
                                    for t in range(TT):
                                        act.wait_ge(ht_ready, q * ((NS + 1) * TT) + (t + 1))
                                        act.activation(y[:, t, :], hT[t][:], ACT.Copy).then_inc(y_started, 1)
                            if units and s - 1 in SHARED:
                                scale_last(q, par, s - 1)
                            if pre and s == 1:
                                act.wait_ge(nw_in, a * 5 + 1)
                                act.activation(nt_in[:, 1, :], nt_in[:, 0, :], ACT.Ln).then_inc(rs_in, 1)
                                act.wait_ge(rs_in, a * 2 + 1)
                                act.activation(nt_in[:, 2, :], nt_in[:, 1, :], ACT.Exp, scale=-0.5).then_inc(rs_in, 1)
                            if post and s == 10:
                                act.wait_ge(nw_mid, p * 5 + 1)
                                act.activation(nt_mid[:, 1, :], nt_mid[:, 0, :], ACT.Ln).then_inc(rs_mid, 1)
                                act.wait_ge(rs_mid, p * 2 + 1)
                                act.activation(nt_mid[:, 2, :], nt_mid[:, 1, :], ACT.Exp, scale=-0.5).then_inc(rs_mid, 1)
                            if post and s == 12:
                                act.wait_ge(shift_ready, p + 1)
                                for t in range(TT):
                                    act.activation(xhat[:, t, :], x1[:, t, :], ACT.Identity,
                                                   scale=nt_mid[:, 6, t:t + 1], bias=nt_mid[:, 7, t:t + 1]
                                                   ).then_inc(xhat_ready, 1)
                            if pre and s == 11:
                                for i in range(IB):
                                    evacuated(act, q, post, pre, f"dt{i}")
                                act.activation(dt_log[:], dt_log[:], ACT.Exp, scale=-1.0).then_inc(sp_ready, 1)
                        if post:
                            for name in ("rt0", "rt1"):
                                evacuated(act, q, post, pre, name)
                                act.sem_inc(wait_held, 1)
                            act.dma_start(logit_chunks[prev], logitT[:]).then_inc(logit_stored, 16)

                    def scale_last(q, par, s):
                        k = shared_before(s)
                        if k:
                            act.wait_ge(last_added, q * NS + SHARED[k - 1] + 1)
                        act.wait_ge(ht_ready, q * ((NS + 1) * TT) + (s + 2) * TT)
                        act.activation(scaled[:], hT[TT - 1][:], ACT.Copy,
                                       scale=c_tok[par][:, TT - 1, NS + s:NS + s + 1]).then_inc(last_scaled, 1)

                    def decay(q, par, s, i):
                        wait(act, scan_done, q * (NS * IB) + (s * IB + i - 1))
                        act.activation(da[i % 2][:], dt[par][:, i, :], ACT.Exp,
                                       scale=a_sb[:, i, s:s + 1]).then_inc(da_ready, 1)

                    def evacuate(q, a, p, nxt, post, pre, name):
                        kind, k = name.rstrip("0123456789"), int(name[-1]) if name[-1].isdigit() else 0
                        if name == "out0":
                            act.wait_ge(xhat_stored, q * 16)
                        if name == "xi0":
                            wait(act, tail_kept, a - 1)
                            wait(act, dt_ready, a)
                            wait(act, dt_shared, a)
                        if name == "rt0":
                            act.wait_ge(logit_stored, q * 16)
                        if name == "bc":
                            wait(act, b_stored, a * 16)
                        if name == "dt0":
                            act.wait_ge(u_ready, a + 1)
                        bank, free = mm_wait(act, q, post, pre, name)
                        if kind == "xi":
                            act.activation(conv[:, k, :], bank[:], ACT.Identity,
                                           scale=vecs[:, (TAPS - 1) * IB + k:(TAPS - 1) * IB + k + 1],
                                           bias=vecs[:, CONVB + k:CONVB + k + 1])
                        if kind == "dt":
                            act.activation(dt[nxt][:, k, :], bank[:], ACT.Relu, bias=vecs[:, BDT + k:BDT + k + 1])
                        dst, src, func, kw = {
                            "yT": (du[nxt][:, k, :], bank[:], ACT.Copy, {}),
                            "xnT": (xnT[:, k % KD, :], bank[:], ACT.Copy, {}),
                            "xhT": (xhatT[:, k % KD, :], bank[:], ACT.Copy, {}),
                            "out": (xhat[:, k % TT, :], bank[:, 0:D], ACT.Copy, {}),
                            "xi": (xpad[nxt][:, k, TAPS - 1:], bank[:], ACT.Copy, {}),
                            "z": (zg[nxt][:, k, :], bank[:], ACT.Copy, {}),
                            "bc": (bc[:], bank[0:2 * NS, :], ACT.Copy, {}),
                            "dti": (dt_in[:, k % KD, :], bank[:], ACT.Copy, {}),
                            "ct": (c_tok[nxt][:].rearrange("p t s -> p (t s)"), bank[:, 0:TT * 2 * NS], ACT.Copy, {}),
                            "dt": (dt_log[:, k, :], bank[:], ACT.Abs, {"bias": vecs[:, BDT + k:BDT + k + 1]}),
                            "rt": (logitT[:, (k % 2) * 256:(k % 2 + 1) * 256], bank[0:E, 0:256], ACT.Identity,
                                   {"bias": b_router_sb[:, 0:1]}),
                        }[kind]
                        act.activation(dst, src, func, **kw).then_inc(free, 1)

                    body(chunk)(act)

                @block.tensor
                def _(pe):
                    pe.wait_ge(ident_ready, 2)
                    pe.wait_ge(consts_loaded, 8 * 16)
                    pe.transpose(mm[0][:, 0:NVEC], vec_rows[0:NVEC, :], ident[0:NVEC, 0:NVEC])
                    pe.transpose(mm[0][:, 128:256], b1_rows[:], ident[:])
                    for k in range(KD):
                        last = pe.transpose(mm[0][:, 256 + k * E:256 + (k + 1) * E], w_router_rows[:, k * P:(k + 1) * P],
                                            ident[0:E, 0:E])
                    last.then_inc(vec_turned, 1)
                    pe.wait_ge(vec_ready, 2 + KD)

                    def chunk(q, par, pair, units, post, pre):
                        a = q + 1
                        p = q - 1
                        nxt = 1 - par

                        if units:
                            for t in range(TT):
                                if t < VT:
                                    wait(pe, y_added, q * (NS * VT) - (VT - 1 - t))
                                else:
                                    wait(pe, last_added, q * NS)
                                for i in range(IB):
                                    last = pe.transpose(hT[t][:, i * P:(i + 1) * P],
                                                        u[par][:, i, t * P:(t + 1) * P], ident[:])
                                last.then_inc(ht_ready, 1)
                        for s in range(NS):
                            names = uses(s, post, pre)
                            first, rest = (names[:len(names) // 2], names[len(names) // 2:]) if units else ([], names)
                            if units:
                                pe.wait_ge(scan_done, q * (NS * IB) + (s + 1) * IB)
                                for t in range(TT):
                                    if s == 0:
                                        pe.wait_ge(y_started, q * TT + (t + 1))
                                    elif t < VT:
                                        pe.wait_ge(y_added, q * (NS * VT) + ((s - 1) * VT + t + 1))
                                    elif s - 1 in SHARED:
                                        pe.wait_ge(last_scaled, q * len(SHARED) + shared_before(s))
                                    else:
                                        pe.wait_ge(last_added, q * NS + s)
                                    for i in range(IB):
                                        last = pe.transpose(hT[t][:, i * P:(i + 1) * P],
                                                            h[s % 2][:, i, t * P:(t + 1) * P], ident[:])
                                    last.then_inc(ht_ready, 1)
                                    if t == 1:
                                        for name in first:
                                            product(q, a, p, nxt, post, pre, name)
                            for name in rest:
                                product(q, a, p, nxt, post, pre, name)

                    def product(q, a, p, nxt, post, pre, name):
                        kind, k = name.rstrip("0123456789"), int(name[-1]) if name[-1].isdigit() else 0

                        def ready(*names):
                            for n in names:
                                evacuated(pe, q, post, pre, n)

                        if name == "yT0":
                            pe.wait_ge(y_gated, q)
                        if name == "xnT0":
                            pe.wait_ge(xn_ready, a * TT + TT)
                        if name == "xhT0":
                            pe.wait_ge(xhat_ready, p * TT + TT)
                        if name == "out0":
                            ready("yT2", "yT3")
                        if name == "xi0":
                            ready("xnT0", "xnT1")
                            if isinstance(q, int) and q < 0:
                                pe.wait_ge(w_in_loaded, 16)
                        if name == "rt0":
                            ready("xhT0", "xhT1")
                        if name == "dti0":
                            pe.wait_ge(u_ready, a + 1)
                            if isinstance(q, int) and q < 0:
                                pe.wait_ge(weights_loaded, 3 * 16)
                        if name == "ct":
                            ready("bc")
                        if name == "dt0":
                            ready("dti0", "dti1")
                        bank = mm_take(q, post, pre, name)
                        if kind == "ct":
                            pe.sem_inc(wait_held, 1)
                            for t in range(TT):
                                last = pe.transpose(bank[:, t * 2 * NS:(t + 1) * 2 * NS], bc[:, t * P:(t + 1) * P],
                                                    ident[0:2 * NS, 0:2 * NS])
                        elif kind in ("yT", "xnT", "xhT"):
                            src = {"yT": yg, "xnT": xn, "xhT": xhat}[kind]
                            for t in range(TT):
                                last = pe.transpose(bank[:, t * P:(t + 1) * P], src[:, t, k * P:(k + 1) * P], ident[:])
                        else:
                            tile = slice(k * P, (k + 1) * P)
                            dst, lhsT, rhs, n = {
                                "xi": (bank[:], lambda j: w_in_sb[:, j, tile], lambda j: xnT[:, j, :], KD),
                                "z": (bank[:], lambda j: xnT[:, j, tile], lambda j: w_in_sb[:, j, DI:2 * DI], KD),
                                "bc": (bank[0:2 * NS, :], lambda j: w_x_sb[:, j, D:D + 2 * NS],
                                       lambda j: u[nxt][:, j, :], IB),
                                "dti": (bank[:], lambda j: w_x_sb[:, j, tile], lambda j: u[nxt][:, j, :], IB),
                                "dt": (bank[:], lambda j: w_dt_sb[:, j, tile], lambda j: dt_in[:, j, :], KD),
                                "out": (bank[:, 0:D], lambda j: du[nxt][:, j, tile], lambda j: w_out_sb[:, j, :], IB),
                                "rt": (bank[0:E, 0:256], lambda j: w_router_T[:, j, :],
                                       lambda j: xhatT[:, j, k * 256:(k + 1) * 256], KD),
                            }[kind]
                            for j in range(n):
                                last = pe.matmul(dst, lhsT(j), rhs(j), start=(j == 0), stop=(j == n - 1))
                        last.then_inc(mm_full, 1)

                    body(chunk)(pe)

                @block.vector
                def _(dve):
                    dve.wait_ge(vec_ready, 2)
                    dve.wait_ge(carry_zeroed, 1)

                    def chunk(q, par, pair, units, post, pre):
                        a = q + 1
                        p = q - 1
                        nxt = 1 - par

                        def add_state(s, t):
                            if s == 0:
                                dve.wait_ge(y_started, q * TT + (t + 1))
                            else:
                                if t < VT:
                                    dve.wait_ge(y_added, q * (NS * VT) + ((s - 1) * VT + t + 1))
                                else:
                                    dve.wait_ge(last_added, q * NS + s)
                            dve.wait_ge(ht_ready, q * ((NS + 1) * TT) + ((s + 1) * TT + t + 1))
                            dve.scalar_tensor_tensor(out=y[:, t, :], in0=hT[t][:],
                                                     scalar=c_tok[par][:, t, NS + s:NS + s + 1], in1=y[:, t, :],
                                                     op0=ALU.mult, op1=ALU.add
                                                     ).then_inc(y_added if t < VT else last_added, 1)

                        def newton(nt, guessed, done, at, guesses):
                            dve.wait_ge(guessed, guesses)
                            dve.tensor_tensor(nt[:, 3, :], nt[:, 0, :], nt[:, 2, :], ALU.mult).then_inc(done, 1)
                            dve.wait_ge(done, at + 2)
                            dve.tensor_tensor(nt[:, 4, :], nt[:, 3, :], nt[:, 2, :], ALU.mult).then_inc(done, 1)
                            dve.wait_ge(done, at + 3)
                            dve.tensor_scalar(nt[:, 5, :], nt[:, 4, :], -0.5, 1.5, ALU.mult, ALU.add).then_inc(done, 1)
                            dve.wait_ge(done, at + 4)
                            dve.tensor_tensor(nt[:, 6, :], nt[:, 5, :], nt[:, 2, :], ALU.mult).then_inc(done, 1)
                            dve.wait_ge(done, at + 5)

                        def softplus():
                            dve.wait_ge(sp_ready, a * 2 + 2)
                            dve.tensor_tensor(dt[nxt][:, 0:2], dt_log[:, 0:2], dt[nxt][:, 0:2], ALU.add
                                              ).then_inc(dt_ready, 1)

                        def keep_carry(s):
                            dve.wait_ge(scan_done, q * (NS * IB) + (s + 1) * IB)
                            dve.tensor_copy(carry[:, par, s, :], h[s % 2][:, :, TC - 1]).then_inc(carry_kept, 1)

                        def adds_after(s, i):
                            if s == 0:
                                return ()
                            if s == 6:
                                return ((), (0, 1, 2, 3), (), ())[i]
                            return ((), (0,), (1,), (2, 3))[i]

                        def other_tap(tile, k):
                            before = k if tile == 0 else (TAPS - 1) + 2 * k + (tile - 3)
                            if k == 0:
                                evacuated(dve, q, post, pre, f"xi{tile}")
                            else:
                                dve.wait_ge(taps_added, a * (3 * (TAPS - 1)) + before)
                            dve.scalar_tensor_tensor(out=conv[:, tile, :], in0=xpad[nxt][:, tile, k:k + TC],
                                                     scalar=vecs[:, k * IB + tile:k * IB + tile + 1],
                                                     in1=conv[:, tile, :], op0=ALU.mult, op1=ALU.add
                                                     ).then_inc(taps_added, 1)

                        for s in range(NS):
                            if units:
                                dve.wait_ge(db_ready, q * NS + (s + 1))
                                if s >= 2:
                                    dve.wait_ge(ht_ready, q * ((NS + 1) * TT) + s * TT)
                                else:
                                    wait(dve, ht_ready, q * ((NS + 1) * TT) - (2 - s - 1) * TT)
                                wait(dve, carry_kept, q * NS + (s - 1))
                                for i in range(IB):
                                    dve.wait_ge(da_ready, q * (NS * IB) + (s * IB + i + 1))
                                    dve.tensor_tensor_scan(h[s % 2][:, i, :], da[i % 2][:], db[s % 2][:, i, :],
                                                           carry[:, par, s, i:i + 1], ALU.mult, ALU.add
                                                           ).then_inc(scan_done, 1)
                                    if s > 0 and i == 0:
                                        keep_carry(s - 1)
                                    for t in adds_after(s, i):
                                        if t < VT or s - 1 not in SHARED:
                                            add_state(s - 1, t)
                                    if pre and s in (4, 5) and i > 0:
                                        for tile in ((0,), (2, 3))[s - 4]:
                                            other_tap(tile, i - 1)
                                    if pre and s == 12 and i == IB - 1:
                                        softplus()
                            if pre and s == 0:
                                dve.wait_ge(x_loaded, (a + 1) * 16)
                                for t in range(TT):
                                    dve.bn_stats(st_in[:, t, :], x_in[:, t, :]).then_inc(stats_in, 1)
                                wait(dve, xn_ready, a * TT)
                                dve.wait_ge(stats_in, a * TT + TT)
                                dve.sem_inc(wait_held, 1)
                                for t in range(TT):
                                    dve.bn_aggr(mv_in[:, t, :], st_in[:, t, :]).then_inc(aggr_in, 1)
                                dve.wait_ge(aggr_in, a * TT + TT)
                                dve.tensor_scalar(nt_in[:, 0, :], mv_in[:, :, 1], EPS, None, ALU.add).then_inc(nw_in, 1)
                            if pre and s == 1:
                                newton(nt_in, rs_in, nw_in, a * 5, a * 2 + 2)
                                dve.scalar_tensor_tensor(out=nt_in[:, 7, :], in0=mv_in[:, :, 0], scalar=-1.0,
                                                         in1=nt_in[:, 6, :], op0=ALU.mult, op1=ALU.mult
                                                         ).then_inc(shift_in, 1)
                            if pre and s in (4, 5) and not units:
                                for k in range(TAPS - 1):
                                    for tile in ((0,), (2, 3))[s - 4]:
                                        other_tap(tile, k)
                            if pre and s == 12 and not units:
                                softplus()
                            if pre and s == 5:
                                dve.wait_ge(taps_added, (a + 1) * (3 * (TAPS - 1)))
                                dve.wait_ge(taps_shared, (a + 1) * (TAPS - 1))
                                dve.tensor_copy(xpad[nxt][:, :, 0:TAPS - 1], xpad[nxt][:, :, TC:TC + TAPS - 1]
                                                ).then_inc(tail_kept, 1)
                            if post and not units and s == 9:
                                dve.wait_ge(xres_loaded, q * 16)
                                for t in range(TT):
                                    evacuated(dve, q, post, pre, f"out{t}")
                                dve.tensor_tensor(x1[:], xhat[:], x1[:], ALU.add).then_inc(x1_ready, 1)
                            if post and s == 9:
                                dve.wait_ge(x1_ready, p + 1)
                                for t in range(TT):
                                    dve.bn_stats(st_mid[:, t, :], x1[:, t, :]).then_inc(stats_mid, 1)
                                dve.wait_ge(stats_mid, p * TT + TT)
                                dve.sem_inc(wait_held, 1)
                                for t in range(TT):
                                    dve.bn_aggr(mv_mid[:, t, :], st_mid[:, t, :]).then_inc(aggr_mid, 1)
                                dve.wait_ge(aggr_mid, p * TT + TT)
                                dve.tensor_scalar(nt_mid[:, 0, :], mv_mid[:, :, 1], 1.0 + EPS, EPS * EPS, ALU.mult,
                                                  ALU.add).then_inc(nw_mid, 1)
                            if post and s == 10:
                                newton(nt_mid, rs_mid, nw_mid, p * 5, p * 2 + 2)
                                dve.scalar_tensor_tensor(out=nt_mid[:, 7, :], in0=mv_mid[:, :, 0], scalar=-1.0,
                                                         in1=nt_mid[:, 6, :], op0=ALU.mult, op1=ALU.mult
                                                         ).then_inc(shift_ready, 1)
                        if units:
                            keep_carry(NS - 1)
                            for t in range(TT):
                                add_state(NS - 1, t)
                            dve.wait_ge(y_added, (q + 1) * (NS * VT))
                            dve.wait_ge(last_added, (q + 1) * NS)
                            dve.wait_ge(zg_ready, q + 1)
                            dve.tensor_tensor(yg[:], y[:], zg[par][:], ALU.mult).then_inc(y_gated, 1)

                    body(chunk)(dve)

        idx_all = sb("idx_all", [P, E * CH], I32)
        wt_all = sb("wt_all", [P, E * CH])
        w1 = [sb(f"w1_{k}", [P, KF, D]) for k in range(2)]
        w2 = [sb(f"w2_{k}", [P, KD, F]) for k in range(2)]
        b2_all = sb("b2_all", [P, E, D])
        b2_loaded = sem("b2_loaded")
        w_loaded = [sem(f"w_loaded{k}") for k in range(2)]
        w_fc1_rows = w_fc1.rearrange("e (f p) d -> e p f d", p=P)
        w_fc2_rows = w_fc2.rearrange("e (k p) f -> e p k f", p=P)

        def load_weights(sp, e, par):
            sp.dma_start(w1[par][:], w_fc1_rows[e]).then_inc(w_loaded[par], 16)
            sp.dma_start(w2[par][:], w_fc2_rows[e]).then_inc(w_loaded[par], 16)

        with ExitStack() as part2:
            def sb2(name, shape, dt=F32):
                return part2.enter_context(nc.sbuf_tensor(name, shape, dt))

            BIG = 8192.0
            QUARTERINGS = 12
            CUTS = 3
            STEPS = CUTS + 4

            zero = sb2("zero", [P, TC])
            lt = sb2("lt", [P, TC])
            work = sb2("work", [P, TC])
            r_own = sb2("r_own", [P, 1])
            r_all = sb2("r_all", [P, 1])
            lo = sb2("lo", [P, 1])
            cuts = sb2("cuts", [P, CUTS])
            ahead = [sb2(f"ahead{k}", [P, CUTS]) for k in range(2)]
            count = sb2("count", [P, CUTS])
            enough = sb2("enough", [P, CUTS])
            hits = sb2("hits", [P, 1])
            hi = sb2("hi", [P, 1])
            above = sb2("above", [P, TC])
            band = sb2("band", [P, TC])
            c_above = sb2("c_above", [P, TC])
            c_band = sb2("c_band", [P, TC])
            totals = sb2("totals", [P, 2])
            offs = sb2("offs", [P, 5])
            slot = sb2("slot", [P, TC])
            lg = sb2("lg", [P, TC])
            mask = sb2("mask", [P, TC])
            slot_i = sb2("slot_i", [P, TC], I32)
            slot_hi = sb2("slot_hi", [P, TC], I32)
            slot_lo = sb2("slot_lo", [P, TC], I32)
            ex = sb2("ex", [P, TC])
            wts = sb2("wts", [P, TC])
            best = sb2("best", [P, 4, TT * NC])
            hot_hi = [sb2(f"hot_hi{k}", [P, NC, E, HB]) for k in range(2)]
            hot_lo = [sb2(f"hot_lo{k}", [P, NC, E, HB]) for k in range(2)]
            values = [sb2(f"values{k}", [P, 2, NC, E, HB]) for k in range(2)]
            diag = [sb2(f"diag{k}", [P, 2, HB, EH]) for k in range(GROUPS)]
            listed = sb2("listed", [P, GROUPS, 2, HB])
            list_rows = sb2("list_rows", [2 * E * CH, P])

            zero_ready = sem("zero_ready")
            lt_loaded = sem("lt_loaded")
            r_ready = sem("r_ready")
            bis = sem("bis")
            counted = sem("counted")
            lg_turned = sem("lg_turned")
            ranked = sem("ranked")
            totalled = sem("totalled")
            slot_turned = sem("slot_turned")
            wt_step = sem("wt_step")
            wt_exp = sem("wt_exp")
            hot_ready = sem("hot_ready")
            tok_ready = sem("tok_ready")
            wv_ready = sem("wv_ready")
            scanned = sem("scanned")
            lists_kept = sem("lists_kept")
            lists_done = sem("lists_done")
            lists_read = sem("lists_read")
            lists_stored = sem("lists_stored")
            lists_loaded = sem("lists_loaded")
            lists_turned = sem("lists_turned")

            with ExitStack() as banks:
                ps_count = banks.enter_context(nc.psum_tensor("ps_count", [P, TC], F32))
                ps_lg = banks.enter_context(nc.psum_tensor("ps_lg", [P, TC], F32))
                ps_slot = banks.enter_context(nc.psum_tensor("ps_slot", [P, TC], F32))
                ps_list = [banks.enter_context(nc.psum_tensor(f"ps_list{k}", [P, TC], F32)) for k in range(GROUPS)]
                ps_turn = banks.enter_context(nc.psum_tensor("ps_turn", [P, TC], F32))
                by_jec = ps_lg[:].rearrange("p (j e c) -> p j c e", e=E, c=NC)

                with nc.Block() as block:

                    @block.sync
                    def _(sp):
                        sp.dma_start(lt[:], logit_dram.rearrange("e (c t) -> (e c) t", t=TC)).then_inc(lt_loaded, 16)
                        load_weights(sp, 0, 0)
                        load_weights(sp, 1, 1)
                        sp.dma_start(b2_all[:], b_fc2.rearrange("(a e) d -> a e d", a=1).partition_broadcast(P)
                                     ).then_inc(b2_loaded, 16)
                        sp.wait_ge(lists_read, GROUPS)
                        for v in range(2):
                            sp.dma_start(list_dram[v].rearrange("r (a b) -> (r a) b", b=HB).rearrange(
                                "(g p) b -> p g b", p=P), listed[:, :, v, :]).then_inc(lists_stored, 16)
                        sp.wait_ge(lists_stored, 32)
                        sp.dma_start(list_rows[:], list_dram.rearrange("v r s -> (v r) s")).then_inc(lists_loaded, 16)

                    @block.gpsimd
                    def _(pool):
                        pool.memset(zero[:], 0.0).then_inc(zero_ready, 1)
                        pool.wait_ge(r_ready, 1)
                        pool.partition_all_reduce(r_all[:], r_own[:], P, bass.bass_isa.ReduceOp.max).then_inc(r_ready, 1)
                        for j in range(TT):
                            if j >= 2:
                                pool.wait_ge(lists_done, j - 1)
                            pool.wait_ge(hot_ready, 2 * j + 2)
                            pool.tensor_tensor(values[j % 2][:, 0, :, :, :].rearrange("p c e b -> p c (e b)"),
                                               hot_lo[j % 2][:].rearrange("p c e b -> p c (e b)"),
                                               token[:, j, :].unsqueeze(2).broadcast_to([P, NC, E * HB]),
                                               ALU.mult).then_inc(tok_ready, 1)

                    @block.scalar
                    def _(act):
                        act.wait_ge(wt_step, 6)
                        act.activation(ex[:], ex[:], ACT.Exp).then_inc(wt_exp, 1)
                        act.activation(best[:, 2, :], best[:, 2, :], ACT.Exp).then_inc(wt_exp, 1)

                    @block.tensor
                    def _(pe):
                        pe.wait_ge(lt_loaded, 16)
                        for j in range(TT):
                            last = pe.transpose(ps_lg[:, j * P:(j + 1) * P], lt[:, j * P:(j + 1) * P], ident[:])
                        last.then_inc(lg_turned, 1)
                        pe.wait_ge(route_ready, 7)

                        def count_experts(it, k):
                            pe.wait_ge(bis, it * (2 * STEPS) + (k * STEPS + CUTS))
                            pe.matmul(ps_count[:, 0:CUTS], same[:], count[:], start=True, stop=True
                                      ).then_inc(counted, 1)

                        with pe.Fori(0, QUARTERINGS // 2) as it:
                            count_experts(it, 0)
                            count_experts(it, 1)
                        pe.wait_ge(bis, QUARTERINGS * STEPS + 2 + CUTS)
                        pe.matmul(ps_count[:, 0:CUTS], same[:], count[:], start=True, stop=True).then_inc(counted, 1)
                        pe.wait_ge(ranked, 6)
                        pe.matmul(ps_count[:, 4:6], before[:], totals[:], start=True, stop=True)
                        pe.matmul(ps_count[:, 6:7], same[:], totals[:, 0:1], start=True, stop=True).then_inc(totalled, 1)
                        pe.wait_ge(ranked, 12)
                        for j in range(TT):
                            last = pe.transpose(ps_slot[:, j * P:(j + 1) * P], slot[:, j * P:(j + 1) * P], ident[:])
                        last.then_inc(slot_turned, 1)
                        for j in range(TT):
                            pe.wait_ge(hot_ready, 2 * j + 2)
                            pe.wait_ge(tok_ready, j + 1)
                            pe.wait_ge(wv_ready, j + 1)
                            for c in range(NC):
                                for g in range(GROUPS):
                                    e = slice(g * EH, (g + 1) * EH)
                                    last = pe.matmul(
                                        ps_list[g][:, 0:2 * EH * HB],
                                        hot_hi[j % 2][:, c, e, :].rearrange("p e a -> p (e a)"),
                                        values[j % 2][:, :, c, e, :].rearrange("p v e b -> p v (e b)"),
                                        start=(j == 0 and c == 0), stop=(j == TT - 1 and c == NC - 1))
                            last.then_inc(lists_done, 1)
                        pe.wait_ge(lists_loaded, 16)
                        pe.transpose(ps_turn[:, 0:2 * E * CH], list_rows[:], ident[0:2 * E * CH, 0:2 * E * CH]
                                     ).then_inc(lists_turned, 1)

                    @block.vector
                    def _(dve):
                        dve.wait_ge(lt_loaded, 16)
                        dve.tensor_reduce(r_own[:], lt[:], AX.X, ALU.max, apply_absolute_value=True).then_inc(r_ready, 1)
                        dve.wait_ge(r_ready, 2)
                        dve.tensor_scalar(r_own[:].bitcast(I32), r_all[:].bitcast(I32), 0x7F800000, None,
                                          ALU.bitwise_and).then_inc(r_ready, 1)
                        dve.wait_ge(r_ready, 3)
                        dve.tensor_scalar(lo[:], r_own[:], -2.0, None, ALU.mult).then_inc(r_ready, 1)
                        for k in range(CUTS):
                            dve.tensor_scalar(ahead[0][:, k:k + 1], r_own[:], k + 1.0, None, ALU.mult).then_inc(r_ready, 1)
                        dve.wait_ge(r_ready, 4 + CUTS)
                        dve.tensor_scalar(cuts[:], ahead[0][:], lo[:, 0:1], None, ALU.add).then_inc(r_ready, 1)
                        dve.wait_ge(route_ready, 7)
                        dve.wait_ge(r_ready, 5 + CUTS)
                        def jec(tile):
                            return tile[:].rearrange("p (j e c) -> p j e c", e=E, c=NC)

                        def over_e(k):
                            return best[:, k, :].rearrange("p (j c) -> p j c", c=NC).unsqueeze(2).broadcast_to(
                                [P, TT, E, NC])

                        def row(k):
                            return best[:, k, :].rearrange("p (j c) -> p j c", c=NC)

                        dve.wait_ge(lg_turned, 1)
                        dve.tensor_reduce(row(0), by_jec, AX.X, ALU.max).then_inc(wt_step, 1)

                        def count_cuts():
                            for k, dump in enumerate((work, above, band)):
                                dve.tensor_scalar(dump[:], lt[:], cuts[:, k:k + 1], 0.0, ALU.is_ge, ALU.add,
                                                  accum_out=count[:, k:k + 1]).then_inc(bis, 1)

                        def move_lo(ahead_now, before, count_no):
                            dve.wait_ge(counted, count_no)
                            dve.tensor_scalar(enough[:], ps_count[:, 0:CUTS], float(CAP), 0.0, ALU.is_ge, ALU.add,
                                              accum_out=hits[:]).then_inc(bis, 1)
                            dve.wait_ge(bis, before + 1)
                            dve.scalar_tensor_tensor(out=lo[:], in0=hits[:], scalar=ahead_now[:, 0:1], in1=lo[:],
                                                     op0=ALU.mult, op1=ALU.add).then_inc(bis, 1)
                            dve.wait_ge(bis, before + 2)

                        def quarter(it, k):
                            at = k * STEPS
                            count_cuts()
                            dve.tensor_scalar(ahead[1 - k][:], ahead[k][:], 0.25, None, ALU.mult).then_inc(bis, 1)
                            move_lo(ahead[k], it * (2 * STEPS) + (at + CUTS + 1), it * 2 + (k + 1))
                            dve.tensor_scalar(cuts[:], ahead[1 - k][:], lo[:, 0:1], None, ALU.add).then_inc(bis, 1)
                            dve.wait_ge(bis, it * (2 * STEPS) + (at + STEPS))

                        with dve.Fori(0, QUARTERINGS // 2) as it:
                            quarter(it, 0)
                            quarter(it, 1)
                        done = QUARTERINGS * STEPS
                        dve.tensor_scalar(ahead[1][:], ahead[0][:], 2.0, None, ALU.mult).then_inc(bis, 1)
                        dve.wait_ge(bis, done + 1)
                        dve.tensor_scalar(cuts[:], ahead[1][:], lo[:, 0:1], None, ALU.add).then_inc(bis, 1)
                        dve.wait_ge(bis, done + 2)
                        count_cuts()
                        move_lo(ahead[1], done + 2 + CUTS, QUARTERINGS + 1)
                        dve.tensor_tensor(hi[:], lo[:], ahead[1][:, 0:1], ALU.add).then_inc(ranked, 2)
                        dve.wait_ge(ranked, 2)
                        dve.tensor_scalar(above[:], lt[:], hi[:, 0:1], None, ALU.is_ge).then_inc(ranked, 1)
                        dve.wait_ge(ranked, 3)
                        dve.scalar_tensor_tensor(out=band[:], in0=lt[:], scalar=lo[:, 0:1], in1=above[:],
                                                 op0=ALU.is_ge, op1=ALU.subtract).then_inc(ranked, 1)
                        dve.wait_ge(zero_ready, 1)
                        dve.tensor_tensor_scan(c_above[:], above[:], zero[:], 0.0, ALU.add, ALU.add).then_inc(scanned, 1)
                        dve.wait_ge(ranked, 4)
                        dve.tensor_tensor_scan(c_band[:], band[:], zero[:], 0.0, ALU.add, ALU.add).then_inc(scanned, 1)
                        dve.wait_ge(scanned, 2)
                        dve.tensor_copy(totals[:, 0:1], c_above[:, TC - 1:TC]).then_inc(ranked, 1)
                        dve.tensor_copy(totals[:, 1:2], c_band[:, TC - 1:TC]).then_inc(ranked, 1)
                        dve.wait_ge(totalled, 1)
                        dve.tensor_copy(offs[:, 0:3], ps_count[:, 4:7]).then_inc(ranked, 1)
                        dve.wait_ge(ranked, 7)
                        dve.tensor_scalar(offs[:, 3:4], offs[:, 1:2], offs[:, 2:3], -1.0 - BIG, ALU.add, ALU.add
                                          ).then_inc(ranked, 1)
                        dve.tensor_scalar(offs[:, 4:5], offs[:, 0:1], -1.0 - BIG, None, ALU.add).then_inc(ranked, 1)
                        dve.wait_ge(ranked, 9)
                        dve.scalar_tensor_tensor(out=c_above[:], in0=c_above[:], scalar=offs[:, 4:5], in1=above[:],
                                                 op0=ALU.add, op1=ALU.mult).then_inc(ranked, 1)
                        dve.scalar_tensor_tensor(out=c_band[:], in0=c_band[:], scalar=offs[:, 3:4], in1=band[:],
                                                 op0=ALU.add, op1=ALU.mult).then_inc(ranked, 1)
                        dve.wait_ge(ranked, 11)
                        dve.scalar_tensor_tensor(out=slot[:], in0=c_above[:], scalar=BIG, in1=c_band[:],
                                                 op0=ALU.add, op1=ALU.add).then_inc(ranked, 1)
                        dve.wait_ge(slot_turned, 1)
                        dve.tensor_copy(slot_i[:], ps_slot[:]).then_inc(ranked, 1)
                        dve.tensor_scalar(mask[:], ps_slot[:], float(CAP), None, ALU.is_lt).then_inc(ranked, 1)
                        dve.wait_ge(ranked, 13)
                        dve.tensor_scalar(slot_hi[:], slot_i[:], 4, None, ALU.arith_shift_right).then_inc(ranked, 1)
                        dve.tensor_scalar(slot_lo[:], slot_i[:], HB - 1, None, ALU.bitwise_and).then_inc(ranked, 1)

                        dve.wait_ge(ranked, 14)
                        dve.tensor_scalar(work[:], mask[:], -1.0, 1e30, ALU.add, ALU.mult).then_inc(wt_step, 1)
                        dve.wait_ge(wt_step, 2)
                        dve.tensor_tensor(lg[:], ps_lg[:], work[:], ALU.add).then_inc(wt_step, 1)
                        dve.wait_ge(wt_step, 3)
                        dve.tensor_reduce(row(1), lg[:].rearrange("p (j e c) -> p j c e", e=E, c=NC), AX.X, ALU.max
                                          ).then_inc(wt_step, 1)
                        dve.wait_ge(wt_step, 4)
                        dve.tensor_tensor(best[:, 2, :], best[:, 1, :], best[:, 0, :], ALU.subtract).then_inc(wt_step, 1)
                        dve.tensor_tensor(jec(ex), jec(lg), over_e(1), ALU.subtract).then_inc(wt_step, 1)

                        def hot(j):
                            if j >= 2:
                                dve.wait_ge(lists_done, j - 1)
                            for dst, part in ((hot_hi, slot_hi), (hot_lo, slot_lo)):
                                dve.tensor_tensor(
                                    dst[j % 2][:],
                                    part[:, j * P:(j + 1) * P].rearrange("p (e c) -> p c e", c=NC).unsqueeze(3
                                                                         ).broadcast_to([P, NC, E, HB]),
                                    iota_hb[:].unsqueeze(1).unsqueeze(1).broadcast_to([P, NC, E, HB]),
                                    ALU.is_equal).then_inc(hot_ready, 1)

                        def weights_by_low(j):
                            dve.wait_ge(hot_ready, 2 * j + 2)
                            dve.tensor_tensor(
                                values[j % 2][:, 1], hot_lo[j % 2][:],
                                wts[:, j * P:(j + 1) * P].rearrange("p (e c) -> p c e", c=NC).unsqueeze(3
                                                                    ).broadcast_to([P, NC, E, HB]),
                                ALU.mult).then_inc(wv_ready, 1)

                        dve.wait_ge(ranked, 16)
                        hot(0)
                        dve.wait_ge(wt_exp, 2)
                        dve.tensor_reduce(row(3), ex[:].rearrange("p (j e c) -> p j c e", e=E, c=NC), AX.X, ALU.add
                                          ).then_inc(wt_step, 1)
                        dve.wait_ge(wt_step, 7)
                        dve.reciprocal(best[:, 3, :], best[:, 3, :]).then_inc(wt_step, 1)
                        dve.wait_ge(wt_step, 8)
                        dve.scalar_tensor_tensor(out=best[:, 3, :], in0=best[:, 2, :], scalar=0.0, in1=best[:, 3, :],
                                                 op0=ALU.is_gt, op1=ALU.mult).then_inc(wt_step, 1)
                        dve.wait_ge(wt_step, 9)
                        dve.tensor_tensor(jec(wts), jec(ex), over_e(3), ALU.mult).then_inc(wt_step, 1)
                        dve.wait_ge(wt_step, 10)
                        weights_by_low(0)
                        for j in range(1, TT):
                            hot(j)
                            weights_by_low(j)
                        dve.wait_ge(lists_done, TT)
                        for g in range(GROUPS):
                            dve.tensor_tensor(diag[g][:],
                                              ps_list[g][:, 0:2 * EH * HB].rearrange("p (v e b) -> p v b e", e=EH, b=HB),
                                              own[:].unsqueeze(1).unsqueeze(1).broadcast_to([P, 2, HB, EH]),
                                              ALU.mult).then_inc(lists_kept, 1)
                        for g in range(GROUPS):
                            dve.wait_ge(lists_kept, g + 1)
                            dve.tensor_reduce(listed[:, g], diag[g][:], AX.X, ALU.add).then_inc(lists_read, 1)
                        dve.wait_ge(lists_turned, 1)
                        dve.tensor_copy(idx_all[:], ps_turn[:, 0:E * CH])
                        dve.tensor_copy(wt_all[:], ps_turn[:, E * CH:2 * E * CH])

        with ExitStack() as part3:
            def sb3(name, shape, dt=F32):
                return part3.enter_context(nc.sbuf_tensor(name, shape, dt))

            def psum3(name):
                return part3.enter_context(nc.psum_tensor(name, [P, 512], F32))

            def parts(name, shape):
                return [sb3(f"{name}_{part}", shape, BF16) for part in ("hi", "lo")]

            w1T = [parts(f"w1T{k}", [P, KD, F]) for k in range(2)]
            w2T = [parts(f"w2T{k}", [P, KF, D]) for k in range(2)]
            xe = [[sb3(f"xe{k}_{half}", [P, D]) for half in range(CH)] for k in range(2)]
            xeT = [parts(f"xeT{k}", [P, KD, CAP]) for k in range(2)]
            hid = sb3("hid", [P, KF, CAP])
            hid_parts = parts("hid", [P, KF, CAP])
            ye = [sb3(f"ye{half}", [P, D]) for half in range(CH)]
            gather_idx = [sb3(f"gather_idx{k}", [P, CH], I32) for k in range(2)]
            scatter_idx = sb3("scatter_idx", [P, CH], I32)
            wt_e = sb3("wt_e", [P, CH])
            b1_e = [sb3(f"b1_e{k}", [P, KF]) for k in range(2)]

            hb = [psum3(f"hb{k}") for k in range(KF // 2)]
            yb = psum3("yb")
            TURNS = 3
            turn = [psum3(f"turn{k}") for k in range(TURNS)]
            USES = [("w1", k) for k in range(4)] + [("w2", k) for k in range(4)] + [("x", 0)]
            NU = len(USES)
            BETWEEN = [[0], [1, 2], [3], [4]]
            AFTER = [5, 6, 7, 8]
            EVERY = 3
            assert NU % TURNS == 0

            xe_loaded = [sem(f"xe_loaded{k}") for k in range(2)]
            gidx_ready = sem("gidx_ready")
            b1_ready = sem("b1_ready")
            turn_full = sem("turn_full")
            turn_free = [sem(f"turn_free{k}") for k in range(TURNS)]
            hi_ready = sem("hi_ready")
            hid_hi = sem("hid_hi")
            hid_lo = sem("hid_lo")
            h_full = sem("h_full")
            gelu_done = sem("gelu_done")
            y_full = sem("y_full")
            y_cols = sem("y_cols")
            y_biased = sem("y_biased")
            y_ready = sem("y_ready")
            scattered = sem("scattered")

            def span(e, n):
                return slice(e * n, (e + 1) * n) if isinstance(e, int) else bass.ds(e * n, n)

            def experts(first, expert):
                with_next = dict(turn_next=True, fetch_next=True)

                def run(eng):
                    first()
                    expert(0, 0, **with_next)
                    with eng.Fori(0, (E - 4) // 2) as pair:
                        expert(pair * 2 + 1, 1, loads=pair + 2, **with_next)
                        expert(pair * 2 + 2, 0, loads=pair + 2, **with_next)
                    expert(E - 3, 1, **with_next)
                    expert(E - 2, 0, turn_next=True, fetch_next=False)
                    expert(E - 1, 1, turn_next=False, fetch_next=False)
                return run

            with nc.Block() as block:

                @block.sync
                def _(sp):
                    def expert(e, par, turn_next, fetch_next, loads=None):
                        if fetch_next:
                            sp.wait_ge(turn_full, (e + 1) * NU)
                            sp.sem_inc(wait_held, 1)
                            load_weights(sp, e + 2, par)

                    experts(lambda: None, expert)(sp)
                    sp.wait_ge(b2_loaded, 16)
                    sp.wait_ge(scattered, E * CH * 16)

                @block.gpsimd
                def _(pool):
                    def gather(e, par):
                        pool.wait_ge(gidx_ready, e + 1)
                        if not isinstance(e, int):
                            pool.sem_inc(wait_held, 1)
                        for half in range(CH):
                            pool.indirect_dma_start(
                                out=xe[par][half][:], out_offset=None, in_=xhat_dram,
                                in_offset=bass.IndirectOffsetOnAxis(ap=gather_idx[par][:, half:half + 1], axis=0)
                            ).then_inc(xe_loaded[par], 16)

                    def first():
                        gather(0, 0)
                        gather(1, 1)

                    def expert(e, par, turn_next, fetch_next, loads=None):
                        if fetch_next:
                            pool.wait_ge(turn_full, e * NU + NU)
                            gather(e + 2, par)
                        pool.wait_ge(y_ready, e * CH + CH)
                        wait(pool, scattered, e * (CH * 16))
                        pool.sem_inc(wait_held, 1)
                        for half in range(CH):
                            pool.indirect_dma_start(
                                out=out_flat, out_offset=bass.IndirectOffsetOnAxis(
                                    ap=scatter_idx[:, half:half + 1], axis=0),
                                in_=ye[half][:], in_offset=None, compute_op=ALU.add
                            ).then_inc(scattered, 16)

                    experts(first, expert)(pool)

                def target(n, par):
                    kind, k = USES[n]
                    if kind == "x":
                        return [part[:].rearrange("p k s -> p (k s)") for part in xeT[par]], None
                    if kind == "w1":
                        cols = slice(k % 2 * 512, (k % 2 + 1) * 512)
                        return [part[:, k // 2, cols] for part in w1T[par]], vecs[:, NW + k // 2:NW + k // 2 + 1]
                    return [part[:, 2 * k:2 * k + 2, :].rearrange("p f d -> p (f d)") for part in w2T[par]], None

                def turned_hi(act, e, par, n):
                    (high, _), scale = target(n, par)
                    act.wait_ge(turn_full, e * NU + (n + 1))
                    act.activation(high, turn[n % TURNS][:], ACT.Copy, scale=1.0 if scale is None else scale
                                   ).then_inc(hi_ready, 1)

                def turned_lo(dve, e, par, n):
                    (high, low), scale = target(n, par)
                    dve.wait_ge(hi_ready, e * NU + (n + 1))
                    bank = turn[n % TURNS]
                    if scale is None:
                        done = dve.tensor_tensor(low, bank[:], high, ALU.subtract)
                    else:
                        done = dve.scalar_tensor_tensor(out=low, in0=bank[:], scalar=scale, in1=high,
                                                        op0=ALU.mult, op1=ALU.subtract)
                    done.then_inc(turn_free[n % TURNS], 1)

                @block.scalar
                def _(act):
                    act.preload_act_table_set("gelu_and_others")

                    def first():
                        for n in range(NU):
                            turned_hi(act, 0, 0, n)

                    def expert(e, par, turn_next, fetch_next, loads=None):
                        act.wait_ge(b1_ready, e + 1)
                        for k in range(KF // 2):
                            act.wait_ge(h_full, e * (KF // 2) + (k + 1))
                            for f in (2 * k, 2 * k + 1):
                                act.activation(hid[:, f, :], hb[k][:, f % 2 * CAP:(f % 2 + 1) * CAP], ACT.Gelu,
                                               bias=b1_e[par][:, f:f + 1]).then_inc(gelu_done, 1)
                            act.wait_ge(gelu_done, e * KF + (2 * k + 2))
                            act.activation(hid_parts[0][:, 2 * k:2 * k + 2, :], hid[:, 2 * k:2 * k + 2, :], ACT.Copy
                                           ).then_inc(hid_hi, 1)
                            if turn_next:
                                for n in BETWEEN[k]:
                                    turned_hi(act, e + 1, 1 - par, n)
                        if turn_next:
                            for n in AFTER:
                                turned_hi(act, e + 1, 1 - par, n)

                    experts(first, expert)(act)

                @block.tensor
                def _(pe):
                    def turn_use(e, par, loads, n):
                        kind, k = USES[n]
                        if kind == "x":
                            pe.wait_ge(xe_loaded[par], loads * (CH * 16))
                            pe.sem_inc(wait_held, 1)
                        if kind == "w1" and k == 0:
                            pe.wait_ge(w_loaded[par], loads * 32)
                            pe.sem_inc(wait_held, 1)
                        bank = turn[n % TURNS]
                        before = e * (NU // TURNS) + n // TURNS
                        wait(pe, turn_free[n % TURNS], before)
                        pe.sem_inc(wait_held, 1)
                        for i in range(4):
                            if kind == "x":
                                src = xe[par][i % 2][:, i // 2 * P:(i // 2 + 1) * P]
                            elif kind == "w1":
                                src = w1[par][:, k % 2 * 4 + i, k // 2 * P:(k // 2 + 1) * P]
                            else:
                                f = 2 * k + i // 2
                                src = w2[par][:, i % 2, f * P:(f + 1) * P]
                            last = pe.transpose(bank[:, i * P:(i + 1) * P], src, ident[:])
                        last.then_inc(turn_full, 1)

                    def product3(out, a, b, cols_a, cols_b, start, stop):
                        for i, (x, y) in enumerate(((0, 0), (0, 1), (1, 0))):
                            last = pe.matmul(out, cols_a(a[x]), cols_b(b[y]), start=start and i == 0, stop=stop and i == 2)
                        return last

                    def first():
                        for n in range(NU):
                            turn_use(0, 0, 1, n)

                    def expert(e, par, turn_next, fetch_next, loads=None):
                        if isinstance(e, int):
                            loads = (e + 1) // 2 + 1

                        def turn_next_use(n):
                            if turn_next:
                                turn_use(e + 1, 1 - par, loads, n)

                        for k in range(TURNS):
                            pe.wait_ge(turn_free[k], (e + 1) * (NU // TURNS))
                        for f in range(KF):
                            for k in range(KD):
                                last = product3(hb[f // 2][:, f % 2 * CAP:(f % 2 + 1) * CAP], w1T[par], xeT[par],
                                                lambda part: part[:, k, f * P:(f + 1) * P], lambda part: part[:, k, :],
                                                k == 0, k == KD - 1)
                            if f % 2:
                                last.then_inc(h_full, 1)
                                for n in BETWEEN[f // 2]:
                                    turn_next_use(n)
                        wait(pe, y_biased, e * CH)
                        after = list(AFTER)
                        for half in range(CH):
                            for f in range(KF):
                                if half == 0 and f % 2 == 0:
                                    pe.wait_ge(hid_lo, e * (KF // 2) + (f // 2 + 1))
                                last = product3(yb[:, half * D:(half + 1) * D], hid_parts, w2T[par],
                                                lambda part: part[:, f, half * P:(half + 1) * P],
                                                lambda part: part[:, f, :], f == 0, f == KF - 1)
                                if (half * KF + f) % EVERY == EVERY - 1 and after:
                                    turn_next_use(after.pop(0))
                        last.then_inc(y_full, 1)

                    experts(first, expert)(pe)

                @block.vector
                def _(dve):
                    def columns(e, par):
                        dve.tensor_copy(gather_idx[par][:], idx_all[:, span(e, CH)]).then_inc(gidx_ready, 1)

                    def biases(e, par):
                        dve.tensor_copy(b1_e[par][:], b1_cols[:, span(e, KF)]).then_inc(b1_ready, 1)

                    def first():
                        columns(0, 0)
                        columns(1, 1)
                        biases(0, 0)
                        for n in range(NU):
                            turned_lo(dve, 0, 0, n)
                        dve.wait_ge(b2_loaded, 16)

                    def expert(e, par, turn_next, fetch_next, loads=None):
                        if fetch_next:
                            dve.wait_ge(turn_full, e * NU + NU)
                            dve.sem_inc(wait_held, 1)
                            columns(e + 2, par)
                        if turn_next:
                            wait(dve, gelu_done, e * KF)
                            dve.sem_inc(wait_held, 1)
                            biases(e + 1, 1 - par)
                        for k in range(KF // 2):
                            dve.wait_ge(hid_hi, e * (KF // 2) + (k + 1))
                            two = slice(2 * k, 2 * k + 2)
                            dve.tensor_tensor(hid_parts[1][:, two, :], hid[:, two, :], hid_parts[0][:, two, :],
                                              ALU.subtract).then_inc(hid_lo, 1)
                            if turn_next:
                                for n in BETWEEN[k]:
                                    turned_lo(dve, e + 1, 1 - par, n)
                        if turn_next:
                            for n in AFTER:
                                turned_lo(dve, e + 1, 1 - par, n)
                        wait(dve, scattered, e * (CH * 16))
                        dve.sem_inc(wait_held, 1)
                        dve.tensor_copy(scatter_idx[:], idx_all[:, span(e, CH)]).then_inc(y_cols, 1)
                        wait(dve, y_ready, e * CH)
                        dve.sem_inc(wait_held, 1)
                        dve.tensor_copy(wt_e[:], wt_all[:, span(e, CH)]).then_inc(y_cols, 1)
                        dve.wait_ge(y_full, e + 1)
                        for half in range(CH):
                            dve.tensor_tensor(ye[half][:], yb[:, half * D:(half + 1) * D], b2_all[:, e, :], ALU.add
                                              ).then_inc(y_biased, 1)
                        dve.wait_ge(y_cols, e * 2 + 2)
                        for half in range(CH):
                            dve.wait_ge(y_biased, e * CH + (half + 1))
                            last = dve.tensor_scalar(ye[half][:], ye[half][:], wt_e[:, half:half + 1], None, ALU.mult)
                            last.then_inc(y_ready, 1)

                    experts(first, expert)(dve)


_INS = ['L0_attn_inputs', 'L0_attn_W_in', 'L0_attn_conv_w', 'L0_attn_conv_b', 'L0_attn_W_x', 'L0_attn_W_dt',
        'L0_attn_b_dt', 'L0_attn_A_log', 'L0_attn_W_out', 'L0_ffn_norm_weight', 'L0_ffn_router_weight',
        'L0_ffn_router_bias', 'L0_ffn_fc1_weight', 'L0_ffn_fc1_bias', 'L0_ffn_fc2_weight', 'L0_ffn_fc2_bias']
_OUTS = [((2, 2048, 256), 'float32')]


def kernel(**inputs):
    import numpy as _np
    import concourse.bacc as _bacc
    from concourse import mybir as _mybir
    from concourse.bass_utils import run_bass_kernel_spmd as _run

    nc = _bacc.Bacc("TRN2", target_bir_lowering=False, num_devices=1)
    arrays, args = {}, []
    for name in _INS:
        a = _np.ascontiguousarray(inputs[name])
        arrays[f"in_{name}_dram"] = a
        args.append(nc.dram_tensor(f"in_{name}_dram", a.shape, _mybir.dt.from_np(a.dtype), kind="ExternalInput").ap())
    for i, (shape, dtype) in enumerate(_OUTS):
        dt = _mybir.dt.from_np(_np.dtype(dtype))
        args.append(nc.dram_tensor(f"out_{i}_dram", shape, dt, kind="ExternalOutput").ap())
    mixer_moe(nc, *args)
    r = _run(nc, [arrays], core_ids=[0])
    return r.results[0]["out_0_dram"]
```
